# Optimizing a Trainium2 kernel written in Bass

```python
import numpy as np
import jax
import jax.numpy as jnp

def _softmax(x, axis=-1):
    return jax.nn.softmax(x, axis=axis)

def _gelu(x):
    return jax.nn.gelu(x, approximate=True)

def _silu(x):
    return jax.nn.silu(x)

def _sigmoid(x):
    return jax.nn.sigmoid(x)

def _layernorm(x, axis=-1, eps=1e-05):
    m = jnp.mean(x, axis=axis, keepdims=True)
    v = jnp.var(x, axis=axis, keepdims=True)
    return (x - m) / jnp.sqrt(v + eps)

def _scatter_add(tgt, idx, src, axis=0):
    return tgt.at[idx].add(src)

def _segment_sum(src, seg, n):
    return jax.ops.segment_sum(src, seg, n)
kernel_name = 'mk_macaron_d1_jaxref_r4_17347d'

def setup_inputs(seed: int=0):
    np.random.seed(seed)
    _w = jnp.asarray

    def _L0_attn_setup():
        import jax, jax.numpy as jnp
        import numpy as np
        B, T, D_MODEL = (2, 512, 512)
        D_HEAD = 128
        H_PER_G = 4
        N_GROUPS = D_MODEL // (H_PER_G * D_HEAD)
        ROT_BASE = 2500
        EPS = 1e-06

        def _rmsnorm(t):
            rms = jnp.sqrt(jnp.mean(jnp.square(t), axis=-1, keepdims=True) + EPS)
            return t / rms

        def _rope(t):
            length, width = (t.shape[-2], t.shape[-1])
            pos = jnp.arange(length)[:, None]
            dims = jnp.arange(width // 2)[None, :]
            ang = jnp.power(float(ROT_BASE), -dims / (width // 2))
            rad = (pos * ang).astype(t.dtype)
            cos, sin = (jnp.cos(rad), jnp.sin(rad))
            even, odd = jnp.split(t, 2, axis=-1)
            return jnp.concatenate([even * cos - odd * sin, even * sin + odd * cos], axis=-1)
        key = jax.random.key(seed)
        ks = jax.random.split(key, 5)
        s = D_MODEL ** (-0.5)
        return {'x': jax.random.normal(ks[0], (B, T, D_MODEL), jnp.float32), 'wq': jax.random.normal(ks[1], (D_MODEL, D_MODEL), jnp.float32) * s, 'wk': jax.random.normal(ks[2], (D_MODEL, D_MODEL // H_PER_G), jnp.float32) * s, 'wv': jax.random.normal(ks[3], (D_MODEL, D_MODEL // H_PER_G), jnp.float32) * s, 'wo': jax.random.normal(ks[4], (D_MODEL, D_MODEL), jnp.float32) * s, 'gq': jnp.ones((N_GROUPS, H_PER_G, D_HEAD), jnp.float32), 'gk': jnp.ones((N_GROUPS, D_HEAD), jnp.float32)}
    _L0_attn_in = _L0_attn_setup()

    def _L0_ffn_setup():
        import jax, jax.numpy as jnp
        import numpy as np
        E = 32
        K = 6
        H = 512
        I = 256
        T = 512
        CAP = 192
        SCALE = 1.5
        SWIGLU_LIMIT = 10.0
        key = jax.random.key(seed)
        ks = jax.random.split(key, 9)

        def s(k, shape, fan):
            return jax.random.normal(k, shape, jnp.float32) * fan ** (-0.5)
        return {'x': jax.random.normal(ks[0], (1, T, H), jnp.float32), 'gate_w': s(ks[1], (E, H), H), 'bias': jax.random.normal(ks[2], (E,), jnp.float32) * 0.01, 'w_gate': s(ks[3], (E, I, H), H), 'w_up': s(ks[4], (E, I, H), H), 'w_down': s(ks[5], (E, H, I), I), 'sg': s(ks[6], (I, H), H), 'su': s(ks[7], (I, H), H), 'sd': s(ks[8], (H, I), I)}
    _L0_ffn_in = _L0_ffn_setup()
    _d = {'L0_attn_x': _L0_attn_in['x'], 'L0_attn_wq': _L0_attn_in['wq'], 'L0_attn_wk': _L0_attn_in['wk'], 'L0_attn_wv': _L0_attn_in['wv'], 'L0_attn_wo': _L0_attn_in['wo'], 'L0_attn_gq': _L0_attn_in['gq'], 'L0_attn_gk': _L0_attn_in['gk'], 'L0_ffn_gate_w': _L0_ffn_in['gate_w'], 'L0_ffn_bias': _L0_ffn_in['bias'], 'L0_ffn_w_gate': _L0_ffn_in['w_gate'], 'L0_ffn_w_up': _L0_ffn_in['w_up'], 'L0_ffn_w_down': _L0_ffn_in['w_down'], 'L0_ffn_sg': _L0_ffn_in['sg'], 'L0_ffn_su': _L0_ffn_in['su'], 'L0_ffn_sd': _L0_ffn_in['sd']}
    _x0 = _d['L0_attn_x']
    _d['L0_attn_x'] = jax.random.normal(jax.random.fold_in(jax.random.key(seed), 1), (4, 1024, 512), dtype=_x0.dtype)
    del _x0
    return _d

def reference(L0_attn_x, L0_attn_wq, L0_attn_wk, L0_attn_wv, L0_attn_wo, L0_attn_gq, L0_attn_gk, L0_ffn_gate_w, L0_ffn_bias, L0_ffn_w_gate, L0_ffn_w_up, L0_ffn_w_down, L0_ffn_sg, L0_ffn_su, L0_ffn_sd):

    def _L0_attn_ref(x, wq, wk, wv, wo, gq, gk):
        import jax, jax.numpy as jnp
        import numpy as np
        B, T, D_MODEL = (2, 512, 512)
        D_HEAD = 128
        H_PER_G = 4
        N_GROUPS = D_MODEL // (H_PER_G * D_HEAD)
        ROT_BASE = 2500
        EPS = 1e-06

        def _rmsnorm(t):
            rms = jnp.sqrt(jnp.mean(jnp.square(t), axis=-1, keepdims=True) + EPS)
            return t / rms

        def _rope(t):
            length, width = (t.shape[-2], t.shape[-1])
            pos = jnp.arange(length)[:, None]
            dims = jnp.arange(width // 2)[None, :]
            ang = jnp.power(float(ROT_BASE), -dims / (width // 2))
            rad = (pos * ang).astype(t.dtype)
            cos, sin = (jnp.cos(rad), jnp.sin(rad))
            even, odd = jnp.split(t, 2, axis=-1)
            return jnp.concatenate([even * cos - odd * sin, even * sin + odd * cos], axis=-1)
        b, t, _ = x.shape
        q = jnp.einsum('bti,io->bto', x, wq)
        k = jnp.einsum('bti,io->bto', x, wk)
        v = jnp.einsum('bti,io->bto', x, wv)
        q = q.reshape(b, t, N_GROUPS, H_PER_G, D_HEAD).transpose(0, 2, 3, 1, 4)
        k = k.reshape(b, t, N_GROUPS, D_HEAD).transpose(0, 2, 1, 3)
        v = v.reshape(b, t, N_GROUPS, D_HEAD).transpose(0, 2, 1, 3)
        q = _rmsnorm(q) * gq[None, :, :, None, :]
        k = _rmsnorm(k) * gk[None, :, None, :]
        q = _rope(q)
        k = _rope(k)
        mult = jnp.asarray(D_HEAD ** (-0.25), x.dtype)
        s = jnp.einsum('bghid,bgjd->bghij', q * mult, k * mult)
        i = jnp.arange(t)[:, None]
        j = jnp.arange(t)[None, :]
        s = s - jnp.asarray(1e+30, s.dtype) * (i < j)
        p = jax.nn.softmax(s, axis=-1)
        o = jnp.einsum('bghij,bgjd->bghid', p, v)
        o = o.transpose(0, 3, 1, 2, 4).reshape(b, t, D_MODEL)
        return jnp.einsum('bti,io->bto', o, wo)

    def _L0_ffn_ref(x, gate_w, bias, w_gate, w_up, w_down, sg, su, sd):
        import jax, jax.numpy as jnp
        import numpy as np
        E = 32
        K = 6
        H = 512
        I = 256
        T = 512
        CAP = 192
        SCALE = 1.5
        SWIGLU_LIMIT = 10.0
        B, S, Hd = x.shape
        h = x.reshape(-1, Hd)
        logits = h @ gate_w.T
        scores = jnp.sqrt(jax.nn.softplus(logits))
        _, topk_idx = jax.lax.top_k(scores + bias[None, :], K)
        topk_w = jnp.take_along_axis(scores, topk_idx, axis=1)
        topk_w = topk_w / jnp.sum(topk_w, axis=-1, keepdims=True)
        topk_w = topk_w * SCALE
        eid = topk_idx.reshape(-1)
        onehot = jax.nn.one_hot(eid, E, dtype=jnp.int32)
        pos = jnp.cumsum(onehot, axis=0) - 1
        pos = jnp.take_along_axis(pos, eid[:, None], axis=1)[:, 0]
        valid = pos < CAP
        pos = jnp.where(valid, pos, CAP)
        h_rep = jnp.repeat(h, K, axis=0)
        xb = jnp.zeros((E, CAP + 1, Hd), x.dtype).at[eid, pos].set(h_rep)
        g = jnp.einsum('ech,eih->eci', xb, w_gate)
        u = jnp.einsum('ech,eih->eci', xb, w_up)
        inter = jax.nn.silu(g) * u
        yb = jnp.einsum('eci,ehi->ech', inter, w_down)
        w_slot = jnp.where(valid, topk_w.reshape(-1), 0.0)
        y = yb[eid, pos] * w_slot[:, None]
        routed = y.reshape(-1, K, Hd).sum(axis=1)
        si = jax.nn.silu(h @ sg.T) * (h @ su.T)
        si = jnp.clip(si, -SWIGLU_LIMIT, SWIGLU_LIMIT)
        shared = si @ sd.T
        return (routed + shared).reshape(B, S, Hd)
    x = L0_attn_x
    x = x + 0.5 * _L0_ffn_ref(_layernorm(x, axis=-1), L0_ffn_gate_w, L0_ffn_bias, L0_ffn_w_gate, L0_ffn_w_up, L0_ffn_w_down, L0_ffn_sg, L0_ffn_su, L0_ffn_sd)
    x = x + _L0_attn_ref(_layernorm(x, axis=-1), L0_attn_wq, L0_attn_wk, L0_attn_wv, L0_attn_wo, L0_attn_gq, L0_attn_gk)
    x = x + 0.5 * _L0_ffn_ref(_layernorm(x, axis=-1), L0_ffn_gate_w, L0_ffn_bias, L0_ffn_w_gate, L0_ffn_w_up, L0_ffn_w_down, L0_ffn_sg, L0_ffn_su, L0_ffn_sd)
    return x

_drawn_inputs = setup_inputs


def setup_inputs(seed=0):
    import zlib

    import numpy as np

    out = dict(_drawn_inputs(seed))
    spreads = {'L0_attn_gq': (1.0, 0.6), 'L0_attn_gk': (1.0, 0.6)}
    factors = {}
    for name, (base, spread) in spreads.items():
        noise = np.random.default_rng([zlib.crc32(name.encode()), seed]).standard_normal(out[name].shape)
        drawn = base * np.exp(spread * noise) if base else spread * noise
        out[name] = jnp.asarray(drawn.astype(out[name].dtype))
    for name, factor in factors.items():
        out[name] = (out[name] * factor).astype(out[name].dtype)
    return out
```

```python
from contextlib import ExitStack

import numpy as np

import concourse.bass as bass
from concourse import mybir

F32 = mybir.dt.float32
F32R = mybir.dt.float32r
BF16 = mybir.dt.bfloat16
I32 = mybir.dt.int32
U32 = mybir.dt.uint32
ALU = mybir.AluOpType
ACT = mybir.ActivationFunctionType
AX = mybir.AxisListType

P = 128
B, SEQ, D = 4, 1024, 512
TOK = B * SEQ
NT = TOK // P
KB = D // P
E, TOPK, FF = 32, 6, 256
FB = FF // P
CAP = 192
HALF = CAP // 2
ROUTE_SCALE = 1.5
H, DH = 4, 128
GT = 4
G = NT // GT
GTOK = GT * P
SA, SB_ = 12, 16
ROW = D + E
DUMP = TOK
ROWS = TOK + HALF
EG = 8
NQ = SEQ // P
WGU, WDN = KB * 2 * FF, FB * D
WALL = WGU + WDN
NO_SLOT = 4000.0
QUERY_ORDER = tuple(range(NQ))
SWIGLU_LIMIT = 10.0
LN_EPS, RMS_EPS = 1e-5, 1e-6


def split_products(pe, out, hi_lo_weights, hi_lo_moving, first, last):
    wh, wl = hi_lo_weights
    mh, ml = hi_lo_moving
    pe.matmul(out, wh, mh, start=first, stop=False)
    pe.matmul(out, wh, ml, start=False, stop=False)
    return pe.matmul(out, wl, mh, start=False, stop=last)


class Kept:
    pass


def allocate_kept(nc, ctx):
    k = Kept()

    def sb(name, shape, dt):
        return ctx.enter_context(nc.sbuf_tensor(name, shape, dt))

    k.ident = sb("ident", [P, P], F32)
    k.causal_bf = sb("causal_bf", [P, P], BF16)
    k.ident_bf = sb("ident_bf", [P, P], BF16)
    k.upto_bf = sb("upto_bf", [P, P], BF16)
    k.ones_bf = sb("ones_bf", [P, P], BF16)
    k.ln_eps = sb("ln_eps", [P, 1], F32)
    k.rms_eps = sb("rms_eps", [P, 1], F32)
    k.shared_hi = sb("shared_hi", [P, WALL], F32R)
    k.shared_lo = sb("shared_lo", [P, WALL], F32R)
    k.router = sb("router", [P, KB, 2, E], F32R)
    k.wqkv_hi = sb("wqkv_hi", [P, KB, 6 * DH], F32R)
    k.wqkv_lo = sb("wqkv_lo", [P, KB, 6 * DH], F32R)
    k.wo_hi = sb("wo_hi", [P, H, D], F32R)
    k.wo_lo = sb("wo_lo", [P, H, D], F32R)
    return k


def setup(nc, a, k, htab, accs):
    with ExitStack() as ctx:
        sb = lambda name, shape, dt: ctx.enter_context(nc.sbuf_tensor(name, shape, dt))
        sem = lambda name: ctx.enter_context(nc.semaphore(name))
        raw_shared = sb("raw_shared", [P, WALL], F32)
        raw_router = sb("raw_router", [P, KB, E], F32)
        raw_qkv = sb("raw_qkv", [P, KB, 6 * DH], F32)
        raw_wo = sb("raw_wo", [P, H, D], F32)
        raw_causal = sb("raw_causal", [P, P], F32)
        raw_upto = sb("raw_upto", [P, P], F32)
        zeros = sb("zeros", [HALF, ROW], F32)
        loaded, zeroed, dumps = sem("setup_loaded"), sem("setup_zeroed"), sem("setup_dumps")
        hi_ready = sem("setup_hi")
        with nc.Block() as block:

            @block.sync
            def _(sp):
                pairs = [(raw_router[:, :, :], a["router_w"]), (k.ident[:, :], a["ident"]),
                         (raw_causal[:, :], a["causal"]), (raw_upto[:, :], a["upto"]),
                         (raw_shared[:, :], a["w_shared"]), (raw_qkv[:, :, :], a["w_qkv"]),
                         (raw_wo[:, :, :], a["w_out"])]
                for dst, src in pairs:
                    sp.dma_start(dst, src).then_inc(loaded, 16)
                sp.wait_ge(zeroed, 1)
                sp.dma_start(htab[DUMP:ROWS, :], zeros[:, :]).then_inc(dumps, 16)
                for acc in accs:
                    sp.dma_start(acc[DUMP:ROWS, :], zeros[:, 0:D]).then_inc(dumps, 16)
                sp.wait_ge(dumps, 16 * (1 + len(accs)))

            @block.gpsimd
            def _(pool):
                pool.memset(k.ones_bf[:, :], 1.0)
                pool.memset(k.ln_eps[:, :], LN_EPS)
                pool.memset(k.rms_eps[:, :], RMS_EPS)
                pool.memset(zeros[:, :], 0.0).then_inc(zeroed, 1)

            @block.scalar
            def _(act):
                act.wait_ge(loaded, 16 * 7)
                act.activation(k.router[:, :, 0, :], raw_router[:, :, :], ACT.Copy)
                act.activation(k.ident_bf[:, :], k.ident[:, :], ACT.Copy)
                act.activation(k.causal_bf[:, :], raw_causal[:, :], ACT.Copy)
                act.activation(k.upto_bf[:, :], raw_upto[:, :], ACT.Copy)
                act.activation(k.shared_hi[:, :], raw_shared[:, :], ACT.Copy)
                act.activation(k.wqkv_hi[:, :, :], raw_qkv[:, :, :], ACT.Copy)
                act.activation(k.wo_hi[:, :, :], raw_wo[:, :, :], ACT.Copy).then_inc(hi_ready, 1)

            @block.vector
            def _(dve):
                dve.wait_ge(hi_ready, 1)
                for lo, raw, hi in ((k.router[:, :, 1, :], raw_router[:, :, :], k.router[:, :, 0, :]),
                                    (k.shared_lo[:, :], raw_shared[:, :], k.shared_hi[:, :]),
                                    (k.wqkv_lo[:, :, :], raw_qkv[:, :, :], k.wqkv_hi[:, :, :]),
                                    (k.wo_lo[:, :, :], raw_wo[:, :, :], k.wo_hi[:, :, :])):
                    dve.tensor_tensor(lo, raw, hi.bitcast(F32), ALU.subtract)


def dense_ffn(nc, k, n, src, acc, htab, logits):
    with ExitStack() as ctx:
        sb = lambda name, shape, dt: ctx.enter_context(nc.sbuf_tensor(f"{name}{n}", shape, dt))
        pb = lambda name: ctx.enter_context(nc.psum_tensor(f"{name}{n}", [P, 512], F32))
        sem = lambda name: ctx.enter_context(nc.semaphore(f"{name}{n}"))
        x = [sb(f"d_x{u}_", [P, GT, D], F32) for u in range(2)]
        h = [sb(f"d_h{u}_", [P, GT, D], F32) for u in range(2)]
        y = [sb(f"d_y{u}_", [P, GT, D], F32) for u in range(2)]
        stats = sb("d_stats", [P, GT, 6], F32)
        mv = [sb(f"d_mv{u}_", [P, GT, 2], F32) for u in range(2)]
        std = [sb(f"d_std{u}_", [P, GT], F32) for u in range(2)]
        rstd = [sb(f"d_rstd{u}_", [P, GT], F32) for u in range(2)]
        ht_hi = [sb(f"d_ht_hi{u}_", [P, KB, GTOK], F32R) for u in range(2)]
        ht_lo = [sb(f"d_ht_lo{u}_", [P, KB, GTOK], F32R) for u in range(2)]
        silu = [sb(f"d_silu{b}_", [P, GTOK], F32) for b in range(FB)]
        inter = [sb(f"d_inter{b}_", [P, GTOK], F32) for b in range(FB)]
        in_hi = [sb(f"d_in_hi{u}_", [P, FB, GTOK], F32R) for u in range(2)]
        in_lo = [sb(f"d_in_lo{u}_", [P, FB, GTOK], F32R) for u in range(2)]
        ps_t = [pb(f"d_ps_t{i}_") for i in range(2)]
        ps_gate = [pb(f"d_ps_gate{b}_") for b in range(FB)]
        ps_up = [pb(f"d_ps_up{b}_") for b in range(FB)]
        ps_down = [pb(f"d_ps_down{i}_") for i in range(2)]
        x_loaded = [sem(f"d_x_loaded{u}_") for u in range(2)]
        h_stored = [sem(f"d_h_stored{u}_") for u in range(2)]
        y_stored = [sem(f"d_y_stored{u}_") for u in range(2)]
        stats_ready, std_ready, h_ready = sem("d_stats_ready"), sem("d_std_ready"), sem("d_h_ready")
        t_ready, t_hi, t_lo = sem("d_t_ready"), sem("d_t_hi"), sem("d_t_lo")
        lg_ready, lg_taken = sem("d_lg_ready"), sem("d_lg_taken")
        gu_ready, silu_ready, mul_ready = sem("d_gu_ready"), sem("d_silu_ready"), sem("d_mul_ready")
        ihi_ready, ilo_ready = sem("d_ihi_ready"), sem("d_ilo_ready")
        d_ready, y_done = sem("d_d_ready"), sem("d_y_done")
        gu_hi = k.shared_hi[:, 0:WGU].rearrange("p (k c) -> p k c", k=KB)
        gu_lo = k.shared_lo[:, 0:WGU].rearrange("p (k c) -> p k c", k=KB)
        dn_hi = k.shared_hi[:, WGU:].rearrange("p (k c) -> p k c", k=FB)
        dn_lo = k.shared_lo[:, WGU:].rearrange("p (k c) -> p k c", k=FB)
        group = lambda ap, g: ap[bass.ds(g * GTOK, GTOK), :].rearrange("(j p) d -> p j d", p=P)
        last = G // 2 - 1

        with nc.Block() as block:

            @block.sync
            def _(sp):
                for u in range(2):
                    sp.sem_inc(h_stored[u], 16)
                    sp.sem_inc(y_stored[u], 16)
                    sp.dma_start(x[u][:, :, :], group(src, u)).then_inc(x_loaded[u], 16)

                def body(i, u, load=True):
                    g = 2 * i + u
                    sp.wait_ge(h_ready, g + 1)
                    sp.dma_start(group(htab, g)[:, :, 0:D], h[u][:, :, :]).then_inc(h_stored[u], 16)
                    sp.wait_ge(y_done, 4 * g + 4 + 2)
                    sp.dma_start(group(acc, g), y[u][:, :, :]).then_inc(y_stored[u], 16)
                    if load:
                        sp.dma_start(x[u][:, :, :], group(src, g + 2)).then_inc(x_loaded[u], 16)

                with sp.Fori(0, last) as i:
                    body(i, 0)
                    body(i, 1)
                body(last, 0, load=False)
                body(last, 1, load=False)
                for u in range(2):
                    sp.wait_ge(h_stored[u], 16 * (G // 2 + 1))
                    sp.wait_ge(y_stored[u], 16 * (G // 2 + 1))

            @block.scalar
            def _(act):
                def root(g, u):
                    act.wait_ge(stats_ready, g + 1)
                    act.activation(std[u][:, :], mv[u][:, :, 1], ACT.Sqrt, bias=k.ln_eps[:, :]).then_inc(std_ready, 1)

                def body(i, u, ahead=True):
                    g = 2 * i + u
                    for c in range(KB):
                        act.wait_ge(t_ready, 4 * g + c + 1)
                        act.activation(ht_hi[u][:, c, :], ps_t[c % 2][:, :], ACT.Copy).then_inc(t_hi, 1)
                    if ahead:
                        root(g + 1, 1 - u)
                    for b in range(FB):
                        act.wait_ge(gu_ready, 2 * g + b + 1)
                        act.activation(silu[b][:, :], ps_gate[b][:, :], ACT.Silu).then_inc(silu_ready, 1)
                        act.wait_ge(mul_ready, 2 * g + b + 1 + 2)
                        act.activation(in_hi[u][:, b, :], inter[b][:, :], ACT.Copy).then_inc(ihi_ready, 1)

                root(0, 0)
                with act.Fori(0, last) as i:
                    body(i, 0)
                    body(i, 1)
                body(last, 0)
                body(last, 1, ahead=False)

            @block.vector
            def _(dve):
                dve.sem_inc(t_lo, 2)
                dve.sem_inc(mul_ready, 2)
                dve.sem_inc(y_done, 2)
                dve.sem_inc(lg_taken, 1)

                def layernorm(i, u):
                    g = 2 * i + u
                    dve.wait_ge(x_loaded[u], 16 * i + 16)
                    for j in range(GT):
                        dve.bn_stats(stats[:, j, :], x[u][:, j, :])
                    dve.drain()
                    for j in range(GT):
                        got = dve.bn_aggr(mv[u][:, j, :], stats[:, j, :])
                    got.then_inc(stats_ready, 1)
                    dve.wait_ge(std_ready, g + 1)
                    dve.reciprocal(rstd[u][:, :], std[u][:, :])
                    dve.drain()
                    dve.wait_ge(h_stored[u], 16 * i + 16)
                    for j in range(GT):
                        got = dve.tensor_scalar(h[u][:, j, :], x[u][:, j, :], mv[u][:, j, 0:1],
                                                rstd[u][:, j:j + 1], ALU.subtract, ALU.mult)
                    got.then_inc(h_ready, 1)

                def body(i, u, ahead=True):
                    g = 2 * i + u
                    for c in range(KB):
                        dve.wait_ge(t_hi, 4 * g + c + 1)
                        dve.tensor_tensor(ht_lo[u][:, c, :], ps_t[c % 2][:, :], ht_hi[u][:, c, :].bitcast(F32),
                                          ALU.subtract).then_inc(t_lo, 1)
                    dve.wait_ge(lg_ready, g + 1)
                    dve.tensor_scalar(logits[:, bass.ds(g * GT, GT), :],
                                      ps_t[0][:, 0:GT * 2 * E].rearrange("p (j c) -> p j c", j=GT),
                                      1.0, None, ALU.mult).then_inc(lg_taken, 1)
                    if ahead:
                        if u == 0:
                            layernorm(i, 1)
                        else:
                            layernorm(i + 1, 0)
                    for b in range(FB):
                        dve.wait_ge(silu_ready, 2 * g + b + 1)
                        dve.tensor_tensor(inter[b][:, :], silu[b][:, :], ps_up[b][:, :], ALU.mult)
                        dve.drain()
                        dve.tensor_scalar(inter[b][:, :], inter[b][:, :], SWIGLU_LIMIT, -SWIGLU_LIMIT,
                                          ALU.min, ALU.max).then_inc(mul_ready, 1)
                        dve.wait_ge(ihi_ready, 2 * g + b + 1)
                        dve.tensor_tensor(in_lo[u][:, b, :], inter[b][:, :], in_hi[u][:, b, :].bitcast(F32),
                                          ALU.subtract).then_inc(ilo_ready, 1)
                    dve.wait_ge(y_stored[u], 16 * i + 16)
                    for j in range(GT):
                        dve.wait_ge(d_ready, 4 * g + j + 1)
                        dve.scalar_tensor_tensor(y[u][:, j, :], ps_down[j % 2][:, :], 0.5, x[u][:, j, :],
                                                 ALU.mult, ALU.add).then_inc(y_done, 1)

                layernorm(0, 0)
                with dve.Fori(0, last) as i:
                    body(i, 0)
                    body(i, 1)
                body(last, 0)
                body(last, 1, ahead=False)

            @block.tensor
            def _(pe):
                def body(i, u):
                    g = 2 * i + u
                    pe.wait_ge(h_ready, g + 1)
                    pe.wait_ge(lg_taken, g + 1)
                    for c in range(KB):
                        pe.wait_ge(t_lo, 4 * g + c + 1)
                        for j in range(GT):
                            got = pe.transpose(ps_t[c % 2][:, j * P:(j + 1) * P], h[u][:, j, c * P:(c + 1) * P],
                                               k.ident[:, :])
                        got.then_inc(t_ready, 1)
                    pe.wait_ge(t_lo, 4 * g + 4 + 2)
                    for j in range(GT):
                        for c in range(KB):
                            for part, ht in enumerate((ht_hi, ht_lo)):
                                got = pe.matmul(ps_t[0][:, j * 2 * E:(j + 1) * 2 * E],
                                                ht[u][:, c, j * P:(j + 1) * P], k.router[:, c, :, :],
                                                start=(c == 0 and part == 0), stop=(c == KB - 1 and part == 1))
                    got.then_inc(lg_ready, 1)
                    for b in range(FB):
                        pe.wait_ge(mul_ready, 2 * g + b + 1)
                        for bank, at in ((ps_gate[b], b * P), (ps_up[b], FF + b * P)):
                            for c in range(KB):
                                got = split_products(pe, bank[:, :], (gu_hi[:, c, at:at + P], gu_lo[:, c, at:at + P]),
                                                     (ht_hi[u][:, c, :], ht_lo[u][:, c, :]), c == 0, c == KB - 1)
                        got.then_inc(gu_ready, 1)
                    pe.wait_ge(ilo_ready, 2 * g + 2)
                    for j in range(GT):
                        pe.wait_ge(y_done, 4 * g + j + 1)
                        tok = slice(j * P, (j + 1) * P)
                        for b in range(FB):
                            got = split_products(pe, ps_down[j % 2][:, :], (in_hi[u][:, b, tok], in_lo[u][:, b, tok]),
                                                 (dn_hi[:, b, :], dn_lo[:, b, :]), b == 0, b == FB - 1)
                        got.then_inc(d_ready, 1)

                with pe.Fori(0, last) as i:
                    body(i, 0)
                    body(i, 1)
                body(last, 0)
                body(last, 1)


def route(nc, a, k, n, htab, logits, slot_dram, slots):
    with ExitStack() as ctx:
        sb = lambda name, shape, dt: ctx.enter_context(nc.sbuf_tensor(f"{name}{n}", shape, dt))
        pb = lambda name: ctx.enter_context(nc.psum_tensor(f"{name}{n}", [P, 512], F32))
        sem = lambda name: ctx.enter_context(nc.semaphore(f"{name}{n}"))
        wide = [P, NT, E]
        t1, t2, t3, t4, t5 = (sb(f"r_t{i}_", wide, F32) for i in range(1, 6))
        score = sb("r_score", wide, F32)
        small = sb("r_small", wide, U32)
        seg = sb("r_seg", wide, F32)
        mask = sb("r_mask", wide, F32)
        mask_bf = sb("r_mask_bf", wide, BF16)
        bias = sb("r_bias", [P, E], F32)
        top8 = sb("r_top8", [P, NT, 8], F32)
        per_tok = sb("r_per_tok", [P, NT], F32)
        code = sb("r_code", wide, I32)
        code_a = sb("r_code_a", wide, I32)
        code_b = sb("r_code_b", wide, I32)
        slot_a = sb("r_slot_a", wide, F32)
        slot_b = sb("r_slot_b", wide, F32)
        iota_a = sb("r_iota_a", [P, SA], F32)
        iota_b = sb("r_iota_b", [P, SB_], F32)
        tok_id = sb("r_tok_id", [P, NT], F32)
        diag = sb("r_diag", [EG * SA, EG, SB_], F32)
        dump = sb("r_dump", [HALF, 1], F32)
        hot_a = [sb(f"r_hot_a{u}_", [P, E, SA], F32) for u in range(2)]
        id_a = [sb(f"r_id_a{u}_", [P, E * SA], F32R) for u in range(2)]
        hot_b = [sb(f"r_hot_b{u}_", [P, E * SB_], F32R) for u in range(2)]
        picked = sb("r_picked", [EG * SA, E // EG, EG, SB_], F32)
        table = sb("r_table", [EG * SA, E // EG, SB_], F32)
        table2 = sb("r_table2", [EG * SA, E // EG, SB_], F32)
        rows = sb("r_rows", [2 * E, HALF], F32)
        idx = sb("r_idx", [HALF, 2 * E], F32)
        off = sb("r_off", [HALF, 2 * E], F32)
        ps_cum = [pb(f"r_ps_cum{i}_") for i in range(2)]
        ps_tot = [pb(f"r_ps_tot{i}_") for i in range(2)]
        ps_tab = [pb(f"r_ps_tab{i}_") for i in range(E // EG)]
        loaded, w_stored, t_stored, t_read = sem("r_loaded"), sem("r_w_stored"), sem("r_t_stored"), sem("r_t_read")
        lg_sum, exp_done, poly, ln_done = sem("r_lg_sum"), sem("r_exp"), sem("r_poly"), sem("r_ln")
        sp_done, score_done, mask_done, w_done = sem("r_sp"), sem("r_score_d"), sem("r_mask_d"), sem("r_w")
        counted, code_done = sem("r_counted"), sem("r_code_d")
        hots, ida, tabbed, tab_done = sem("r_hots"), sem("r_ida"), sem("r_tabbed"), sem("r_tab")
        turned = sem("r_turned")
        flat = lambda t: t[:, :, :].rearrange("p t e -> p (t e)")
        per_token = lambda ap: ap.rearrange("p (t o) -> p t o", o=1).to_broadcast(wide)

        with nc.Block() as block:

            @block.sync
            def _(sp):
                for dst, src in ((bias[:, :], a["bias"]), (seg[:, :, :], a["seg"]), (iota_a[:, :], a["iota_a"]),
                                 (iota_b[:, :], a["iota_b"]), (tok_id[:, :], a["tok_id"]),
                                 (diag[:, :, :], a["diag"]), (dump[:, :], a["dump"])):
                    sp.dma_start(dst, src).then_inc(loaded, 16)
                sp.wait_ge(w_done, 1)
                with nc.allow_non_contiguous_dma(reason="32 weights behind each row of tokens"):
                    sp.dma_start(htab[0:TOK, D:ROW].rearrange("(t p) e -> p t e", p=P), t1[:, :, :]).then_inc(w_stored, 16)
                sp.wait_ge(tab_done, 1)
                sp.dma_start(slot_dram.rearrange("(g r b) -> r g b", g=E // EG, b=SB_), table2[:, :, :]).then_inc(t_stored, 16)
                sp.wait_ge(t_stored, 16)
                sp.dma_start(rows[:, :], slot_dram.rearrange("(q s) -> q s", s=HALF)).then_inc(t_read, 16)
                sp.wait_ge(w_stored, 16)

            @block.scalar
            def _(act):
                act.wait_ge(lg_sum, 1)
                act.activation(t2[:, :, :], t1[:, :, :], ACT.Abs)
                act.drain()
                act.activation(t3[:, :, :], t2[:, :, :], ACT.Exp, scale=-1.0).then_inc(exp_done, 1)
                act.drain()
                act.activation(t4[:, :, :], t3[:, :, :], ACT.Ln, bias=1.0).then_inc(ln_done, 1)
                act.wait_ge(sp_done, 1)
                act.activation(score[:, :, :], t5[:, :, :], ACT.Sqrt).then_inc(score_done, 1)
                act.wait_ge(w_done, 1)
                with act.Fori(0, NT // 2) as i:
                    for u in range(2):
                        act.wait_ge(hots, 2 * i + u + 1)
                        act.wait_ge(tabbed, 2 * i + u + 1)
                        act.activation(id_a[u][:, :], hot_a[u][:, :, :].rearrange("p e s -> p (e s)"), ACT.Copy,
                                       scale=tok_id[:, bass.ds(2 * i + u, 1)]).then_inc(ida, 1)

            @block.vector
            def _(dve):
                dve.tensor_tensor(t1[:, :, :], logits[:, :, 0:E], logits[:, :, E:2 * E], ALU.add).then_inc(lg_sum, 1)
                dve.wait_ge(exp_done, 1)
                dve.tensor_scalar(t5[:, :, :], t3[:, :, :], 1.0 / 3.0, -0.5, ALU.mult, ALU.add)
                dve.tensor_scalar(small[:, :, :], t3[:, :, :], 0.01, None, ALU.is_lt)
                dve.drain()
                dve.tensor_tensor(t2[:, :, :], t5[:, :, :], t3[:, :, :], ALU.mult)
                dve.drain()
                dve.scalar_tensor_tensor(t5[:, :, :], t2[:, :, :], 1.0, t3[:, :, :], ALU.add, ALU.mult)
                dve.wait_ge(ln_done, 1)
                dve.drain()
                dve.copy_predicated(flat(t4), flat(small), flat(t5))
                dve.drain()
                dve.scalar_tensor_tensor(t5[:, :, :], t1[:, :, :], 0.0, t4[:, :, :], ALU.max, ALU.add).then_inc(sp_done, 1)
                dve.wait_ge(score_done, 1)
                dve.wait_ge(loaded, 16 * 7)
                dve.tensor_tensor(t1[:, :, :], score[:, :, :],
                                  bias[:, :].rearrange("p (o e) -> p o e", o=1).to_broadcast(wide), ALU.add)
                dve.drain()
                for t in range(NT):
                    dve.max(top8[:, t, :], t1[:, t, :])
                dve.drain()
                sixth = top8[:, :, TOPK - 1:TOPK].to_broadcast(wide)
                dve.tensor_tensor(t2[:, :, :], t1[:, :, :], sixth, ALU.is_gt)
                dve.tensor_tensor(t3[:, :, :], t1[:, :, :], sixth, ALU.is_equal)
                dve.drain()
                dve.tensor_reduce(per_tok[:, :], t2[:, :, :], AX.X, ALU.add)
                dve.tensor_tensor_scan(flat(t4), flat(seg), flat(t3), 0.0, ALU.mult, ALU.add)
                dve.drain()
                dve.tensor_tensor(t5[:, :, :], t4[:, :, :], per_token(per_tok[:, :]), ALU.add)
                dve.drain()
                dve.scalar_tensor_tensor(t4[:, :, :], t5[:, :, :], float(TOPK), t3[:, :, :], ALU.is_le, ALU.mult)
                dve.drain()
                dve.tensor_tensor(mask[:, :, :], t4[:, :, :], t2[:, :, :], ALU.add)
                dve.drain()
                dve.tensor_copy(mask_bf[:, :, :], mask[:, :, :]).then_inc(mask_done, 1)
                dve.tensor_tensor(t1[:, :, :], score[:, :, :], mask[:, :, :], ALU.mult)
                dve.drain()
                dve.tensor_reduce(per_tok[:, :], t1[:, :, :], AX.X, ALU.add)
                dve.drain()
                dve.reciprocal(top8[:, :, 0:1].rearrange("p t o -> p (t o)"), per_tok[:, :])
                dve.drain()
                dve.scalar_tensor_tensor(t1[:, :, :], t1[:, :, :], ROUTE_SCALE * 0.5,
                                         top8[:, :, 0:1].to_broadcast(wide), ALU.mult, ALU.mult).then_inc(w_done, 1)
                dve.wait_ge(counted, 1)
                by_expert = lambda t: flat(t).rearrange("p (e t) -> p e t", t=NT)
                for i in range(2):
                    dve.tensor_copy(by_expert(t2)[:, :, i * NT // 2:(i + 1) * NT // 2],
                                    ps_tot[i][:, :].rearrange("p (t e) -> p e t", e=E))
                dve.drain()
                dve.tensor_tensor_scan(flat(t3), flat(seg), flat(t2), 0.0, ALU.mult, ALU.add)
                dve.drain()
                dve.tensor_tensor(t4[:, :, :], t3[:, :, :], t2[:, :, :], ALU.subtract)
                dve.drain()
                for i in range(2):
                    dve.tensor_tensor(t5[:, i * NT // 2:(i + 1) * NT // 2, :],
                                      ps_cum[i][:, :].rearrange("p (t e) -> p t e", e=E),
                                      by_expert(t4)[:, :, i * NT // 2:(i + 1) * NT // 2].rearrange("p e t -> p t e"),
                                      ALU.add)
                dve.drain()
                dve.scalar_tensor_tensor(t2[:, :, :], t5[:, :, :], float(CAP), mask[:, :, :], ALU.is_le, ALU.mult)
                dve.drain()
                dve.scalar_tensor_tensor(t3[:, :, :], t5[:, :, :], -1.0 - NO_SLOT, t2[:, :, :], ALU.add, ALU.mult)
                dve.drain()
                dve.tensor_scalar(code[:, :, :], t3[:, :, :], NO_SLOT, None, ALU.add)
                dve.drain()
                dve.tensor_scalar(code_a[:, :, :], code[:, :, :], 4, None, ALU.arith_shift_right)
                dve.tensor_scalar(code_b[:, :, :], code[:, :, :], SB_ - 1, None, ALU.bitwise_and)
                dve.drain()
                dve.tensor_copy(slot_a[:, :, :], code_a[:, :, :])
                dve.tensor_copy(slot_b[:, :, :], code_b[:, :, :])
                dve.drain()
                with dve.Fori(0, NT // 2) as i:
                    for u in range(2):
                        t = 2 * i + u
                        dve.wait_ge(tabbed, 2 * i + u + 1)
                        dve.tensor_tensor(hot_b[u][:, :].rearrange("p (e s) -> p e s", e=E),
                                          slot_b[:, bass.ds(t, 1), :].rearrange("p o e -> p e o").to_broadcast([P, E, SB_]),
                                          iota_b[:, :].rearrange("p (o s) -> p o s", o=1).to_broadcast([P, E, SB_]),
                                          ALU.is_equal)
                        dve.tensor_tensor(hot_a[u][:, :, :],
                                          slot_a[:, bass.ds(t, 1), :].rearrange("p o e -> p e o").to_broadcast([P, E, SA]),
                                          iota_a[:, :].rearrange("p (o s) -> p o s", o=1).to_broadcast([P, E, SA]),
                                          ALU.is_equal).then_inc(hots, 1)
                dve.wait_ge(tabbed, NT + 2)
                for g in range(E // EG):
                    dve.tensor_tensor(picked[:, g, :, :], ps_tab[g][0:EG * SA, 0:EG * SB_].rearrange("p (e s) -> p e s", e=EG),
                                      diag[:, :, :], ALU.mult)
                dve.drain()
                for g in range(E // EG):
                    dve.tensor_reduce(table[:, g, :], picked[:, g, :, :].rearrange("p e s -> p s e"), AX.X, ALU.add)
                dve.drain()
                dve.tensor_scalar(table2[:, :, :], table[:, :, :], float(DUMP), None, ALU.add).then_inc(tab_done, 1)
                dve.wait_ge(turned, 1)
                dve.tensor_copy(idx[:, :], ps_cum[0][0:HALF, 0:2 * E])
                dve.drain()
                dve.tensor_scalar(off[:, :], idx[:, :], float(DUMP), dump[:, :], ALU.is_ge, ALU.mult)
                dve.drain()
                dve.tensor_tensor(slots[:, :], idx[:, :], off[:, :], ALU.add)

            @block.tensor
            def _(pe):
                pe.wait_ge(mask_done, 1)
                for i in range(2):
                    cols = flat(mask_bf)[:, i * 512:(i + 1) * 512]
                    pe.matmul(ps_cum[i][:, :], k.upto_bf[:, :], cols, start=True, stop=True)
                    got = pe.matmul(ps_tot[i][:, :], k.ones_bf[:, :], cols, start=True, stop=True)
                got.then_inc(counted, 1)
                pe.sem_inc(tabbed, 2)

                def body(i, u, first=False, last=False):
                    pe.wait_ge(ida, 2 * i + u + 1)
                    for g in range(E // EG):
                        got = pe.matmul(ps_tab[g][0:EG * SA, 0:EG * SB_], id_a[u][:, g * EG * SA:(g + 1) * EG * SA],
                                        hot_b[u][:, g * EG * SB_:(g + 1) * EG * SB_], start=first, stop=last)
                    got.then_inc(tabbed, 1)

                body(0, 0, first=True)
                body(0, 1)
                with pe.Fori(1, NT // 2 - 1) as i:
                    body(i, 0)
                    body(i, 1)
                body(NT // 2 - 1, 0)
                body(NT // 2 - 1, 1, last=True)
                pe.wait_ge(t_read, 16)
                pe.transpose(ps_cum[0][0:HALF, 0:2 * E], rows[:, :], k.ident[0:2 * E, 0:2 * E]).then_inc(turned, 1)


def routed_experts(nc, a, k, n, htab, acc, slots):
    with ExitStack() as ctx:
        sb = lambda name, shape, dt: ctx.enter_context(nc.sbuf_tensor(f"{name}{n}", shape, dt))
        pb = lambda name: ctx.enter_context(nc.psum_tensor(f"{name}{n}", [P, 512], F32))
        sem = lambda name: ctx.enter_context(nc.semaphore(f"{name}{n}"))
        raw = [sb(f"e_raw{u}_", [P, WALL], F32) for u in range(2)]
        w_hi = [sb(f"e_w_hi{u}_", [P, WALL], F32R) for u in range(2)]
        w_lo = [sb(f"e_w_lo{u}_", [P, WALL], F32R) for u in range(2)]
        gather_idx = [[sb(f"e_gather_idx{u}{q}_", [HALF, 1], U32) for q in range(2)] for u in range(2)]
        add_idx = [[sb(f"e_add_idx{u}{q}_", [HALF, 1], U32) for q in range(2)] for u in range(2)]
        xg = [[sb(f"e_xg{u}{q}_", [HALF, ROW], F32) for q in range(2)] for u in range(2)]
        xt_hi = [sb(f"e_xt_hi{u}_", [P, KB, CAP], F32R) for u in range(2)]
        xt_lo = [sb(f"e_xt_lo{u}_", [P, KB, CAP], F32R) for u in range(2)]
        wcol = sb("e_wcol", [HALF, 2 * E], F32)
        silu = sb("e_silu", [HALF, 2, FF], F32)
        inter = sb("e_inter", [HALF, 2, FF], F32)
        in_hi = sb("e_in_hi", [P, FB * CAP], F32R)
        in_lo = sb("e_in_lo", [P, FB * CAP], F32R)
        y = [[sb(f"e_y{u}{q}_", [HALF, D], F32) for q in range(2)] for u in range(2)]
        ps_t = [pb(f"e_ps_t{i}_") for i in range(2)]
        ps_gu = [pb(f"e_ps_gu{q}_") for q in range(2)]
        ps_in = pb("e_ps_in")
        ps_down = [pb(f"e_ps_down{q}_") for q in range(2)]
        w_loaded = [sem(f"e_w_loaded{u}_") for u in range(2)]
        gathered = [sem(f"e_gathered{u}_") for u in range(2)]
        added, y_free = sem("e_added"), sem("e_y_free")
        hi_ready, lo_ready = sem("e_hi_ready"), sem("e_lo_ready")
        t_ready, t_hi, t_lo, col_done = sem("e_t_ready"), sem("e_t_hi"), sem("e_t_lo"), sem("e_col_done")
        gu_ready, silu_ready, mul_ready = sem("e_gu_ready"), sem("e_silu_ready"), sem("e_mul_ready")
        in_turned, ihi_ready, ilo_ready = sem("e_in_turned"), sem("e_ihi_ready"), sem("e_ilo_ready")
        d_ready, y_ready = sem("e_d_ready"), sem("e_y_ready")
        TC = 2 * CAP
        THIRD = WALL // 3

        with nc.Block() as block:

            @block.sync
            def _(sp):
                for u in range(2):
                    sp.dma_start(raw[u][:, :], a["w_experts"][u, :, :]).then_inc(w_loaded[u], 16)
                with sp.Fori(0, E // 2 - 1) as i:
                    for u in range(2):
                        e = 2 * i + u
                        sp.wait_ge(lo_ready, 3 * e + 3)
                        sp.dma_start(raw[u][:, :], a["w_experts"][bass.ds(e + 2, 1), :, :].rearrange("o p c -> p (o c)")).then_inc(w_loaded[u], 16)

            @block.gpsimd
            def _(pool):
                pool.sem_inc(y_free, 2)

                def gather(i, u):
                    e = 2 * i + u
                    for q in range(2):
                        pool.tensor_copy(gather_idx[u][q][:, :], slots[:, bass.ds(2 * e + q, 1)])
                    pool.drain()
                    for q in range(2):
                        pool.indirect_dma_start(xg[u][q][:, :], None, htab,
                                                bass.IndirectOffsetOnAxis(ap=gather_idx[u][q][:, 0:1], axis=0)).then_inc(gathered[u], 16)

                def scatter(i, u):
                    e = 2 * i + u
                    pool.wait_ge(y_ready, 2 * e + 2 + 2)
                    for q in range(2):
                        pool.tensor_copy(add_idx[u][q][:, :], slots[:, bass.ds(2 * e + q, 1)])
                    pool.drain()
                    for q in range(2):
                        pool.indirect_dma_start(acc, bass.IndirectOffsetOnAxis(ap=add_idx[u][q][:, 0:1], axis=0),
                                                y[u][q][:, :], None, compute_op=ALU.add).then_inc(added, 16)
                    pool.wait_ge(added, 32 * e + 32)
                    pool.sem_inc(y_free, 1)

                def step(i, u):
                    pool.wait_ge(col_done, 2 * i + u + 1)
                    gather(i + 1, u)
                    if u == 1:
                        scatter(i, 0)
                    else:
                        scatter(i - 1, 1)

                gather(0, 0)
                gather(0, 1)
                pool.wait_ge(col_done, 1)
                gather(1, 0)
                with pool.Fori(0, E // 2 - 2) as i:
                    step(i, 1)
                    step(i + 1, 0)
                step(E // 2 - 2, 1)
                scatter(E // 2 - 2, 1)
                scatter(E // 2 - 1, 0)
                scatter(E // 2 - 1, 1)

            @block.scalar
            def _(act):
                act.sem_inc(y_ready, 2)

                def split(i, u, thirds):
                    act.wait_ge(w_loaded[u], 16 * i + 16)
                    for c in thirds:
                        cols = slice(c * THIRD, (c + 1) * THIRD)
                        act.activation(w_hi[u][:, cols], raw[u][:, cols], ACT.Copy).then_inc(hi_ready, 1)

                def turn(i, u):
                    e = 2 * i + u
                    for c in range(2):
                        act.wait_ge(t_ready, 2 * e + c + 1)
                        act.activation(xt_hi[u][:, 2 * c:2 * c + 2, :].rearrange("p k s -> p (k s)"),
                                       ps_t[c][:, 0:TC], ACT.Copy).then_inc(t_hi, 1)

                def gate(i, u):
                    e = 2 * i + u
                    for q in range(2):
                        act.wait_ge(gu_ready, 2 * e + q + 1)
                        act.activation(silu[:, q, :], ps_gu[q][0:HALF, 0:FF], ACT.Silu).then_inc(silu_ready, 1)

                def turn_inner(i, u):
                    act.wait_ge(in_turned, 2 * i + u + 1)
                    act.activation(in_hi[:, :], ps_in[:, 0:FB * CAP], ACT.Copy).then_inc(ihi_ready, 1)

                def weigh(i, u):
                    e = 2 * i + u
                    act.wait_ge(y_free, e + 1)
                    act.wait_ge(col_done, e + 1)
                    for q in range(2):
                        act.wait_ge(d_ready, 2 * e + q + 1)
                        act.activation(y[u][q][:, :], ps_down[q][0:HALF, :], ACT.Copy,
                                       scale=wcol[:, bass.ds(2 * e + q, 1)]).then_inc(y_ready, 1)

                def step(i, u, ahead=True, behind=True):
                    ni, nu = (i, 1) if u == 0 else (i + 1, 0)
                    pi = i if u == 1 else i - 1
                    if behind:
                        turn_inner(pi, nu)
                    if ahead:
                        turn(ni, nu)
                        split(ni, nu, (0, 1))
                    gate(i, u)
                    if behind:
                        weigh(pi, nu)
                    if ahead:
                        split(ni, nu, (2,))

                turn(0, 0)
                split(0, 0, (0, 1, 2))
                step(0, 0, behind=False)
                with act.Fori(0, E // 2 - 1) as i:
                    step(i, 1)
                    step(i + 1, 0)
                step(E // 2 - 1, 1, ahead=False)
                turn_inner(E // 2 - 1, 1)
                weigh(E // 2 - 1, 1)

            @block.vector
            def _(dve):
                dve.sem_inc(t_lo, 2)
                dve.sem_inc(mul_ready, 2)
                dve.sem_inc(ilo_ready, 1)

                def split(i, u, thirds):
                    e = 2 * i + u
                    for c in thirds:
                        cols = slice(c * THIRD, (c + 1) * THIRD)
                        dve.wait_ge(hi_ready, 3 * e + c + 1)
                        dve.tensor_tensor(w_lo[u][:, cols], raw[u][:, cols], w_hi[u][:, cols].bitcast(F32),
                                          ALU.subtract).then_inc(lo_ready, 1)

                def turn(i, u):
                    e = 2 * i + u
                    for c in range(2):
                        dve.wait_ge(t_hi, 2 * e + c + 1)
                        dve.tensor_tensor(xt_lo[u][:, 2 * c:2 * c + 2, :].rearrange("p k s -> p (k s)"), ps_t[c][:, 0:TC],
                                          xt_hi[u][:, 2 * c:2 * c + 2, :].rearrange("p k s -> p (k s)").bitcast(F32),
                                          ALU.subtract).then_inc(t_lo, 1)
                    for q in range(2):
                        got = dve.tensor_scalar(wcol[:, bass.ds(2 * e + q, 1)], xg[u][q][:, bass.ds(D + e, 1)],
                                                1.0, None, ALU.mult)
                    got.then_inc(col_done, 1)

                def gate(i, u):
                    e = 2 * i + u
                    for q in range(2):
                        dve.wait_ge(silu_ready, 2 * e + q + 1)
                        dve.tensor_tensor(inter[:, q, :], silu[:, q, :], ps_gu[q][0:HALF, FF:2 * FF],
                                          ALU.mult).then_inc(mul_ready, 1)

                def turn_inner(i, u):
                    dve.wait_ge(ihi_ready, 2 * i + u + 1)
                    dve.tensor_tensor(in_lo[:, :], ps_in[:, 0:FB * CAP], in_hi[:, :].bitcast(F32),
                                      ALU.subtract).then_inc(ilo_ready, 1)

                def step(i, u, ahead=True, behind=True):
                    ni, nu = (i, 1) if u == 0 else (i + 1, 0)
                    if behind:
                        turn_inner(i if u == 1 else i - 1, nu)
                    if ahead:
                        turn(ni, nu)
                        split(ni, nu, (0, 1))
                    gate(i, u)
                    if ahead:
                        split(ni, nu, (2,))

                turn(0, 0)
                split(0, 0, (0, 1, 2))
                step(0, 0, behind=False)
                with dve.Fori(0, E // 2 - 1) as i:
                    step(i, 1)
                    step(i + 1, 0)
                step(E // 2 - 1, 1, ahead=False)
                turn_inner(E // 2 - 1, 1)

            @block.tensor
            def _(pe):
                def turn(i, u):
                    e = 2 * i + u
                    pe.wait_ge(gathered[u], 32 * i + 32)
                    for c in range(2):
                        pe.wait_ge(t_lo, 2 * e + c + 1)
                        for b in range(2):
                            for q in range(2):
                                at = b * CAP + q * HALF
                                got = pe.transpose(ps_t[c][:, at:at + HALF],
                                                   xg[u][q][:, (2 * c + b) * P:(2 * c + b + 1) * P],
                                                   k.ident[0:HALF, 0:HALF])
                        got.then_inc(t_ready, 1)

                def gate_up(i, u):
                    e = 2 * i + u
                    w = [t[u][:, 0:WGU].rearrange("p (k c) -> p k c", k=KB) for t in (w_hi, w_lo)]
                    pe.wait_ge(t_lo, 2 * e + 2 + 2)
                    pe.wait_ge(lo_ready, 3 * e + 2)
                    for q in range(2):
                        pe.wait_ge(mul_ready, 2 * e + q + 1)
                        s = slice(q * HALF, (q + 1) * HALF)
                        for c in range(KB):
                            got = split_products(pe, ps_gu[q][0:HALF, :], (xt_hi[u][:, c, s], xt_lo[u][:, c, s]),
                                                 (w[0][:, c, :], w[1][:, c, :]), c == 0, c == KB - 1)
                        got.then_inc(gu_ready, 1)

                def turn_inner(i, u):
                    e = 2 * i + u
                    pe.wait_ge(mul_ready, 2 * e + 2 + 2)
                    pe.wait_ge(ilo_ready, e + 1)
                    for b in range(FB):
                        for q in range(2):
                            at = b * CAP + q * HALF
                            got = pe.transpose(ps_in[:, at:at + HALF], inter[:, q, b * P:(b + 1) * P],
                                               k.ident[0:HALF, 0:HALF])
                    got.then_inc(in_turned, 1)

                def down(i, u):
                    e = 2 * i + u
                    w = [t[u][:, WGU:].rearrange("p (k c) -> p k c", k=FB) for t in (w_hi, w_lo)]
                    pe.wait_ge(lo_ready, 3 * e + 3)
                    pe.wait_ge(ilo_ready, e + 1 + 1)
                    for q in range(2):
                        pe.wait_ge(y_ready, 2 * e + q + 1)
                        for b in range(FB):
                            s = slice(b * CAP + q * HALF, b * CAP + (q + 1) * HALF)
                            got = split_products(pe, ps_down[q][0:HALF, :], (in_hi[:, s], in_lo[:, s]),
                                                 (w[0][:, b, :], w[1][:, b, :]), b == 0, b == FB - 1)
                        got.then_inc(d_ready, 1)

                turn(0, 0)
                turn(0, 1)
                gate_up(0, 0)
                with pe.Fori(0, E // 2 - 1) as i:
                    for u in range(2):
                        turn_inner(i, u)
                        turn(i + 1, u)
                        gate_up(i if u == 0 else i + 1, 1 - u)
                        down(i, u)
                turn_inner(E // 2 - 1, 0)
                gate_up(E // 2 - 1, 1)
                down(E // 2 - 1, 0)
                turn_inner(E // 2 - 1, 1)
                down(E // 2 - 1, 1)


def attention(nc, a, k, src, dst):
    softmax_scale = DH ** -0.5
    HK = H + 1
    with ExitStack() as ctx:
        sb = lambda name, shape, dt: ctx.enter_context(nc.sbuf_tensor(name, shape, dt))
        sem = lambda name: ctx.enter_context(nc.semaphore(name))
        rope_c = sb("a_rope_c", [P, NQ, HK, DH], F32)
        rope_s = sb("a_rope_s", [P, NQ, HK, DH], F32)
        qt = [sb(f"a_qt_{part}", [P, H, SEQ], F32R) for part in ("hi", "lo")]
        kt_ = [sb(f"a_kt_{part}", [P, SEQ], F32R) for part in ("hi", "lo")]
        v = [sb(f"a_v_{part}", [P, NQ, DH], F32R) for part in ("hi", "lo")]
        q_scale = sb("a_q_scale", [P, NQ, H], F32)
        loaded = sem("a_loaded")
        x_loaded = [sem(f"a_x_loaded{u}") for u in range(2)]
        stats_ready, std_ready, h_ready = sem("a_stats"), sem("a_std_ready"), sem("a_h_ready")
        t_ready, t_hi, t_lo = sem("a_t_ready"), sem("a_t_hi"), sem("a_t_lo")
        proj_ready, raw_ready, rms_ready = sem("a_proj_ready"), sem("a_raw_ready"), sem("a_rms_ready")
        rot_ready, qk_turned, qk_hi, qk_lo = sem("a_rot_ready"), sem("a_qk_turned"), sem("a_qk_hi"), sem("a_qk_lo")
        s_ready, m_ready, exp_ready, p_ready = sem("a_s_ready"), sem("a_m_ready"), sem("a_exp_ready"), sem("a_p_ready")
        p_turned, p_hi, p_lo = sem("a_p_turned"), sem("a_p_hi"), sem("a_p_lo")
        o_ready, o_hi, o_lo = sem("a_o_ready"), sem("a_o_hi"), sem("a_o_lo")
        out_ready, y_done, stored_all = sem("a_out_ready"), sem("a_y_done"), sem("a_stored_all")
        r_loaded = [sem(f"a_r_loaded{u}") for u in range(2)]
        y_stored = [sem(f"a_y_stored{u}") for u in range(2)]

        with ExitStack() as inner:
            sbi = lambda name, shape, dt: inner.enter_context(nc.sbuf_tensor(name, shape, dt))
            cos = sbi("a_cos", [P, NQ, DH // 2], F32)
            sin = sbi("a_sin", [P, NQ, DH // 2], F32)
            gains = sbi("a_gains", [P, HK, DH], F32)
            with nc.Block() as block:

                @block.sync
                def _(sp):
                    for t, name in ((cos, "cos"), (sin, "sin"), (gains, "gains")):
                        sp.dma_start(t[:, :, :], a[name]).then_inc(loaded, 16)

                @block.scalar
                def _(act):
                    act.sem_inc(exp_ready, 2)

                @block.vector
                def _(dve):
                    dve.sem_inc(t_lo, 2)
                    dve.sem_inc(rot_ready, 2)
                    dve.sem_inc(qk_lo, 1)
                    dve.sem_inc(p_lo, 2)
                    dve.sem_inc(o_lo, 1)
                    dve.sem_inc(y_done, 1)
                    dve.wait_ge(loaded, 48)
                    half = DH // 2
                    for m in range(HK):
                        even = gains[:, m:m + 1, 0:half].to_broadcast([P, NQ, half])
                        odd = gains[:, m:m + 1, half:DH].to_broadcast([P, NQ, half])
                        dve.tensor_tensor(rope_c[:, :, m, 0:half], cos[:, :, :], even, ALU.mult)
                        dve.tensor_tensor(rope_c[:, :, m, half:DH], cos[:, :, :], odd, ALU.mult)
                        dve.scalar_tensor_tensor(rope_s[:, :, m, 0:half], sin[:, :, :], -1.0, odd, ALU.mult, ALU.mult)
                        dve.tensor_tensor(rope_s[:, :, m, half:DH], sin[:, :, :], even, ALU.mult)

        with nc.Fori(0, B) as b:
            project_qkv(nc, k, b, src, softmax_scale, HK, rope_c, rope_s, qt, kt_, v, q_scale,
                        (x_loaded, stats_ready, std_ready, h_ready, t_ready, t_hi, t_lo, proj_ready, raw_ready,
                         rms_ready, rot_ready, qk_turned, qk_hi, qk_lo))
            attend(nc, k, b, src, dst, qt, kt_, v, q_scale,
                   (s_ready, m_ready, exp_ready, p_ready, p_turned, p_hi, p_lo, o_ready, o_hi, o_lo,
                    out_ready, y_done, r_loaded, y_stored, stored_all))


def project_qkv(nc, k, b, src, softmax_scale, HK, rope_c, rope_s, qt, kt_, v, q_scale, sems):
    (x_loaded, stats_ready, std_ready, h_ready, t_ready, t_hi, t_lo, proj_ready, raw_ready,
     rms_ready, rot_ready, qk_turned, qk_hi, qk_lo) = sems
    with ExitStack() as ctx:
        sb = lambda name, shape, dt: ctx.enter_context(nc.sbuf_tensor(name, shape, dt))
        pb = lambda name: ctx.enter_context(nc.psum_tensor(name, [P, 512], F32))
        x = [sb(f"q_x{u}", [P, D], F32) for u in range(2)]
        h = [sb(f"q_h{u}", [P, D], F32) for u in range(2)]
        stats = sb("q_stats", [P, 6], F32)
        mv = [sb(f"q_mv{u}", [P, 2], F32) for u in range(2)]
        std = [sb(f"q_std{u}", [P, 1], F32) for u in range(2)]
        rstd = [sb(f"q_rstd{u}", [P, 1], F32) for u in range(2)]
        ht = [[sb(f"q_ht{part}{u}", [P, KB, P], F32R) for u in range(2)] for part in range(2)]
        raw = [sb(f"q_raw{u}", [P, HK, DH], F32) for u in range(2)]
        square = sb("q_square", [P, HK, DH], F32)
        sum_sq = [sb(f"q_sum_sq{u}", [P, HK], F32) for u in range(2)]
        rms = [sb(f"q_rms{u}", [P, HK], F32) for u in range(2)]
        inv = [sb(f"q_inv{u}", [P, HK], F32) for u in range(2)]
        by_cos = [sb(f"q_by_cos{u}", [P, HK, DH], F32) for u in range(2)]
        by_sin = [sb(f"q_by_sin{u}", [P, HK, DH], F32) for u in range(2)]
        rot = [sb(f"q_rot{u}", [P, HK, DH], F32) for u in range(2)]
        ps_t = [pb(f"q_ps_t{u}") for u in range(2)]
        ps_q = [pb(f"q_ps_q{u}") for u in range(2)]
        ps_kv = [pb(f"q_ps_kv{u}") for u in range(2)]
        ps_qt, ps_kt = pb("q_ps_qt"), pb("q_ps_kt")
        half = DH // 2
        n0 = b * NQ

        with nc.Block() as block:

            @block.sync
            def _(sp):
                for j in range(NQ):
                    row = sp.snap(b * SEQ + j * P)
                    if j >= 2:
                        sp.wait_ge(h_ready, n0 + j - 1)
                    sp.dma_start(x[j % 2][:, :], src[bass.ds(row, P), :]).then_inc(x_loaded[j % 2], 16)

            @block.scalar
            def _(act):
                def root(j):
                    act.wait_ge(stats_ready, n0 + j + 1)
                    act.activation(std[j % 2][:, :], mv[j % 2][:, 1:2], ACT.Sqrt, bias=k.ln_eps[:, :]).then_inc(std_ready, 1)

                def turn(j):
                    act.wait_ge(t_ready, n0 + j + 1)
                    act.activation(ht[0][j % 2][:, :, :].rearrange("p k t -> p (k t)"), ps_t[j % 2][:, :],
                                   ACT.Copy).then_inc(t_hi, 1)

                def unload(j):
                    u = j % 2
                    act.wait_ge(proj_ready, n0 + j + 1)
                    act.activation(v[0][:, j, :], ps_kv[u][:, DH:2 * DH], ACT.Copy)
                    act.activation(raw[u][:, 0:H, :].rearrange("p m d -> p (m d)"), ps_q[u][:, :], ACT.Copy)
                    act.activation(raw[u][:, H, :], ps_kv[u][:, 0:DH], ACT.Copy).then_inc(raw_ready, 1)
                    act.drain()
                    for m in range(HK):
                        act.activation(square[:, m, :], raw[u][:, m, :], ACT.Square, accum_out=sum_sq[u][:, m:m + 1])
                    act.drain()
                    act.activation(rms[u][:, :], sum_sq[u][:, :], ACT.Sqrt, scale=1.0 / DH,
                                   bias=k.rms_eps[:, :]).then_inc(rms_ready, 1)

                def turn_qk(j):
                    act.wait_ge(qk_turned, n0 + j + 1)
                    tok = slice(j * P, (j + 1) * P)
                    act.activation(qt[0][:, :, tok], ps_qt[:, :].rearrange("p (m t) -> p m t", m=H), ACT.Copy)
                    act.activation(kt_[0][:, tok], ps_kt[:, 0:P], ACT.Copy).then_inc(qk_hi, 1)

                root(0)
                turn(0)
                root(1)
                for j in range(NQ):
                    if j + 1 < NQ:
                        turn(j + 1)
                    if j + 2 < NQ:
                        root(j + 2)
                    unload(j)
                    if j:
                        turn_qk(j - 1)
                turn_qk(NQ - 1)

            @block.vector
            def _(dve):
                def layernorm(j):
                    u = j % 2
                    dve.wait_ge(x_loaded[u], b * 16 * (NQ // 2) + 16 * (j // 2) + 16)
                    dve.bn_stats(stats[:, :], x[u][:, :])
                    dve.drain()
                    dve.bn_aggr(mv[u][:, :], stats[:, :]).then_inc(stats_ready, 1)
                    dve.wait_ge(std_ready, n0 + j + 1)
                    dve.reciprocal(rstd[u][:, :], std[u][:, :])
                    dve.drain()
                    dve.tensor_scalar(h[u][:, :], x[u][:, :], mv[u][:, 0:1], rstd[u][:, :],
                                      ALU.subtract, ALU.mult).then_inc(h_ready, 1)

                def turn(j):
                    u = j % 2
                    dve.wait_ge(t_hi, n0 + j + 1)
                    dve.tensor_tensor(ht[1][u][:, :, :].rearrange("p k t -> p (k t)"), ps_t[u][:, :],
                                      ht[0][u][:, :, :].rearrange("p k t -> p (k t)").bitcast(F32),
                                      ALU.subtract).then_inc(t_lo, 1)

                def rotate(j):
                    u = j % 2
                    dve.wait_ge(raw_ready, n0 + j + 1)
                    dve.tensor_tensor(v[1][:, j, :], ps_kv[u][:, DH:2 * DH], v[0][:, j, :].bitcast(F32), ALU.subtract)
                    dve.tensor_tensor(by_cos[u][:, :, :], raw[u][:, :, :], rope_c[:, j, :, :], ALU.mult)
                    dve.tensor_tensor(by_sin[u][:, :, 0:half], raw[u][:, :, half:DH], rope_s[:, j, :, 0:half], ALU.mult)
                    dve.tensor_tensor(by_sin[u][:, :, half:DH], raw[u][:, :, 0:half], rope_s[:, j, :, half:DH], ALU.mult)
                    dve.wait_ge(rms_ready, n0 + j + 1)
                    dve.reciprocal(inv[u][:, :], rms[u][:, :])
                    dve.drain()
                    dve.tensor_scalar(q_scale[:, j, :], inv[u][:, 0:H], softmax_scale, None, ALU.mult)
                    dve.tensor_tensor(rot[u][:, 0:H, :], by_cos[u][:, 0:H, :], by_sin[u][:, 0:H, :], ALU.add)
                    dve.tensor_tensor(by_cos[u][:, H, :], by_cos[u][:, H, :], by_sin[u][:, H, :], ALU.add)
                    dve.drain()
                    dve.tensor_scalar(rot[u][:, H, :], by_cos[u][:, H, :], inv[u][:, H:HK], None,
                                      ALU.mult).then_inc(rot_ready, 1)

                def turn_qk(j):
                    dve.wait_ge(qk_hi, n0 + j + 1)
                    tok = slice(j * P, (j + 1) * P)
                    dve.tensor_tensor(qt[1][:, :, tok], ps_qt[:, :].rearrange("p (m t) -> p m t", m=H),
                                      qt[0][:, :, tok].bitcast(F32), ALU.subtract)
                    dve.tensor_tensor(kt_[1][:, tok], ps_kt[:, 0:P], kt_[0][:, tok].bitcast(F32),
                                      ALU.subtract).then_inc(qk_lo, 1)

                layernorm(0)
                turn(0)
                layernorm(1)
                for j in range(NQ):
                    if j + 1 < NQ:
                        turn(j + 1)
                    if j + 2 < NQ:
                        layernorm(j + 2)
                    rotate(j)
                    if j:
                        turn_qk(j - 1)
                turn_qk(NQ - 1)

            @block.tensor
            def _(pe):
                def turn(j):
                    u = j % 2
                    pe.wait_ge(h_ready, n0 + j + 1)
                    pe.wait_ge(t_lo, n0 + j + 1)
                    for c in range(KB):
                        got = pe.transpose(ps_t[u][:, c * P:(c + 1) * P], h[u][:, c * P:(c + 1) * P], k.ident[:, :])
                    got.then_inc(t_ready, 1)

                def project(j):
                    u = j % 2
                    pe.wait_ge(t_lo, n0 + j + 1 + 2)
                    pe.wait_ge(rot_ready, n0 + j + 1)
                    for bank, at, width in ((ps_q[u], 0, H * DH), (ps_kv[u], H * DH, 2 * DH)):
                        for c in range(KB):
                            got = split_products(pe, bank[:, 0:width], (ht[0][u][:, c, :], ht[1][u][:, c, :]),
                                                 (k.wqkv_hi[:, c, at:at + width], k.wqkv_lo[:, c, at:at + width]),
                                                 c == 0, c == KB - 1)
                    got.then_inc(proj_ready, 1)

                def turn_qk(j):
                    u = j % 2
                    pe.wait_ge(rot_ready, n0 + j + 1 + 2)
                    pe.wait_ge(qk_lo, n0 + j + 1)
                    for m in range(H):
                        pe.transpose(ps_qt[:, m * P:(m + 1) * P], rot[u][:, m, :], k.ident[:, :])
                    pe.transpose(ps_kt[:, 0:P], rot[u][:, H, :], k.ident[:, :]).then_inc(qk_turned, 1)

                turn(0)
                for j in range(NQ):
                    if j + 1 < NQ:
                        turn(j + 1)
                    project(j)
                    if j:
                        turn_qk(j - 1)
                turn_qk(NQ - 1)


def attend(nc, k, b, src, dst, qt, kt_, v, q_scale, sems):
    (s_ready, m_ready, exp_ready, p_ready, p_turned, p_hi, p_lo, o_ready, o_hi, o_lo,
     out_ready, y_done, r_loaded, y_stored, stored_all) = sems
    with ExitStack() as ctx:
        sb = lambda name, shape, dt: ctx.enter_context(nc.sbuf_tensor(name, shape, dt))
        res = [sb(f"t_res{u}", [P, D], F32) for u in range(2)]
        top = [sb(f"t_top{u}", [P, H], F32) for u in range(2)]
        neg_max = [sb(f"t_neg_max{u}", [P, H], F32) for u in range(2)]
        total = [sb(f"t_total{u}", [P, H], F32) for u in range(2)]
        inv = [sb(f"t_inv{u}", [P, H], F32) for u in range(2)]
        prob = [sb(f"t_prob{u}", [P, H, SEQ], F32) for u in range(2)]
        pt = [[sb(f"t_pt{part}{r}", [P, H * P], F32R) for r in range(2)] for part in range(2)]
        ot = [sb(f"t_ot{part}", [P, H * P], F32R) for part in range(2)]
        ps_s = [ctx.enter_context(nc.psum_tensor(f"t_ps_s{i}", [P, SEQ], F32)) for i in range(2)]
        ps_p = [ctx.enter_context(nc.psum_tensor(f"t_ps_p{i}", [P, 512], F32)) for i in range(2)]
        ps_o = ctx.enter_context(nc.psum_tensor("t_ps_o", [P, 512], F32))
        ps_y = ctx.enter_context(nc.psum_tensor("t_ps_y", [P, 512], F32))
        order = QUERY_ORDER
        keys = lambda s: order[s] + 1
        base = [sum(keys(i) for i in range(s)) for s in range(NQ)]
        turned0 = b * (NQ * (NQ + 1) // 2)
        n0 = b * NQ
        quarter = lambda s, i: range(keys(s) * i // H, keys(s) * (i + 1) // H)

        with nc.Block() as block:

            @block.sync
            def _(sp):
                row = lambda s: sp.snap(b * SEQ + order[s] * P)
                for s in range(2):
                    sp.dma_start(res[s][:, :], src[bass.ds(row(s), P), :]).then_inc(r_loaded[s], 16)
                for s in range(NQ):
                    u = s % 2
                    this, following = row(s), row(s + 2) if s + 2 < NQ else None
                    sp.wait_ge(y_done, n0 + s + 1 + 1)
                    sp.dma_start(dst[bass.ds(this, P), :], res[u][:, :]).then_inc(y_stored[u], 16)
                    if s + 2 < NQ:
                        sp.wait_ge(y_stored[u], b * 16 * (NQ // 2) + 16 * (s // 2) + 16)
                        sp.dma_start(res[u][:, :], src[bass.ds(following, P), :]).then_inc(r_loaded[u], 16)
                for u in range(2):
                    sp.wait_ge(y_stored[u], b * 16 * (NQ // 2) + 16 * (NQ // 2))
                sp.sem_inc(stored_all, 1)

            @block.scalar
            def _(act):
                def soften(s, m):
                    u = s % 2
                    act.wait_ge(m_ready, (n0 + s) * H + m + 1)
                    act.activation(prob[u][:, m, 0:keys(s) * P], ps_s[m % 2][:, 0:keys(s) * P], ACT.Exp,
                                   scale=q_scale[:, order[s], m:m + 1], bias=neg_max[u][:, m:m + 1],
                                   accum_out=total[u][:, m:m + 1]).then_inc(exp_ready, 1)

                def turn(s, c):
                    at = base[s] + c
                    act.wait_ge(p_turned, turned0 + at + 1)
                    act.activation(pt[0][at % 2][:, :], ps_p[at % 2][:, :], ACT.Copy).then_inc(p_hi, 1)

                def collect(s):
                    act.wait_ge(o_ready, n0 + s + 1)
                    act.activation(ot[0][:, :], ps_o[:, :], ACT.Copy).then_inc(o_hi, 1)

                for m in range(H):
                    soften(0, m)
                for s in range(NQ):
                    if s:
                        collect(s - 1)
                    for m in range(H):
                        if s + 1 < NQ:
                            soften(s + 1, m)
                        for c in quarter(s, m):
                            turn(s, c)
                collect(NQ - 1)

            @block.vector
            def _(dve):
                def maximum(s, m):
                    u = s % 2
                    dve.wait_ge(s_ready, (n0 + s) * H + m + 1)
                    dve.reduce_max(top[u][:, m:m + 1], ps_s[m % 2][:, 0:keys(s) * P], AX.X)
                    dve.drain()
                    dve.tensor_scalar(neg_max[u][:, m:m + 1], top[u][:, m:m + 1], q_scale[:, order[s], m:m + 1], -1.0,
                                      ALU.mult, ALU.mult).then_inc(m_ready, 1)

                def normalise(s):
                    u = s % 2
                    dve.wait_ge(exp_ready, (n0 + s) * H + H + 2)
                    dve.reciprocal(inv[u][:, :], total[u][:, :])
                    dve.drain()
                    for m in range(H):
                        got = dve.tensor_scalar(prob[u][:, m, 0:keys(s) * P], prob[u][:, m, 0:keys(s) * P],
                                                inv[u][:, m:m + 1], None, ALU.mult)
                    got.then_inc(p_ready, 1)

                def turn(s, c):
                    at = base[s] + c
                    dve.wait_ge(p_hi, turned0 + at + 1)
                    dve.tensor_tensor(pt[1][at % 2][:, :], ps_p[at % 2][:, :], pt[0][at % 2][:, :].bitcast(F32),
                                      ALU.subtract).then_inc(p_lo, 1)

                def collect(s):
                    dve.wait_ge(o_hi, n0 + s + 1)
                    dve.tensor_tensor(ot[1][:, :], ps_o[:, :], ot[0][:, :].bitcast(F32), ALU.subtract).then_inc(o_lo, 1)

                def add_residual(s):
                    u = s % 2
                    dve.wait_ge(r_loaded[u], b * 16 * (NQ // 2) + 16 * (s // 2) + 16)
                    dve.wait_ge(out_ready, n0 + s + 1)
                    dve.tensor_tensor(res[u][:, :], ps_y[:, :], res[u][:, :], ALU.add).then_inc(y_done, 1)

                for m in range(H):
                    maximum(0, m)
                normalise(0)
                for s in range(NQ):
                    if s:
                        collect(s - 1)
                    for m in range(H):
                        if s + 1 < NQ:
                            maximum(s + 1, m)
                        for c in quarter(s, m):
                            turn(s, c)
                        if s and m == 1:
                            add_residual(s - 1)
                    if s + 1 < NQ:
                        normalise(s + 1)
                collect(NQ - 1)
                add_residual(NQ - 1)

            @block.tensor
            def _(pe):
                def scores(s, m):
                    j = order[s]
                    pe.wait_ge(exp_ready, (n0 + s) * H + m + 1)
                    tok = slice(j * P, (j + 1) * P)
                    qh, ql = (t[:, m, tok] for t in qt)
                    for at in range(0, keys(s) * P, 512):
                        cols = slice(at, min(at + 512, keys(s) * P))
                        out = ps_s[m % 2][:, cols]
                        pe.matmul(out, qh, kt_[0][:, cols], start=True, stop=False)
                        if cols.stop == keys(s) * P:
                            pe.matmul(ps_s[m % 2][:, tok], k.ident_bf[:, :], k.causal_bf[:, :], start=False, stop=False)
                        pe.matmul(out, qh, kt_[1][:, cols], start=False, stop=False)
                        got = pe.matmul(out, ql, kt_[0][:, cols], start=False, stop=True)
                    got.then_inc(s_ready, 1)

                def turn(s, c):
                    at = base[s] + c
                    pe.wait_ge(p_lo, turned0 + at + 1)
                    for m in range(H):
                        got = pe.transpose(ps_p[at % 2][:, m * P:(m + 1) * P], prob[s % 2][:, m, c * P:(c + 1) * P],
                                           k.ident[:, :])
                    got.then_inc(p_turned, 1)

                def values(s, c):
                    at = base[s] + c
                    pe.wait_ge(p_lo, turned0 + at + 1 + 2)
                    got = split_products(pe, ps_o[:, :], (v[0][:, c, :], v[1][:, c, :]),
                                         (pt[0][at % 2][:, :], pt[1][at % 2][:, :]), c == 0, c == keys(s) - 1)
                    if c == keys(s) - 1:
                        got.then_inc(o_ready, 1)

                def output(s):
                    pe.wait_ge(o_lo, n0 + s + 1 + 1)
                    pe.wait_ge(y_done, n0 + s + 1)
                    for m in range(H):
                        tok = slice(m * P, (m + 1) * P)
                        got = split_products(pe, ps_y[:, :], (ot[0][:, tok], ot[1][:, tok]),
                                             (k.wo_hi[:, m, :], k.wo_lo[:, m, :]), m == 0, m == H - 1)
                    got.then_inc(out_ready, 1)

                for m in range(H):
                    scores(0, m)
                for s in range(NQ):
                    first = True
                    for m in range(H):
                        if s + 1 < NQ:
                            scores(s + 1, m)
                        if s and m == 0:
                            output(s - 1)
                        for c in quarter(s, m):
                            if first:
                                pe.wait_ge(p_ready, n0 + s + 1)
                                pe.wait_ge(o_lo, n0 + s + 1)
                                first = False
                            turn(s, c)
                            if c:
                                values(s, c - 1)
                    values(s, keys(s) - 1)
                output(NQ - 1)


def build_program(nc, a, out):
    with ExitStack() as ctx:
        k = allocate_kept(nc, ctx)
        htab = nc.dram_tensor("htab", [ROWS, ROW], F32).ap()
        x1 = nc.dram_tensor("x_after_ffn", [ROWS, D], F32).ap()
        x2 = nc.dram_tensor("x_after_attention", [TOK, D], F32).ap()
        slot_dram = nc.dram_tensor("slot_table", [E * CAP], F32).ap()
        setup(nc, a, k, htab, (x1, out))

        def ffn(n, src, acc):
            with nc.sbuf_tensor(f"slots{n}", [HALF, 2 * E], U32) as slots:
                with nc.sbuf_tensor(f"logits{n}", [P, NT, 2 * E], F32) as logits:
                    dense_ffn(nc, k, n, src, acc, htab, logits)
                    route(nc, a, k, n, htab, logits, slot_dram, slots)
                routed_experts(nc, a, k, n, htab, acc, slots)

        ffn(0, a["x"], x1)
        attention(nc, a, k, x1, x2)
        ffn(1, x2, out)


def constants():
    tok = np.arange(TOK).reshape(NT, P)
    part, col = np.arange(P)[:, None], np.arange(P)[None, :]
    seg = np.ones((P, NT, E), np.float32)
    seg[:, :, 0] = 0.0
    diag = np.zeros((EG * SA, EG, SB_), np.float32)
    for g in range(EG):
        diag[g * SA:(g + 1) * SA, g, :] = 1.0
    dims = np.arange(DH // 2)
    ang = np.power(np.float32(2500.0), (-dims / (DH // 2)).astype(np.float32)).astype(np.float32)
    rad = np.arange(SEQ).astype(np.float32)[:, None] * ang[None, :]
    turn = lambda t: np.ascontiguousarray(t.astype(np.float32).reshape(NQ, P, DH // 2).transpose(1, 0, 2))
    return {
        "ident": np.eye(P, dtype=np.float32),
        "causal": np.where(col > part, np.float32(-1e30), np.float32(0)).astype(np.float32),
        "upto": (part <= col).astype(np.float32),
        "seg": seg,
        "iota_a": np.broadcast_to(np.arange(SA, dtype=np.float32), (P, SA)).copy(),
        "iota_b": np.broadcast_to(np.arange(SB_, dtype=np.float32), (P, SB_)).copy(),
        "tok_id": (tok.T - DUMP).astype(np.float32),
        "diag": diag,
        "dump": np.arange(HALF, dtype=np.float32)[:, None].copy(),
        "cos": turn(np.cos(rad)),
        "sin": turn(np.sin(rad)),
    }


def laid_out(x, wq, wk, wv, wo, gq, gk, gate_w, bias, w_gate, w_up, w_down, sg, su, sd):
    rows = lambda w, blocks: w.reshape(blocks, P, -1).transpose(1, 0, 2)
    whole = lambda g, u, d: np.concatenate(
        [rows(np.concatenate([g.T, u.T], 1), KB).reshape(P, WGU), rows(d.T, FB).reshape(P, WDN)], 1)
    out = {
        "x": x.reshape(TOK, D),
        "router_w": rows(gate_w.T, KB),
        "bias": np.broadcast_to(bias, (P, E)),
        "w_shared": whole(sg, su, sd),
        "w_experts": np.stack([whole(w_gate[e], w_up[e], w_down[e]) for e in range(E)]),
        "w_qkv": rows(np.concatenate([wq, wk, wv], 1), KB),
        "w_out": rows(wo, H),
        "gains": np.broadcast_to(np.concatenate([gq.reshape(H, DH), gk.reshape(1, DH)], 0), (P, H + 1, DH)),
    }
    return {name: np.ascontiguousarray(t) for name, t in out.items()}


def kernel(**inputs):
    import concourse.bacc as bacc
    from concourse.bass_utils import run_bass_kernel_spmd

    arrays = laid_out(*(np.asarray(inputs[name]) for name in (
        "L0_attn_x", "L0_attn_wq", "L0_attn_wk", "L0_attn_wv", "L0_attn_wo", "L0_attn_gq", "L0_attn_gk",
        "L0_ffn_gate_w", "L0_ffn_bias", "L0_ffn_w_gate", "L0_ffn_w_up", "L0_ffn_w_down",
        "L0_ffn_sg", "L0_ffn_su", "L0_ffn_sd")))
    arrays.update(constants())
    arrays = {f"in_{name}": t for name, t in arrays.items()}
    nc = bacc.Bacc("TRN2", target_bir_lowering=False, num_devices=1)
    a = {name[3:]: nc.dram_tensor(name, t.shape, mybir.dt.from_np(t.dtype), kind="ExternalInput").ap()
         for name, t in arrays.items()}
    out = nc.dram_tensor("out", [ROWS, D], F32, kind="ExternalOutput").ap()
    build_program(nc, a, out)
    got = run_bass_kernel_spmd(nc, [arrays], core_ids=[0])
    return got.results[0]["out"][0:TOK].reshape(B, SEQ, D)
```

```python
from contextlib import ExitStack

import numpy as np

import concourse.bass as bass
from concourse import mybir

F32 = mybir.dt.float32
F32R = mybir.dt.float32r
BF16 = mybir.dt.bfloat16
I32 = mybir.dt.int32
U32 = mybir.dt.uint32
ALU = mybir.AluOpType
ACT = mybir.ActivationFunctionType
AX = mybir.AxisListType

P = 128
B, SEQ, D = 4, 1024, 512
TOK = B * SEQ
NT = TOK // P
KB = D // P
E, TOPK, FF = 32, 6, 256
FB = FF // P
CAP = 192
HALF = CAP // 2
ROUTE_SCALE = 1.5
H, DH = 4, 128
GT = 4
G = NT // GT
GTOK = GT * P
SA, SB_ = 12, 16
ROW = D + E
DUMP = TOK
ROWS = TOK + HALF
EG = 8
NQ = SEQ // P
HEADS = NQ * H
EXP_AHEAD, SCORES_AHEAD = 5, 6
RING = 9
WGU, WDN = KB * 2 * FF, FB * D
WALL = WGU + WDN
NO_SLOT = 4000.0
SWIGLU_LIMIT = 10.0
LN_EPS, RMS_EPS = 1e-5, 1e-6


def split_products(pe, out, hi_lo_weights, hi_lo_moving, first, last):
    wh, wl = hi_lo_weights
    mh, ml = hi_lo_moving
    pe.matmul(out, wh, mh, start=first, stop=False)
    pe.matmul(out, wh, ml, start=False, stop=False)
    return pe.matmul(out, wl, mh, start=False, stop=last)


class Kept:
    pass


def own_semaphore(nc, k, name):
    k.ffn_semaphores.append(nc.alloc_semaphore(name=name))
    return k.ffn_semaphores[-1]


def allocate_kept(nc, ctx):
    k = Kept()
    k.ffn_semaphores = []

    def sb(name, shape, dt):
        return ctx.enter_context(nc.sbuf_tensor(name, shape, dt))

    k.ident = sb("ident", [P, P], F32)
    k.causal_bf = sb("causal_bf", [P, P], BF16)
    k.ident_bf = sb("ident_bf", [P, P], BF16)
    k.upto_bf = sb("upto_bf", [P, P], BF16)
    k.ones_bf = sb("ones_bf", [P, P], BF16)
    k.ln_eps = sb("ln_eps", [P, 1], F32)
    k.rms_eps = sb("rms_eps", [P, 1], F32)
    k.shared_hi = sb("shared_hi", [P, WALL], F32R)
    k.shared_lo = sb("shared_lo", [P, WALL], F32R)
    k.router = sb("router", [P, KB, 3, E], F32R)
    k.wqkv_hi = sb("wqkv_hi", [P, KB, 6 * DH], F32R)
    k.wqkv_lo = sb("wqkv_lo", [P, KB, 6 * DH], F32R)
    k.wo_hi = sb("wo_hi", [P, H, D], F32R)
    k.wo_lo = sb("wo_lo", [P, H, D], F32R)
    return k


def setup(nc, a, k, htab, accs):
    with ExitStack() as ctx:
        sb = lambda name, shape, dt: ctx.enter_context(nc.sbuf_tensor(name, shape, dt))
        sem = lambda name: ctx.enter_context(nc.semaphore(name))
        raw_shared = sb("raw_shared", [P, WALL], F32)
        raw_router = sb("raw_router", [P, KB, E], F32)
        raw_qkv = sb("raw_qkv", [P, KB, 6 * DH], F32)
        raw_wo = sb("raw_wo", [P, H, D], F32)
        raw_causal = sb("raw_causal", [P, P], F32)
        raw_upto = sb("raw_upto", [P, P], F32)
        zeros = sb("zeros", [HALF, ROW], F32)
        no_weights = sb("no_weights", [P, KB, E], F32)
        loaded, zeroed, dumps = sem("setup_loaded"), sem("setup_zeroed"), sem("setup_dumps")
        hi_ready = sem("setup_hi")
        with nc.Block() as block:

            @block.sync
            def _(sp):
                pairs = [(raw_router[:, :, :], a["router_w"]), (k.ident[:, :], a["ident"]),
                         (raw_causal[:, :], a["causal"]), (raw_upto[:, :], a["upto"]),
                         (raw_shared[:, :], a["w_shared"]), (raw_qkv[:, :, :], a["w_qkv"]),
                         (raw_wo[:, :, :], a["w_out"])]
                for dst, src in pairs:
                    sp.dma_start(dst, src).then_inc(loaded, 16)
                sp.wait_ge(zeroed, 1)
                sp.dma_start(htab[DUMP:ROWS, :], zeros[:, :]).then_inc(dumps, 16)
                for acc in accs:
                    sp.dma_start(acc[DUMP:ROWS, :], zeros[:, 0:D]).then_inc(dumps, 16)
                sp.wait_ge(dumps, 16 * (1 + len(accs)))

            @block.gpsimd
            def _(pool):
                pool.memset(k.ones_bf[:, :], 1.0)
                pool.memset(no_weights[:, :, :], 0.0)
                pool.memset(k.ln_eps[:, :], LN_EPS)
                pool.memset(k.rms_eps[:, :], RMS_EPS)
                pool.memset(zeros[:, :], 0.0).then_inc(zeroed, 1)

            @block.scalar
            def _(act):
                act.wait_ge(loaded, 16 * 7)
                act.activation(k.router[:, :, 0, :], raw_router[:, :, :], ACT.Copy)
                act.wait_ge(zeroed, 1)
                act.activation(k.router[:, :, 2, :], no_weights[:, :, :], ACT.Copy)
                act.activation(k.ident_bf[:, :], k.ident[:, :], ACT.Copy)
                act.activation(k.causal_bf[:, :], raw_causal[:, :], ACT.Copy)
                act.activation(k.upto_bf[:, :], raw_upto[:, :], ACT.Copy)
                act.activation(k.shared_hi[:, :], raw_shared[:, :], ACT.Copy)
                act.activation(k.wqkv_hi[:, :, :], raw_qkv[:, :, :], ACT.Copy)
                act.activation(k.wo_hi[:, :, :], raw_wo[:, :, :], ACT.Copy).then_inc(hi_ready, 1)

            @block.vector
            def _(dve):
                dve.wait_ge(hi_ready, 1)
                for lo, raw, hi in ((k.router[:, :, 1, :], raw_router[:, :, :], k.router[:, :, 0, :]),
                                    (k.shared_lo[:, :], raw_shared[:, :], k.shared_hi[:, :]),
                                    (k.wqkv_lo[:, :, :], raw_qkv[:, :, :], k.wqkv_hi[:, :, :]),
                                    (k.wo_lo[:, :, :], raw_wo[:, :, :], k.wo_hi[:, :, :])):
                    dve.tensor_tensor(lo, raw, hi.bitcast(F32), ALU.subtract)


def dense_ffn(nc, k, n, src, acc, htab, logits):
    with ExitStack() as ctx:
        sb = lambda name, shape, dt: ctx.enter_context(nc.sbuf_tensor(f"{name}{n}", shape, dt))
        pb = lambda name: ctx.enter_context(nc.psum_tensor(f"{name}{n}", [P, 512], F32))
        sem = lambda name: own_semaphore(nc, k, f"{name}{n}")
        x = [sb(f"d_x{u}_", [P, GT, D], F32) for u in range(2)]
        h = [sb(f"d_h{u}_", [P, GT, D], F32) for u in range(2)]
        y = [sb(f"d_y{u}_", [P, GT, D], F32) for u in range(2)]
        stats = sb("d_stats", [P, GT, 6], F32)
        mv = [sb(f"d_mv{u}_", [P, GT, 2], F32) for u in range(2)]
        std = [sb(f"d_std{u}_", [P, GT], F32) for u in range(2)]
        rstd = [sb(f"d_rstd{u}_", [P, GT], F32) for u in range(2)]
        ht_hi = [sb(f"d_ht_hi{u}_", [P, KB, GTOK], F32R) for u in range(2)]
        ht_lo = [sb(f"d_ht_lo{u}_", [P, KB, GTOK], F32R) for u in range(2)]
        silu = [sb(f"d_silu{b}_", [P, GTOK], F32) for b in range(FB)]
        inter = [sb(f"d_inter{b}_", [P, GTOK], F32) for b in range(FB)]
        in_hi = [sb(f"d_in_hi{u}_", [P, FB, GTOK], F32R) for u in range(2)]
        in_lo = [sb(f"d_in_lo{u}_", [P, FB, GTOK], F32R) for u in range(2)]
        ps_t = [pb(f"d_ps_t{i}_") for i in range(2)]
        ps_gate = [pb(f"d_ps_gate{b}_") for b in range(FB)]
        ps_up = [pb(f"d_ps_up{b}_") for b in range(FB)]
        ps_down = [pb(f"d_ps_down{i}_") for i in range(2)]
        lg_t = sb("d_lg_t", [3 * E, GTOK], F32)
        x_loaded = [[sem(f"d_x_loaded{u}{m}_") for m in range(2)] for u in range(2)]
        h_stored = [sem(f"d_h_stored{u}_") for u in range(2)]
        y_stored = [sem(f"d_y_stored{u}_") for u in range(2)]
        stats_ready, std_ready, h_ready = sem("d_stats_ready"), sem("d_std_ready"), sem("d_h_ready")
        t_ready, t_hi, t_lo = sem("d_t_ready"), sem("d_t_hi"), sem("d_t_lo")
        lg_ready, lg_out, lg_turned, lg_taken = sem("d_lg_ready"), sem("d_lg_out"), sem("d_lg_turned"), sem("d_lg_taken")
        gu_ready, silu_ready, mul_ready = sem("d_gu_ready"), sem("d_silu_ready"), sem("d_mul_ready")
        ihi_ready, ilo_ready = sem("d_ihi_ready"), sem("d_ilo_ready")
        d_ready, y_done = sem("d_d_ready"), sem("d_y_done")
        gu_hi = k.shared_hi[:, 0:WGU].rearrange("p (k c) -> p k c", k=KB)
        gu_lo = k.shared_lo[:, 0:WGU].rearrange("p (k c) -> p k c", k=KB)
        dn_hi = k.shared_hi[:, WGU:].rearrange("p (k c) -> p k c", k=FB)
        dn_lo = k.shared_lo[:, WGU:].rearrange("p (k c) -> p k c", k=FB)
        group = lambda ap, g: ap[bass.ds(g * GTOK, GTOK), :].rearrange("(j p) d -> p j d", p=P)
        last = G // 2 - 1
        half = lambda ap, g, m: ap[bass.ds(g * GTOK + m * (GTOK // 2), GTOK // 2), :].rearrange("(j p) d -> p j d", p=P)

        with nc.Block() as block:

            @block.sync
            def _(sp):
                def load(g, u, m):
                    sp.dma_start(x[u][:, 2 * m:2 * m + 2, :], half(src, g, m)).then_inc(x_loaded[u][m], 16)

                for u in range(2):
                    sp.sem_inc(h_stored[u], 16)
                    sp.sem_inc(y_stored[u], 16)
                    for m in range(2):
                        load(u, u, m)
                sp.wait_ge(h_ready, 1)
                sp.dma_start(group(htab, 0)[:, :, 0:D], h[0][:, :, :]).then_inc(h_stored[0], 16)

                def body(i, u, ahead=True, load_next=True):
                    g = 2 * i + u
                    if ahead:
                        sp.wait_ge(h_ready, g + 2)
                        sp.dma_start(group(htab, g + 1)[:, :, 0:D], h[1 - u][:, :, :]).then_inc(h_stored[1 - u], 16)
                    for m in range(2):
                        sp.wait_ge(y_done, 4 * g + 2 * m + 2 + 2)
                        if load_next:
                            load(g + 2, u, m)
                    sp.dma_start(group(acc, g), y[u][:, :, :]).then_inc(y_stored[u], 16)

                with sp.Fori(0, last) as i:
                    body(i, 0)
                    body(i, 1)
                body(last, 0, load_next=False)
                body(last, 1, ahead=False, load_next=False)
                for u in range(2):
                    sp.wait_ge(h_stored[u], 16 * (G // 2 + 1))
                    sp.wait_ge(y_stored[u], 16 * (G // 2 + 1))

            @block.scalar
            def _(act):
                def root(g, u):
                    act.wait_ge(stats_ready, g + 1)
                    act.activation(std[u][:, :], mv[u][:, :, 1], ACT.Sqrt, bias=k.ln_eps[:, :]).then_inc(std_ready, 1)

                def turn(g, u):
                    for c in range(KB):
                        act.wait_ge(t_ready, 4 * g + c + 1)
                        act.activation(ht_hi[u][:, c, :], ps_t[c % 2][:, :], ACT.Copy).then_inc(t_hi, 1)
                    act.wait_ge(lg_ready, g + 1)
                    act.activation(lg_t[:, :], ps_t[0][0:3 * E, :], ACT.Copy).then_inc(lg_out, 1)

                def inner(g, u, b):
                    act.wait_ge(gu_ready, 2 * g + b + 1)
                    act.activation(silu[b][:, :], ps_gate[b][:, :], ACT.Silu).then_inc(silu_ready, 1)
                    act.wait_ge(mul_ready, 2 * g + b + 1 + 2)
                    act.activation(in_hi[u][:, b, :], inter[b][:, :], ACT.Copy).then_inc(ihi_ready, 1)

                def body(i, u, ahead=True):
                    g = 2 * i + u
                    inner(g, u, 0)
                    if ahead:
                        root(g + 1, 1 - u)
                    inner(g, u, 1)
                    if ahead:
                        turn(g + 1, 1 - u)

                root(0, 0)
                turn(0, 0)
                with act.Fori(0, last) as i:
                    body(i, 0)
                    body(i, 1)
                body(last, 0)
                body(last, 1, ahead=False)

            @block.vector
            def _(dve):
                dve.sem_inc(t_lo, 2)
                dve.sem_inc(mul_ready, 2)
                dve.sem_inc(y_done, 2)

                def take_stats(i, u):
                    for m in range(2):
                        dve.wait_ge(x_loaded[u][m], 16 * i + 16)
                        for j in (2 * m, 2 * m + 1):
                            dve.bn_stats(stats[:, j, :], x[u][:, j, :])
                    dve.drain()
                    for j in range(GT):
                        got = dve.bn_aggr(mv[u][:, j, :], stats[:, j, :])
                    got.then_inc(stats_ready, 1)

                def normalise(i, u):
                    dve.wait_ge(std_ready, 2 * i + u + 1)
                    dve.reciprocal(rstd[u][:, :], std[u][:, :])
                    dve.drain()
                    dve.wait_ge(h_stored[u], 16 * i + 16)
                    for j in range(GT):
                        got = dve.tensor_scalar(h[u][:, j, :], x[u][:, j, :], mv[u][:, j, 0:1],
                                                rstd[u][:, j:j + 1], ALU.subtract, ALU.mult)
                    got.then_inc(h_ready, 1)

                def turn(g, u):
                    for c in range(KB):
                        dve.wait_ge(t_hi, 4 * g + c + 1)
                        dve.tensor_tensor(ht_lo[u][:, c, :], ps_t[c % 2][:, :], ht_hi[u][:, c, :].bitcast(F32),
                                          ALU.subtract).then_inc(t_lo, 1)

                def take_logits(g):
                    dve.wait_ge(lg_turned, g + 1)
                    dve.tensor_scalar(logits[:, bass.ds(g * GT, GT), :],
                                      ps_t[1][:, 0:GT * 3 * E].rearrange("p (j c) -> p j c", j=GT)[:, :, 0:2 * E],
                                      1.0, None, ALU.mult).then_inc(lg_taken, 1)

                def inner(g, u, b):
                    dve.wait_ge(silu_ready, 2 * g + b + 1)
                    dve.tensor_tensor(inter[b][:, :], silu[b][:, :], ps_up[b][:, :], ALU.mult)
                    dve.drain()
                    dve.tensor_scalar(inter[b][:, :], inter[b][:, :], SWIGLU_LIMIT, -SWIGLU_LIMIT,
                                      ALU.min, ALU.max).then_inc(mul_ready, 1)
                    dve.wait_ge(ihi_ready, 2 * g + b + 1)
                    dve.tensor_tensor(in_lo[u][:, b, :], inter[b][:, :], in_hi[u][:, b, :].bitcast(F32),
                                      ALU.subtract).then_inc(ilo_ready, 1)

                def body(i, u, ahead=True):
                    g = 2 * i + u
                    if ahead:
                        take_stats(i + u, 1 - u)
                    inner(g, u, 0)
                    if ahead:
                        normalise(i + u, 1 - u)
                    take_logits(g)
                    inner(g, u, 1)
                    dve.wait_ge(y_stored[u], 16 * i + 16)

                    def add_residual(j):
                        dve.wait_ge(d_ready, 4 * g + j + 1)
                        dve.scalar_tensor_tensor(y[u][:, j, :], ps_down[j % 2][:, :], 0.5, x[u][:, j, :],
                                                 ALU.mult, ALU.add).then_inc(y_done, 1)

                    for j in range(GT):
                        if ahead:
                            dve.wait_ge(t_hi, 4 * g + 4 + j + 1)
                            dve.tensor_tensor(ht_lo[1 - u][:, j, :], ps_t[j % 2][:, :],
                                              ht_hi[1 - u][:, j, :].bitcast(F32), ALU.subtract).then_inc(t_lo, 1)
                        if j:
                            add_residual(j - 1)
                    add_residual(GT - 1)

                take_stats(0, 0)
                normalise(0, 0)
                turn(0, 0)
                with dve.Fori(0, last) as i:
                    body(i, 0)
                    body(i, 1)
                body(last, 0)
                body(last, 1, ahead=False)

            @block.tensor
            def _(pe):
                def turn(g, u, c):
                    pe.wait_ge(t_lo, 4 * g + c + 1)
                    for j in range(GT):
                        got = pe.transpose(ps_t[c % 2][:, j * P:(j + 1) * P], h[u][:, j, c * P:(c + 1) * P],
                                           k.ident[:, :])
                    got.then_inc(t_ready, 1)

                def router(g, u):
                    pe.wait_ge(t_lo, 4 * g + 4 + 2)
                    for c in range(KB):
                        for part, ht in enumerate((ht_hi, ht_lo)):
                            got = pe.matmul(ps_t[0][0:3 * E, :], k.router[:, c, :, :].rearrange("p s e -> p (s e)"),
                                            ht[u][:, c, :], start=(c == 0 and part == 0),
                                            stop=(c == KB - 1 and part == 1))
                    got.then_inc(lg_ready, 1)

                def turn_logits(g):
                    pe.wait_ge(lg_out, g + 1)
                    for j in range(GT):
                        got = pe.transpose(ps_t[1][:, j * 3 * E:(j + 1) * 3 * E], lg_t[:, j * P:(j + 1) * P],
                                           k.ident[0:3 * E, 0:3 * E])
                    got.then_inc(lg_turned, 1)

                def gate_up(g, u, b):
                    pe.wait_ge(mul_ready, 2 * g + b + 1)
                    for bank, at in ((ps_gate[b], b * P), (ps_up[b], FF + b * P)):
                        for c in range(KB):
                            got = split_products(pe, bank[:, :], (gu_hi[:, c, at:at + P], gu_lo[:, c, at:at + P]),
                                                 (ht_hi[u][:, c, :], ht_lo[u][:, c, :]), c == 0, c == KB - 1)
                    got.then_inc(gu_ready, 1)

                def down(g, u, j, b):
                    pe.wait_ge(ilo_ready, 2 * g + b + 1)
                    if b == 0:
                        pe.wait_ge(y_done, 4 * g + j + 1)
                    tok = slice(j * P, (j + 1) * P)
                    got = split_products(pe, ps_down[j % 2][:, :], (in_hi[u][:, b, tok], in_lo[u][:, b, tok]),
                                         (dn_hi[:, b, :], dn_lo[:, b, :]), b == 0, b == FB - 1)
                    if b == FB - 1:
                        got.then_inc(d_ready, 1)

                def body(i, u, ahead=True):
                    g = 2 * i + u
                    gate_up(g, u, 0)
                    turn_logits(g)
                    gate_up(g, u, 1)
                    if ahead:
                        pe.wait_ge(h_ready, g + 2)
                        pe.wait_ge(lg_taken, g + 1)
                        turn(g + 1, 1 - u, 0)
                        turn(g + 1, 1 - u, 1)
                    down(g, u, 0, 0)
                    down(g, u, 1, 0)
                    for j in range(2):
                        down(g, u, j, 1)
                        if ahead:
                            turn(g + 1, 1 - u, j + 2)
                    for j in range(2, GT):
                        for b in range(FB):
                            down(g, u, j, b)
                    if ahead:
                        router(g + 1, 1 - u)

                pe.wait_ge(h_ready, 1)
                for c in range(KB):
                    turn(0, 0, c)
                router(0, 0)
                with pe.Fori(0, last) as i:
                    body(i, 0)
                    body(i, 1)
                body(last, 0)
                body(last, 1, ahead=False)


def route(nc, a, k, n, htab, logits, slot_dram, slots):
    with ExitStack() as ctx:
        sb = lambda name, shape, dt: ctx.enter_context(nc.sbuf_tensor(f"{name}{n}", shape, dt))
        pb = lambda name: ctx.enter_context(nc.psum_tensor(f"{name}{n}", [P, 512], F32))
        sem = lambda name: own_semaphore(nc, k, f"{name}{n}")
        wide = [P, NT, E]
        t1, t2, t3, t4, t5 = (sb(f"r_t{i}_", wide, F32) for i in range(1, 6))
        score = sb("r_score", wide, F32)
        small = sb("r_small", wide, U32)
        seg = sb("r_seg", wide, F32)
        mask = sb("r_mask", wide, F32)
        mask_bf = sb("r_mask_bf", wide, BF16)
        bias = sb("r_bias", [P, E], F32)
        top8 = sb("r_top8", [P, NT, 8], F32)
        per_tok = sb("r_per_tok", [P, NT], F32)
        code = sb("r_code", wide, I32)
        code_a = sb("r_code_a", wide, I32)
        code_b = sb("r_code_b", wide, I32)
        slot_a = sb("r_slot_a", wide, F32)
        slot_b = sb("r_slot_b", wide, F32)
        iota_a = sb("r_iota_a", [P, SA], F32)
        iota_b = sb("r_iota_b", [P, SB_], F32)
        tok_id = sb("r_tok_id", [P, NT], F32)
        diag = sb("r_diag", [EG * SA, EG, SB_], F32)
        dump = sb("r_dump", [HALF, 1], F32)
        hot_a = [sb(f"r_hot_a{u}_", [P, E, SA], F32) for u in range(2)]
        id_a = [sb(f"r_id_a{u}_", [P, E * SA], F32R) for u in range(2)]
        hot_b = [sb(f"r_hot_b{u}_", [P, E * SB_], F32R) for u in range(2)]
        picked = sb("r_picked", [EG * SA, E // EG, EG, SB_], F32)
        table = sb("r_table", [EG * SA, E // EG, SB_], F32)
        table2 = sb("r_table2", [EG * SA, E // EG, SB_], F32)
        rows = sb("r_rows", [2 * E, HALF], F32)
        idx = sb("r_idx", [HALF, 2 * E], F32)
        off = sb("r_off", [HALF, 2 * E], F32)
        ps_cum = [pb(f"r_ps_cum{i}_") for i in range(2)]
        ps_tot = [pb(f"r_ps_tot{i}_") for i in range(2)]
        ps_tab = [pb(f"r_ps_tab{i}_") for i in range(E // EG)]
        loaded, w_stored, t_stored, t_read = sem("r_loaded"), sem("r_w_stored"), sem("r_t_stored"), sem("r_t_read")
        lg_sum, exp_done, poly, ln_done = sem("r_lg_sum"), sem("r_exp"), sem("r_poly"), sem("r_ln")
        sp_done, score_done, mask_done, w_done = sem("r_sp"), sem("r_score_d"), sem("r_mask_d"), sem("r_w")
        counted, code_done = sem("r_counted"), sem("r_code_d")
        hots, ida, tabbed, tab_done = sem("r_hots"), sem("r_ida"), sem("r_tabbed"), sem("r_tab")
        turned = sem("r_turned")
        flat = lambda t: t[:, :, :].rearrange("p t e -> p (t e)")
        per_token = lambda ap: ap.rearrange("p (t o) -> p t o", o=1).to_broadcast(wide)

        with nc.Block() as block:

            @block.sync
            def _(sp):
                for dst, src in ((bias[:, :], a["bias"]), (seg[:, :, :], a["seg"]), (iota_a[:, :], a["iota_a"]),
                                 (iota_b[:, :], a["iota_b"]), (tok_id[:, :], a["tok_id"]),
                                 (diag[:, :, :], a["diag"]), (dump[:, :], a["dump"])):
                    sp.dma_start(dst, src).then_inc(loaded, 16)
                sp.wait_ge(w_done, 1)
                with nc.allow_non_contiguous_dma(reason="32 weights behind each row of tokens"):
                    sp.dma_start(htab[0:TOK, D:ROW].rearrange("(t p) e -> p t e", p=P), t1[:, :, :]).then_inc(w_stored, 16)
                sp.wait_ge(tab_done, 1)
                sp.dma_start(slot_dram.rearrange("(g r b) -> r g b", g=E // EG, b=SB_), table2[:, :, :]).then_inc(t_stored, 16)
                sp.wait_ge(t_stored, 16)
                sp.dma_start(rows[:, :], slot_dram.rearrange("(q s) -> q s", s=HALF)).then_inc(t_read, 16)
                sp.wait_ge(w_stored, 16)

            @block.scalar
            def _(act):
                act.wait_ge(lg_sum, 1)
                act.activation(t2[:, :, :], t1[:, :, :], ACT.Abs)
                act.drain()
                act.activation(t3[:, :, :], t2[:, :, :], ACT.Exp, scale=-1.0).then_inc(exp_done, 1)
                act.drain()
                act.activation(t4[:, :, :], t3[:, :, :], ACT.Ln, bias=1.0).then_inc(ln_done, 1)
                act.wait_ge(sp_done, 1)
                act.activation(score[:, :, :], t5[:, :, :], ACT.Sqrt).then_inc(score_done, 1)
                act.wait_ge(w_done, 1)
                with act.Fori(0, NT // 2) as i:
                    for u in range(2):
                        act.wait_ge(hots, 2 * i + u + 1)
                        act.wait_ge(tabbed, 2 * i + u + 1)
                        act.activation(id_a[u][:, :], hot_a[u][:, :, :].rearrange("p e s -> p (e s)"), ACT.Copy,
                                       scale=tok_id[:, bass.ds(2 * i + u, 1)]).then_inc(ida, 1)

            @block.vector
            def _(dve):
                dve.tensor_tensor(t1[:, :, :], logits[:, :, 0:E], logits[:, :, E:2 * E], ALU.add).then_inc(lg_sum, 1)
                dve.wait_ge(exp_done, 1)
                dve.tensor_scalar(t5[:, :, :], t3[:, :, :], 1.0 / 3.0, -0.5, ALU.mult, ALU.add)
                dve.tensor_scalar(small[:, :, :], t3[:, :, :], 0.01, None, ALU.is_lt)
                dve.drain()
                dve.tensor_tensor(t2[:, :, :], t5[:, :, :], t3[:, :, :], ALU.mult)
                dve.drain()
                dve.scalar_tensor_tensor(t5[:, :, :], t2[:, :, :], 1.0, t3[:, :, :], ALU.add, ALU.mult)
                dve.wait_ge(ln_done, 1)
                dve.drain()
                dve.copy_predicated(flat(t4), flat(small), flat(t5))
                dve.drain()
                dve.scalar_tensor_tensor(t5[:, :, :], t1[:, :, :], 0.0, t4[:, :, :], ALU.max, ALU.add).then_inc(sp_done, 1)
                dve.wait_ge(score_done, 1)
                dve.wait_ge(loaded, 16 * 7)
                dve.tensor_tensor(t1[:, :, :], score[:, :, :],
                                  bias[:, :].rearrange("p (o e) -> p o e", o=1).to_broadcast(wide), ALU.add)
                dve.drain()
                for t in range(NT):
                    dve.max(top8[:, t, :], t1[:, t, :])
                dve.drain()
                sixth = top8[:, :, TOPK - 1:TOPK].to_broadcast(wide)
                dve.tensor_tensor(t2[:, :, :], t1[:, :, :], sixth, ALU.is_gt)
                dve.tensor_tensor(t3[:, :, :], t1[:, :, :], sixth, ALU.is_equal)
                dve.drain()
                dve.tensor_reduce(per_tok[:, :], t2[:, :, :], AX.X, ALU.add)
                dve.tensor_tensor_scan(flat(t4), flat(seg), flat(t3), 0.0, ALU.mult, ALU.add)
                dve.drain()
                dve.tensor_tensor(t5[:, :, :], t4[:, :, :], per_token(per_tok[:, :]), ALU.add)
                dve.drain()
                dve.scalar_tensor_tensor(t4[:, :, :], t5[:, :, :], float(TOPK), t3[:, :, :], ALU.is_le, ALU.mult)
                dve.drain()
                dve.tensor_tensor(mask[:, :, :], t4[:, :, :], t2[:, :, :], ALU.add)
                dve.drain()
                dve.tensor_copy(mask_bf[:, :, :], mask[:, :, :]).then_inc(mask_done, 1)
                dve.tensor_tensor(t1[:, :, :], score[:, :, :], mask[:, :, :], ALU.mult)
                dve.drain()
                dve.tensor_reduce(per_tok[:, :], t1[:, :, :], AX.X, ALU.add)
                dve.drain()
                dve.reciprocal(top8[:, :, 0:1].rearrange("p t o -> p (t o)"), per_tok[:, :])
                dve.drain()
                dve.scalar_tensor_tensor(t1[:, :, :], t1[:, :, :], ROUTE_SCALE * 0.5,
                                         top8[:, :, 0:1].to_broadcast(wide), ALU.mult, ALU.mult).then_inc(w_done, 1)
                dve.wait_ge(counted, 1)
                by_expert = lambda t: flat(t).rearrange("p (e t) -> p e t", t=NT)
                for i in range(2):
                    dve.tensor_copy(by_expert(t2)[:, :, i * NT // 2:(i + 1) * NT // 2],
                                    ps_tot[i][:, :].rearrange("p (t e) -> p e t", e=E))
                dve.drain()
                dve.tensor_tensor_scan(flat(t3), flat(seg), flat(t2), 0.0, ALU.mult, ALU.add)
                dve.drain()
                dve.tensor_tensor(t4[:, :, :], t3[:, :, :], t2[:, :, :], ALU.subtract)
                dve.drain()
                for i in range(2):
                    dve.tensor_tensor(t5[:, i * NT // 2:(i + 1) * NT // 2, :],
                                      ps_cum[i][:, :].rearrange("p (t e) -> p t e", e=E),
                                      by_expert(t4)[:, :, i * NT // 2:(i + 1) * NT // 2].rearrange("p e t -> p t e"),
                                      ALU.add)
                dve.drain()
                dve.scalar_tensor_tensor(t2[:, :, :], t5[:, :, :], float(CAP), mask[:, :, :], ALU.is_le, ALU.mult)
                dve.drain()
                dve.scalar_tensor_tensor(t3[:, :, :], t5[:, :, :], -1.0 - NO_SLOT, t2[:, :, :], ALU.add, ALU.mult)
                dve.drain()
                dve.tensor_scalar(code[:, :, :], t3[:, :, :], NO_SLOT, None, ALU.add)
                dve.drain()
                dve.tensor_scalar(code_a[:, :, :], code[:, :, :], 4, None, ALU.arith_shift_right)
                dve.tensor_scalar(code_b[:, :, :], code[:, :, :], SB_ - 1, None, ALU.bitwise_and)
                dve.drain()
                dve.tensor_copy(slot_a[:, :, :], code_a[:, :, :])
                dve.tensor_copy(slot_b[:, :, :], code_b[:, :, :])
                dve.drain()
                with dve.Fori(0, NT // 2) as i:
                    for u in range(2):
                        t = 2 * i + u
                        dve.wait_ge(tabbed, 2 * i + u + 1)
                        dve.tensor_tensor(hot_b[u][:, :].rearrange("p (e s) -> p e s", e=E),
                                          slot_b[:, bass.ds(t, 1), :].rearrange("p o e -> p e o").to_broadcast([P, E, SB_]),
                                          iota_b[:, :].rearrange("p (o s) -> p o s", o=1).to_broadcast([P, E, SB_]),
                                          ALU.is_equal)
                        dve.tensor_tensor(hot_a[u][:, :, :],
                                          slot_a[:, bass.ds(t, 1), :].rearrange("p o e -> p e o").to_broadcast([P, E, SA]),
                                          iota_a[:, :].rearrange("p (o s) -> p o s", o=1).to_broadcast([P, E, SA]),
                                          ALU.is_equal).then_inc(hots, 1)
                dve.wait_ge(tabbed, NT + 2)
                for g in range(E // EG):
                    dve.tensor_tensor(picked[:, g, :, :], ps_tab[g][0:EG * SA, 0:EG * SB_].rearrange("p (e s) -> p e s", e=EG),
                                      diag[:, :, :], ALU.mult)
                dve.drain()
                for g in range(E // EG):
                    dve.tensor_reduce(table[:, g, :], picked[:, g, :, :].rearrange("p e s -> p s e"), AX.X, ALU.add)
                dve.drain()
                dve.tensor_scalar(table2[:, :, :], table[:, :, :], float(DUMP), None, ALU.add).then_inc(tab_done, 1)
                dve.wait_ge(turned, 1)
                dve.tensor_copy(idx[:, :], ps_cum[0][0:HALF, 0:2 * E])
                dve.drain()
                dve.tensor_scalar(off[:, :], idx[:, :], float(DUMP), dump[:, :], ALU.is_ge, ALU.mult)
                dve.drain()
                dve.tensor_tensor(slots[:, :], idx[:, :], off[:, :], ALU.add)

            @block.tensor
            def _(pe):
                pe.wait_ge(mask_done, 1)
                for i in range(2):
                    cols = flat(mask_bf)[:, i * 512:(i + 1) * 512]
                    pe.matmul(ps_cum[i][:, :], k.upto_bf[:, :], cols, start=True, stop=True)
                    got = pe.matmul(ps_tot[i][:, :], k.ones_bf[:, :], cols, start=True, stop=True)
                got.then_inc(counted, 1)
                pe.sem_inc(tabbed, 2)

                def body(i, u, first=False, last=False):
                    pe.wait_ge(ida, 2 * i + u + 1)
                    for g in range(E // EG):
                        got = pe.matmul(ps_tab[g][0:EG * SA, 0:EG * SB_], id_a[u][:, g * EG * SA:(g + 1) * EG * SA],
                                        hot_b[u][:, g * EG * SB_:(g + 1) * EG * SB_], start=first, stop=last)
                    got.then_inc(tabbed, 1)

                body(0, 0, first=True)
                body(0, 1)
                with pe.Fori(1, NT // 2 - 1) as i:
                    body(i, 0)
                    body(i, 1)
                body(NT // 2 - 1, 0)
                body(NT // 2 - 1, 1, last=True)
                pe.wait_ge(t_read, 16)
                pe.transpose(ps_cum[0][0:HALF, 0:2 * E], rows[:, :], k.ident[0:2 * E, 0:2 * E]).then_inc(turned, 1)


def routed_experts(nc, a, k, n, htab, acc, slots):
    with ExitStack() as ctx:
        sb = lambda name, shape, dt: ctx.enter_context(nc.sbuf_tensor(f"{name}{n}", shape, dt))
        pb = lambda name: ctx.enter_context(nc.psum_tensor(f"{name}{n}", [P, 512], F32))
        sem = lambda name: own_semaphore(nc, k, f"{name}{n}")
        raw = [sb(f"e_raw{u}_", [P, WALL], F32) for u in range(2)]
        w_hi = [sb(f"e_w_hi{u}_", [P, WALL], F32R) for u in range(2)]
        w_lo = [sb(f"e_w_lo{u}_", [P, WALL], F32R) for u in range(2)]
        gather_idx = [[sb(f"e_gather_idx{u}{q}_", [HALF, 1], U32) for q in range(2)] for u in range(2)]
        add_idx = [[sb(f"e_add_idx{u}{q}_", [HALF, 1], U32) for q in range(2)] for u in range(2)]
        xg = [[sb(f"e_xg{u}{q}_", [HALF, ROW], F32) for q in range(2)] for u in range(2)]
        xt_hi = [sb(f"e_xt_hi{u}_", [P, KB, CAP], F32R) for u in range(2)]
        xt_lo = [sb(f"e_xt_lo{u}_", [P, KB, CAP], F32R) for u in range(2)]
        wcol = sb("e_wcol", [HALF, 2 * E], F32)
        silu = sb("e_silu", [HALF, 2, FF], F32)
        inter = sb("e_inter", [HALF, 2, FF], F32)
        in_hi = sb("e_in_hi", [P, FB * CAP], F32R)
        in_lo = sb("e_in_lo", [P, FB * CAP], F32R)
        y = [[sb(f"e_y{u}{q}_", [HALF, D], F32) for q in range(2)] for u in range(2)]
        ps_t = [pb(f"e_ps_t{i}_") for i in range(2)]
        ps_gu = [pb(f"e_ps_gu{q}_") for q in range(2)]
        ps_in = pb("e_ps_in")
        ps_down = [pb(f"e_ps_down{q}_") for q in range(2)]
        w_loaded = [sem(f"e_w_loaded{u}_") for u in range(2)]
        gathered = [sem(f"e_gathered{u}_") for u in range(2)]
        added, y_free = sem("e_added"), sem("e_y_free")
        hi_ready, lo_ready = sem("e_hi_ready"), sem("e_lo_ready")
        t_ready, t_hi, t_lo, col_done = sem("e_t_ready"), sem("e_t_hi"), sem("e_t_lo"), sem("e_col_done")
        gu_ready, silu_ready, mul_ready = sem("e_gu_ready"), sem("e_silu_ready"), sem("e_mul_ready")
        in_turned, ihi_ready, ilo_ready = sem("e_in_turned"), sem("e_ihi_ready"), sem("e_ilo_ready")
        d_ready, y_ready = sem("e_d_ready"), sem("e_y_ready")
        TC = 2 * CAP
        THIRD = WALL // 3

        with nc.Block() as block:

            @block.sync
            def _(sp):
                for u in range(2):
                    sp.dma_start(raw[u][:, :], a["w_experts"][u, :, :]).then_inc(w_loaded[u], 16)
                with sp.Fori(0, E // 2 - 1) as i:
                    for u in range(2):
                        e = 2 * i + u
                        sp.wait_ge(lo_ready, 3 * e + 3)
                        sp.dma_start(raw[u][:, :], a["w_experts"][bass.ds(e + 2, 1), :, :].rearrange("o p c -> p (o c)")).then_inc(w_loaded[u], 16)

            @block.gpsimd
            def _(pool):
                pool.sem_inc(y_free, 2)

                def gather(i, u):
                    e = 2 * i + u
                    for q in range(2):
                        pool.tensor_copy(gather_idx[u][q][:, :], slots[:, bass.ds(2 * e + q, 1)])
                    pool.drain()
                    for q in range(2):
                        pool.indirect_dma_start(xg[u][q][:, :], None, htab,
                                                bass.IndirectOffsetOnAxis(ap=gather_idx[u][q][:, 0:1], axis=0)).then_inc(gathered[u], 16)

                def scatter(i, u):
                    e = 2 * i + u
                    pool.wait_ge(y_ready, 2 * e + 2 + 2)
                    for q in range(2):
                        pool.tensor_copy(add_idx[u][q][:, :], slots[:, bass.ds(2 * e + q, 1)])
                    pool.drain()
                    for q in range(2):
                        pool.indirect_dma_start(acc, bass.IndirectOffsetOnAxis(ap=add_idx[u][q][:, 0:1], axis=0),
                                                y[u][q][:, :], None, compute_op=ALU.add).then_inc(added, 16)
                    pool.wait_ge(added, 32 * e + 32)
                    pool.sem_inc(y_free, 1)

                def step(i, u):
                    pool.wait_ge(col_done, 2 * i + u + 1)
                    gather(i + 1, u)
                    if u == 1:
                        scatter(i, 0)
                    else:
                        scatter(i - 1, 1)

                gather(0, 0)
                gather(0, 1)
                pool.wait_ge(col_done, 1)
                gather(1, 0)
                with pool.Fori(0, E // 2 - 2) as i:
                    step(i, 1)
                    step(i + 1, 0)
                step(E // 2 - 2, 1)
                scatter(E // 2 - 2, 1)
                scatter(E // 2 - 1, 0)
                scatter(E // 2 - 1, 1)

            @block.scalar
            def _(act):
                act.sem_inc(y_ready, 2)

                def split(i, u, thirds):
                    act.wait_ge(w_loaded[u], 16 * i + 16)
                    for c in thirds:
                        cols = slice(c * THIRD, (c + 1) * THIRD)
                        act.activation(w_hi[u][:, cols], raw[u][:, cols], ACT.Copy).then_inc(hi_ready, 1)

                def turn(i, u):
                    e = 2 * i + u
                    for c in range(2):
                        act.wait_ge(t_ready, 2 * e + c + 1)
                        act.activation(xt_hi[u][:, 2 * c:2 * c + 2, :].rearrange("p k s -> p (k s)"),
                                       ps_t[c][:, 0:TC], ACT.Copy).then_inc(t_hi, 1)

                def gate(i, u):
                    e = 2 * i + u
                    for q in range(2):
                        act.wait_ge(gu_ready, 2 * e + q + 1)
                        act.activation(silu[:, q, :], ps_gu[q][0:HALF, 0:FF], ACT.Silu).then_inc(silu_ready, 1)

                def turn_inner(i, u):
                    act.wait_ge(in_turned, 2 * i + u + 1)
                    act.activation(in_hi[:, :], ps_in[:, 0:FB * CAP], ACT.Copy).then_inc(ihi_ready, 1)

                def weigh(i, u):
                    e = 2 * i + u
                    act.wait_ge(y_free, e + 1)
                    act.wait_ge(col_done, e + 1)
                    for q in range(2):
                        act.wait_ge(d_ready, 2 * e + q + 1)
                        act.activation(y[u][q][:, :], ps_down[q][0:HALF, :], ACT.Copy,
                                       scale=wcol[:, bass.ds(2 * e + q, 1)]).then_inc(y_ready, 1)

                def step(i, u, ahead=True, behind=True):
                    ni, nu = (i, 1) if u == 0 else (i + 1, 0)
                    pi = i if u == 1 else i - 1
                    if behind:
                        turn_inner(pi, nu)
                    if ahead:
                        turn(ni, nu)
                        split(ni, nu, (0, 1))
                    gate(i, u)
                    if behind:
                        weigh(pi, nu)
                    if ahead:
                        split(ni, nu, (2,))

                turn(0, 0)
                split(0, 0, (0, 1, 2))
                step(0, 0, behind=False)
                with act.Fori(0, E // 2 - 1) as i:
                    step(i, 1)
                    step(i + 1, 0)
                step(E // 2 - 1, 1, ahead=False)
                turn_inner(E // 2 - 1, 1)
                weigh(E // 2 - 1, 1)

            @block.vector
            def _(dve):
                dve.sem_inc(t_lo, 2)
                dve.sem_inc(mul_ready, 2)
                dve.sem_inc(ilo_ready, 1)

                def split(i, u, thirds):
                    e = 2 * i + u
                    for c in thirds:
                        cols = slice(c * THIRD, (c + 1) * THIRD)
                        dve.wait_ge(hi_ready, 3 * e + c + 1)
                        dve.tensor_tensor(w_lo[u][:, cols], raw[u][:, cols], w_hi[u][:, cols].bitcast(F32),
                                          ALU.subtract).then_inc(lo_ready, 1)

                def turn(i, u):
                    e = 2 * i + u
                    for c in range(2):
                        dve.wait_ge(t_hi, 2 * e + c + 1)
                        dve.tensor_tensor(xt_lo[u][:, 2 * c:2 * c + 2, :].rearrange("p k s -> p (k s)"), ps_t[c][:, 0:TC],
                                          xt_hi[u][:, 2 * c:2 * c + 2, :].rearrange("p k s -> p (k s)").bitcast(F32),
                                          ALU.subtract).then_inc(t_lo, 1)
                    for q in range(2):
                        got = dve.tensor_scalar(wcol[:, bass.ds(2 * e + q, 1)], xg[u][q][:, bass.ds(D + e, 1)],
                                                1.0, None, ALU.mult)
                    got.then_inc(col_done, 1)

                def gate(i, u):
                    e = 2 * i + u
                    for q in range(2):
                        dve.wait_ge(silu_ready, 2 * e + q + 1)
                        dve.tensor_tensor(inter[:, q, :], silu[:, q, :], ps_gu[q][0:HALF, FF:2 * FF],
                                          ALU.mult).then_inc(mul_ready, 1)

                def turn_inner(i, u):
                    dve.wait_ge(ihi_ready, 2 * i + u + 1)
                    dve.tensor_tensor(in_lo[:, :], ps_in[:, 0:FB * CAP], in_hi[:, :].bitcast(F32),
                                      ALU.subtract).then_inc(ilo_ready, 1)

                def step(i, u, ahead=True, behind=True):
                    ni, nu = (i, 1) if u == 0 else (i + 1, 0)
                    if behind:
                        turn_inner(i if u == 1 else i - 1, nu)
                    if ahead:
                        turn(ni, nu)
                        split(ni, nu, (0, 1))
                    gate(i, u)
                    if ahead:
                        split(ni, nu, (2,))

                turn(0, 0)
                split(0, 0, (0, 1, 2))
                step(0, 0, behind=False)
                with dve.Fori(0, E // 2 - 1) as i:
                    step(i, 1)
                    step(i + 1, 0)
                step(E // 2 - 1, 1, ahead=False)
                turn_inner(E // 2 - 1, 1)

            @block.tensor
            def _(pe):
                def turn(i, u):
                    e = 2 * i + u
                    pe.wait_ge(gathered[u], 32 * i + 32)
                    for c in range(2):
                        pe.wait_ge(t_lo, 2 * e + c + 1)
                        for b in range(2):
                            for q in range(2):
                                at = b * CAP + q * HALF
                                got = pe.transpose(ps_t[c][:, at:at + HALF],
                                                   xg[u][q][:, (2 * c + b) * P:(2 * c + b + 1) * P],
                                                   k.ident[0:HALF, 0:HALF])
                        got.then_inc(t_ready, 1)

                def gate_up(i, u):
                    e = 2 * i + u
                    w = [t[u][:, 0:WGU].rearrange("p (k c) -> p k c", k=KB) for t in (w_hi, w_lo)]
                    pe.wait_ge(t_lo, 2 * e + 2 + 2)
                    pe.wait_ge(lo_ready, 3 * e + 2)
                    for q in range(2):
                        pe.wait_ge(mul_ready, 2 * e + q + 1)
                        s = slice(q * HALF, (q + 1) * HALF)
                        for c in range(KB):
                            got = split_products(pe, ps_gu[q][0:HALF, :], (xt_hi[u][:, c, s], xt_lo[u][:, c, s]),
                                                 (w[0][:, c, :], w[1][:, c, :]), c == 0, c == KB - 1)
                        got.then_inc(gu_ready, 1)

                def turn_inner(i, u):
                    e = 2 * i + u
                    pe.wait_ge(mul_ready, 2 * e + 2 + 2)
                    pe.wait_ge(ilo_ready, e + 1)
                    for b in range(FB):
                        for q in range(2):
                            at = b * CAP + q * HALF
                            got = pe.transpose(ps_in[:, at:at + HALF], inter[:, q, b * P:(b + 1) * P],
                                               k.ident[0:HALF, 0:HALF])
                    got.then_inc(in_turned, 1)

                def down(i, u):
                    e = 2 * i + u
                    w = [t[u][:, WGU:].rearrange("p (k c) -> p k c", k=FB) for t in (w_hi, w_lo)]
                    pe.wait_ge(lo_ready, 3 * e + 3)
                    pe.wait_ge(ilo_ready, e + 1 + 1)
                    for q in range(2):
                        pe.wait_ge(y_ready, 2 * e + q + 1)
                        for b in range(FB):
                            s = slice(b * CAP + q * HALF, b * CAP + (q + 1) * HALF)
                            got = split_products(pe, ps_down[q][0:HALF, :], (in_hi[:, s], in_lo[:, s]),
                                                 (w[0][:, b, :], w[1][:, b, :]), b == 0, b == FB - 1)
                        got.then_inc(d_ready, 1)

                turn(0, 0)
                turn(0, 1)
                gate_up(0, 0)
                with pe.Fori(0, E // 2 - 1) as i:
                    for u in range(2):
                        turn_inner(i, u)
                        turn(i + 1, u)
                        gate_up(i if u == 0 else i + 1, 1 - u)
                        down(i, u)
                turn_inner(E // 2 - 1, 0)
                gate_up(E // 2 - 1, 1)
                down(E // 2 - 1, 0)
                turn_inner(E // 2 - 1, 1)
                down(E // 2 - 1, 1)


def attention(nc, a, k, src, dst):
    softmax_scale = DH ** -0.5
    HK = H + 1
    half = DH // 2
    with ExitStack() as ctx:
        sb = lambda name, shape, dt: ctx.enter_context(nc.sbuf_tensor(name, shape, dt))
        sem = lambda name: ctx.enter_context(nc.semaphore(name))
        cos = sb("a_cos", [P, NQ, half], F32)
        sin = sb("a_sin", [P, NQ, DH], F32)
        gains = sb("a_gains", [P, HK, DH], F32)
        qt = [sb(f"a_qt_{part}", [P, H, SEQ], F32R) for part in ("hi", "lo")]
        kt_ = [sb(f"a_kt_{part}", [P, SEQ], F32R) for part in ("hi", "lo")]
        v = [sb(f"a_v_{part}", [P, NQ, DH], F32R) for part in ("hi", "lo")]
        q_scale = sb("a_q_scale", [P, NQ, H], F32)
        x = [sb(f"q_x{u}", [P, D], F32) for u in range(2)]
        h = [sb(f"q_h{u}", [P, D], F32) for u in range(2)]
        stats = [sb(f"q_stats{u}", [P, 6], F32) for u in range(2)]
        mv = [sb(f"q_mv{u}", [P, 2], F32) for u in range(2)]
        std = [sb(f"q_std{u}", [P, 1], F32) for u in range(2)]
        rstd = [sb(f"q_rstd{u}", [P, 1], F32) for u in range(2)]
        ht = [[sb(f"q_ht{part}{u}", [P, KB, P], F32R) for u in range(2)] for part in range(2)]
        raw = sb("q_raw", [P, HK, DH], F32)
        sum_sq = sb("q_sum_sq", [P, HK], F32)
        rms = [sb(f"q_rms{u}", [P, HK], F32) for u in range(2)]
        inv_rms = sb("q_inv_rms", [P, HK], F32)
        gained = sb("q_gained", [P, HK, DH], F32)
        by_cos = sb("q_by_cos", [P, HK, DH], F32)
        by_sin = sb("q_by_sin", [P, HK, DH], F32)
        rot = [sb(f"q_rot{u}", [P, HK, DH], F32) for u in range(2)]
        res = [sb(f"t_res{u}", [P, D], F32) for u in range(2)]
        top, neg_max, total, inv = (sb(f"t_{name}", [P, 2 * H], F32) for name in ("top", "neg_max", "total", "inv"))
        prob = sb("t_prob", [P, RING, SEQ], F32)
        pt = [[sb(f"t_pt{part}{r}", [P, H * P], F32R) for r in range(2)] for part in range(2)]
        ot = [sb(f"t_ot{part}", [P, H * P], F32R) for part in range(2)]
        wide = [ctx.enter_context(nc.psum_tensor(f"a_wide{i}", [P, SEQ], F32)) for i in range(2)]
        bank = [ctx.enter_context(nc.psum_tensor(f"a_bank{i}", [P, 512], F32)) for i in range(4)]
        ps_t = [wide[0][:, 0:512], wide[0][:, 512:1024]]
        ps_q = [wide[1][:, 0:512], bank[0][:, :]]
        ps_kv = [wide[1][:, 512:1024], bank[1][:, :]]
        ps_qt, ps_kt = bank[2][:, :], bank[3][:, :]
        ps_s, ps_p, ps_o, ps_y = wide, [bank[0][:, :], bank[1][:, :]], bank[2][:, :], bank[3][:, :]

        loaded, seen = sem("a_loaded"), sem("a_seen_by_gpsimd")
        x_loaded = [sem(f"a_x_loaded{u}") for u in range(2)]
        stats_ready, std_ready, h_ready = sem("a_stats"), sem("a_std_ready"), sem("a_h_ready")
        t_ready, t_hi, t_lo = sem("a_t_ready"), sem("a_t_hi"), sem("a_t_lo")
        proj_ready, raw_ready, rms_ready = sem("a_proj_ready"), sem("a_raw_ready"), sem("a_rms_ready")
        gained_ready, sin_ready = sem("a_gained_ready"), sem("a_sin_ready")
        rot_ready, qk_turned, qk_hi, qk_lo = sem("a_rot_ready"), sem("a_qk_turned"), sem("a_qk_hi"), sem("a_qk_lo")
        s_ready, m_ready, exp_ready = sem("a_s_ready"), sem("a_m_ready"), sem("a_exp_ready")
        inv_ready, p_ready = sem("a_inv_ready"), sem("a_p_ready")
        p_turned, p_hi, p_lo = sem("a_p_turned"), sem("a_p_hi"), sem("a_p_lo")
        o_ready, o_hi, o_lo = sem("a_o_ready"), sem("a_o_hi"), sem("a_o_lo")
        out_ready, y_done = sem("a_out_ready"), sem("a_y_done")
        r_loaded = [sem(f"a_r_loaded{u}") for u in range(2)]
        y_stored = [sem(f"a_y_stored{u}") for u in range(2)]
        nc.clear_and_free_semaphores(k.ffn_semaphores)
        k.ffn_semaphores = []

        keys = lambda s: s + 1
        base = [s * (s + 1) // 2 for s in range(NQ)]
        width = lambda i: keys(i // H) * P
        quarter = lambda s, m: range(keys(s) * m // H, keys(s) * (m + 1) // H)
        tiles0, heads0, blocks0 = (lambda b: b * NQ), (lambda b: b * HEADS), (lambda b: b * (NQ * (NQ + 1) // 2))

        def over_batches(engine, prepare, body):
            prepare(0)
            with engine.Fori(0, B - 2) as b:
                body(b, True)
            body(B - 2, True)
            body(B - 1, False)

        with nc.Block() as block:

            @block.sync
            def _(sp):
                for t, name in ((cos, "cos"), (sin, "sin"), (gains, "gains")):
                    sp.dma_start(t[:, :, :], a[name]).then_inc(loaded, 16)
                for u in range(2):
                    sp.sem_inc(y_stored[u], 16)

                def load_x(b, j, wait=True):
                    row = sp.snap(b * SEQ + j * P)
                    if wait:
                        sp.wait_ge(h_ready, tiles0(b) + j - 1)
                    sp.dma_start(x[j % 2][:, :], src[bass.ds(row, P), :]).then_inc(x_loaded[j % 2], 16)

                def load_res(b, s):
                    row = sp.snap(b * SEQ + s * P)
                    sp.wait_ge(y_stored[s % 2], b * 16 * (NQ // 2) + 16 * (s // 2) + 16)
                    sp.dma_start(res[s % 2][:, :], src[bass.ds(row, P), :]).then_inc(r_loaded[s % 2], 16)

                def store(b, s):
                    row = sp.snap(b * SEQ + s * P)
                    sp.wait_ge(y_done, tiles0(b) + s + 1 + 1)
                    sp.dma_start(dst[bass.ds(row, P), :], res[s % 2][:, :]).then_inc(y_stored[s % 2], 16)

                def prepare(b):
                    load_x(b, 0, wait=False)
                    load_x(b, 1, wait=False)
                    load_x(b, 2)
                    load_x(b, 3)

                def body(b, ahead):
                    for j in range(4, NQ):
                        load_x(b, j)
                    load_res(b, 0)
                    load_res(b, 1)
                    for s in range(NQ):
                        store(b, s)
                        if s + 2 < NQ:
                            load_res(b, s + 2)
                        if ahead and s == 4:
                            load_x(b + 1, 0)
                            load_x(b + 1, 1)
                        if ahead and s == NQ - 2:
                            load_x(b + 1, 2)
                            load_x(b + 1, 3)

                over_batches(sp, prepare, body)
                for u in range(2):
                    sp.wait_ge(y_stored[u], 16 * (B * NQ // 2 + 1))

            @block.scalar
            def _(act):
                act.sem_inc(exp_ready, 2)

                def root(b, j):
                    act.wait_ge(stats_ready, tiles0(b) + j + 1)
                    act.activation(std[j % 2][:, :], mv[j % 2][:, 1:2], ACT.Sqrt, bias=k.ln_eps[:, :]).then_inc(std_ready, 1)

                def turn(b, j):
                    act.wait_ge(t_ready, tiles0(b) + j + 1)
                    act.activation(ht[0][j % 2][:, :, :].rearrange("p k t -> p (k t)"), ps_t[j % 2],
                                   ACT.Copy).then_inc(t_hi, 1)

                def unload(b, j):
                    act.wait_ge(proj_ready, tiles0(b) + j + 1)
                    act.activation(v[0][:, j, :], ps_kv[j % 2][:, DH:2 * DH], ACT.Copy)
                    act.wait_ge(gained_ready, tiles0(b) + j + 1)
                    act.activation(raw[:, 0:H, :].rearrange("p m d -> p (m d)"), ps_q[j % 2], ACT.Copy)
                    act.activation(raw[:, H, :], ps_kv[j % 2][:, 0:DH], ACT.Copy).then_inc(raw_ready, 1)

                def mean_square(j):
                    act.drain()
                    for m in range(HK):
                        act.activation(rot[j % 2][:, m, :], raw[:, m, :], ACT.Square, accum_out=sum_sq[:, m:m + 1])
                    act.drain()
                    act.activation(rms[j % 2][:, :], sum_sq[:, :], ACT.Sqrt, scale=1.0 / DH,
                                   bias=k.rms_eps[:, :]).then_inc(rms_ready, 1)

                def turn_qk(b, j):
                    act.wait_ge(qk_turned, tiles0(b) + j + 1)
                    tok = slice(j * P, (j + 1) * P)
                    act.activation(qt[0][:, :, tok], ps_qt.rearrange("p (m t) -> p m t", m=H), ACT.Copy)
                    act.activation(kt_[0][:, tok], ps_kt[:, 0:P], ACT.Copy).then_inc(qk_hi, 1)

                def soften(b, i):
                    u = i % (2 * H)
                    act.wait_ge(m_ready, heads0(b) + i + 1)
                    act.activation(prob[:, i % RING, 0:width(i)], ps_s[i % 2][:, 0:width(i)], ACT.Exp,
                                   scale=q_scale[:, i // H, i % H:i % H + 1], bias=neg_max[:, u:u + 1],
                                   accum_out=total[:, u:u + 1]).then_inc(exp_ready, 1)

                def turn_prob(b, s, c):
                    at = base[s] + c
                    act.wait_ge(p_turned, blocks0(b) + at + 1)
                    act.activation(pt[0][at % 2][:, :], ps_p[at % 2], ACT.Copy).then_inc(p_hi, 1)

                def collect(b, s):
                    act.wait_ge(o_ready, tiles0(b) + s + 1)
                    act.activation(ot[0][:, :], ps_o, ACT.Copy).then_inc(o_hi, 1)

                def prepare(b):
                    root(b, 0)
                    root(b, 1)
                    turn(b, 0)
                    turn(b, 1)
                    root(b, 2)

                def body(b, ahead):
                    for j in range(1, NQ + 1):
                        unload(b, j - 1)
                        if j + 1 < NQ:
                            turn(b, j + 1)
                        if j >= 3:
                            turn_qk(b, j - 3)
                        if j + 2 < NQ:
                            root(b, j + 2)
                        mean_square(j - 1)
                    soften(b, 0)
                    soften(b, 1)
                    turn_qk(b, NQ - 2)
                    soften(b, 2)
                    soften(b, 3)
                    turn_qk(b, NQ - 1)
                    soften(b, 4)
                    for s in range(NQ):
                        if s:
                            collect(b, s - 1)
                        for m in range(H):
                            for c in quarter(s, m):
                                turn_prob(b, s, c)
                            if s * H + m + EXP_AHEAD < HEADS:
                                soften(b, s * H + m + EXP_AHEAD)
                            if ahead and s == NQ - 1 and m in (0, 1):
                                root(b + 1, m)
                    if ahead:
                        turn(b + 1, 0)
                        turn(b + 1, 1)
                    collect(b, NQ - 1)
                    if ahead:
                        root(b + 1, 2)

                over_batches(act, prepare, body)

            @block.vector
            def _(dve):
                dve.sem_inc(t_lo, 2)
                dve.sem_inc(rot_ready, 2)
                dve.sem_inc(qk_lo, 1)
                dve.sem_inc(p_lo, 2)
                dve.sem_inc(o_lo, 1)
                dve.sem_inc(y_done, 1)

                def take_stats(b, j):
                    dve.wait_ge(x_loaded[j % 2], b * 16 * (NQ // 2) + 16 * (j // 2) + 16)
                    dve.bn_stats(stats[j % 2][:, :], x[j % 2][:, :])

                def add_stats(j):
                    dve.bn_aggr(mv[j % 2][:, :], stats[j % 2][:, :]).then_inc(stats_ready, 1)

                def invert_std(b, j):
                    dve.wait_ge(std_ready, tiles0(b) + j + 1)
                    dve.reciprocal(rstd[j % 2][:, :], std[j % 2][:, :])

                def normalise(j):
                    dve.tensor_scalar(h[j % 2][:, :], x[j % 2][:, :], mv[j % 2][:, 0:1], rstd[j % 2][:, :],
                                      ALU.subtract, ALU.mult).then_inc(h_ready, 1)

                def turn(b, j):
                    dve.wait_ge(t_hi, tiles0(b) + j + 1)
                    dve.tensor_tensor(ht[1][j % 2][:, :, :].rearrange("p k t -> p (k t)"), ps_t[j % 2],
                                      ht[0][j % 2][:, :, :].rearrange("p k t -> p (k t)").bitcast(F32),
                                      ALU.subtract).then_inc(t_lo, 1)

                def turn_qk(b, j):
                    dve.wait_ge(qk_hi, tiles0(b) + j + 1)
                    tok = slice(j * P, (j + 1) * P)
                    dve.tensor_tensor(qt[1][:, :, tok], ps_qt.rearrange("p (m t) -> p m t", m=H),
                                      qt[0][:, :, tok].bitcast(F32), ALU.subtract)
                    dve.tensor_tensor(kt_[1][:, tok], ps_kt[:, 0:P], kt_[0][:, tok].bitcast(F32),
                                      ALU.subtract).then_inc(qk_lo, 1)

                def window(b, w):
                    j = w - 1
                    if w + 2 < NQ:
                        take_stats(b, w + 2)
                    dve.wait_ge(raw_ready, tiles0(b) + j + 1)
                    dve.tensor_tensor(v[1][:, j, :], ps_kv[j % 2][:, DH:2 * DH], v[0][:, j, :].bitcast(F32), ALU.subtract)
                    if w + 1 < NQ:
                        turn(b, w + 1)
                    if w + 2 < NQ:
                        dve.drain()
                        add_stats(w + 2)
                    if w >= 3:
                        turn_qk(b, w - 3)
                    dve.wait_ge(gained_ready, tiles0(b) + j + 1 + 1)
                    by_half = lambda t, m: t[:, :, :].rearrange("p m (s d) -> p m s d", s=2)[:, :, m, :]
                    for m in range(2):
                        dve.tensor_tensor(by_half(by_cos, m), by_half(gained, m),
                                          cos[:, j:j + 1, :].to_broadcast([P, HK, half]), ALU.mult)
                    if w + 2 < NQ:
                        invert_std(b, w + 2)
                        dve.drain()
                        normalise(w + 2)
                    dve.wait_ge(rms_ready, tiles0(b) + j + 1)
                    dve.reciprocal(inv_rms[:, :], rms[j % 2][:, :])
                    dve.drain()
                    dve.tensor_scalar(q_scale[:, j, :], inv_rms[:, 0:H], softmax_scale, None, ALU.mult)
                    if w == NQ:
                        maximum(b, 0)
                        maximum(b, 1)
                    dve.wait_ge(sin_ready, tiles0(b) + j + 1)
                    dve.tensor_tensor(by_cos[:, H, :], by_cos[:, H, :], by_sin[:, H, :], ALU.add)
                    dve.tensor_tensor(rot[j % 2][:, 0:H, :], by_cos[:, 0:H, :], by_sin[:, 0:H, :], ALU.add)
                    dve.drain()
                    dve.tensor_scalar(rot[j % 2][:, H, :], by_cos[:, H, :], inv_rms[:, H:HK], None,
                                      ALU.mult).then_inc(rot_ready, 1)

                def maximum(b, i):
                    u = i % (2 * H)
                    dve.wait_ge(s_ready, heads0(b) + i + 1)
                    dve.reduce_max(top[:, u:u + 1], ps_s[i % 2][:, 0:width(i)], AX.X)
                    dve.drain()
                    dve.tensor_scalar(neg_max[:, u:u + 1], top[:, u:u + 1], q_scale[:, i // H, i % H:i % H + 1],
                                      -1.0, ALU.mult, ALU.mult).then_inc(m_ready, 1)

                def invert(b, i):
                    u = i % (2 * H)
                    dve.wait_ge(exp_ready, heads0(b) + i + 1 + 2)
                    dve.reciprocal(inv[:, u:u + 1], total[:, u:u + 1]).then_inc(inv_ready, 1)

                def turn_prob(b, s, c):
                    at = base[s] + c
                    dve.wait_ge(p_hi, blocks0(b) + at + 1)
                    dve.tensor_tensor(pt[1][at % 2][:, :], ps_p[at % 2], pt[0][at % 2][:, :].bitcast(F32),
                                      ALU.subtract).then_inc(p_lo, 1)

                def collect(b, s):
                    dve.wait_ge(o_hi, tiles0(b) + s + 1)
                    dve.tensor_tensor(ot[1][:, :], ps_o, ot[0][:, :].bitcast(F32), ALU.subtract).then_inc(o_lo, 1)

                def add_residual(b, s):
                    u = s % 2
                    dve.wait_ge(r_loaded[u], b * 16 * (NQ // 2) + 16 * (s // 2) + 16)
                    dve.wait_ge(out_ready, tiles0(b) + s + 1)
                    dve.tensor_tensor(res[u][:, :], ps_y, res[u][:, :], ALU.add).then_inc(y_done, 1)

                def first_stats(b):
                    take_stats(b, 0)
                    take_stats(b, 1)
                    dve.drain()
                    add_stats(0)
                    add_stats(1)

                def first_roots(b):
                    invert_std(b, 0)
                    invert_std(b, 1)
                    dve.drain()
                    normalise(0)
                    normalise(1)

                def first_turns(b):
                    turn(b, 0)
                    turn(b, 1)
                    take_stats(b, 2)
                    dve.drain()
                    add_stats(2)

                def third_tile(b):
                    invert_std(b, 2)
                    dve.drain()
                    normalise(2)

                def prepare(b):
                    first_stats(b)
                    first_roots(b)
                    first_turns(b)
                    third_tile(b)
                    dve.wait_ge(loaded, 16 * 3)

                def body(b, ahead):
                    for w in range(1, NQ + 1):
                        window(b, w)
                    invert(b, 0)
                    turn_qk(b, NQ - 2)
                    maximum(b, 2)
                    invert(b, 1)
                    maximum(b, 3)
                    invert(b, 2)
                    turn_qk(b, NQ - 1)
                    maximum(b, 4)
                    invert(b, 3)
                    for s in range(NQ):
                        if s:
                            collect(b, s - 1)
                        for m in range(H):
                            i = s * H + m + EXP_AHEAD
                            if i < HEADS:
                                maximum(b, i)
                            for c in quarter(s, m):
                                turn_prob(b, s, c)
                            if i - 1 < HEADS:
                                invert(b, i - 1)
                            if s and m == 1:
                                add_residual(b, s - 1)
                            if ahead and s == NQ - 1 and m in (0, 1):
                                (first_stats, first_roots)[m](b + 1)
                    if ahead:
                        first_turns(b + 1)
                    collect(b, NQ - 1)
                    if ahead:
                        third_tile(b + 1)
                    add_residual(b, NQ - 1)

                over_batches(dve, prepare, body)

            @block.gpsimd
            def _(pool):
                pool.sem_inc(gained_ready, 1)

                def rotate(b, j):
                    pool.wait_ge(rot_ready, tiles0(b) + j + 2)
                    pool.wait_ge(raw_ready, tiles0(b) + j + 1)
                    pool.sem_inc(seen, 1)
                    pool.tensor_tensor(gained[:, :, :], raw[:, :, :], gains[:, :, :], ALU.mult).then_inc(gained_ready, 1)
                    pool.drain()
                    for m in range(2):
                        one, other = slice(m * half, (m + 1) * half), slice((1 - m) * half, (2 - m) * half)
                        got = pool.tensor_tensor(by_sin[:, :, one], gained[:, :, other],
                                                 sin[:, j:j + 1, one].to_broadcast([P, HK, half]), ALU.mult)
                    got.then_inc(sin_ready, 1)

                def prepare(b):
                    pool.wait_ge(loaded, 16 * 3)

                def body(b, ahead):
                    for w in range(1, NQ + 1):
                        rotate(b, w - 1)
                    for i in range(HEADS):
                        u = i % (2 * H)
                        pool.wait_ge(inv_ready, heads0(b) + i + 1)
                        pool.sem_inc(seen, 1)
                        pool.tensor_scalar(prob[:, i % RING, 0:width(i)], prob[:, i % RING, 0:width(i)], inv[:, u:u + 1],
                                           1.0, ALU.mult, ALU.mult).then_inc(p_ready, 1)
                over_batches(pool, prepare, body)

            @block.tensor
            def _(pe):
                def turn(b, j):
                    pe.wait_ge(h_ready, tiles0(b) + j + 1)
                    for c in range(KB):
                        got = pe.transpose(ps_t[j % 2][:, c * P:(c + 1) * P], h[j % 2][:, c * P:(c + 1) * P], k.ident[:, :])
                    got.then_inc(t_ready, 1)

                def project(b, j):
                    u = j % 2
                    pe.wait_ge(t_lo, tiles0(b) + j + 1 + 2)
                    pe.wait_ge(rot_ready, tiles0(b) + j + 1)
                    for bank_, at, n in ((ps_kv[u], H * DH, 2 * DH), (ps_q[u], 0, H * DH)):
                        for c in range(KB):
                            got = split_products(pe, bank_[:, 0:n], (ht[0][u][:, c, :], ht[1][u][:, c, :]),
                                                 (k.wqkv_hi[:, c, at:at + n], k.wqkv_lo[:, c, at:at + n]),
                                                 c == 0, c == KB - 1)
                    got.then_inc(proj_ready, 1)

                def turn_qk(b, j):
                    u = j % 2
                    pe.wait_ge(rot_ready, tiles0(b) + j + 1 + 2)
                    pe.wait_ge(qk_lo, tiles0(b) + j + 1)
                    if j == 0:
                        pe.wait_ge(y_done, tiles0(b) + 1)
                    for m in range(H):
                        pe.transpose(ps_qt[:, m * P:(m + 1) * P], rot[u][:, m, :], k.ident[:, :])
                    pe.transpose(ps_kt[:, 0:P], rot[u][:, H, :], k.ident[:, :]).then_inc(qk_turned, 1)

                def scores(b, i):
                    m, s = i % H, i // H
                    if m == 0:
                        pe.wait_ge(qk_lo, tiles0(b) + s + 1 + 1)
                    pe.wait_ge(exp_ready, heads0(b) + i + 1)
                    tok = slice(s * P, (s + 1) * P)
                    qh, ql = (t[:, m, tok] for t in qt)
                    for at in range(0, width(i), 512):
                        cols = slice(at, min(at + 512, width(i)))
                        out = ps_s[i % 2][:, cols]
                        pe.matmul(out, qh, kt_[0][:, cols], start=True, stop=False)
                        if cols.stop == width(i):
                            pe.matmul(ps_s[i % 2][:, tok], k.ident_bf[:, :], k.causal_bf[:, :], start=False, stop=False)
                        pe.matmul(out, qh, kt_[1][:, cols], start=False, stop=False)
                        got = pe.matmul(out, ql, kt_[0][:, cols], start=False, stop=True)
                    got.then_inc(s_ready, 1)

                def turn_prob(b, s, c):
                    at = base[s] + c
                    if c == 0:
                        pe.wait_ge(p_ready, heads0(b) + H * (s + 1))
                    pe.wait_ge(p_lo, blocks0(b) + at + 1)
                    for m in range(H):
                        got = pe.transpose(ps_p[at % 2][:, m * P:(m + 1) * P],
                                           prob[:, (H * s + m) % RING, c * P:(c + 1) * P], k.ident[:, :])
                    got.then_inc(p_turned, 1)

                def values(b, s, c):
                    at = base[s] + c
                    if c == 0:
                        pe.wait_ge(o_lo, tiles0(b) + s + 1)
                    pe.wait_ge(p_lo, blocks0(b) + at + 1 + 2)
                    got = split_products(pe, ps_o, (v[0][:, c, :], v[1][:, c, :]),
                                         (pt[0][at % 2][:, :], pt[1][at % 2][:, :]), c == 0, c == keys(s) - 1)
                    if c == keys(s) - 1:
                        got.then_inc(o_ready, 1)

                def output(b, s):
                    pe.wait_ge(o_lo, tiles0(b) + s + 1 + 1)
                    pe.wait_ge(y_done, tiles0(b) + s + 1)
                    for m in range(H):
                        tok = slice(m * P, (m + 1) * P)
                        got = split_products(pe, ps_y, (ot[0][:, tok], ot[1][:, tok]),
                                             (k.wo_hi[:, m, :], k.wo_lo[:, m, :]), m == 0, m == H - 1)
                    got.then_inc(out_ready, 1)

                def prepare(b):
                    turn(b, 0)
                    turn(b, 1)
                    project(b, 0)

                def body(b, ahead):
                    turn(b, 2)
                    for j in range(1, NQ):
                        project(b, j)
                        if j >= 2:
                            turn_qk(b, j - 2)
                        if j + 2 < NQ:
                            turn(b, j + 2)
                    scores(b, 0)
                    scores(b, 1)
                    turn_qk(b, NQ - 2)
                    scores(b, 2)
                    scores(b, 3)
                    turn_qk(b, NQ - 1)
                    scores(b, 4)
                    pe.wait_ge(qk_lo, tiles0(b) + NQ + 1)
                    scores(b, 5)
                    for s in range(NQ):
                        for m in range(H):
                            for c in quarter(s, m):
                                turn_prob(b, s, c)
                            if s * H + m + SCORES_AHEAD < HEADS:
                                scores(b, s * H + m + SCORES_AHEAD)
                            if s and m == 0:
                                output(b, s - 1)
                            if ahead and s == NQ - 1 and m == H - 1:
                                pe.wait_ge(exp_ready, heads0(b) + HEADS + 2)
                                turn(b + 1, 0)
                                turn(b + 1, 1)
                            for c in quarter(s, m):
                                values(b, s, c)
                    if ahead:
                        project(b + 1, 0)
                    output(b, NQ - 1)

                over_batches(pe, prepare, body)


def build_program(nc, a, out):
    with ExitStack() as ctx:
        k = allocate_kept(nc, ctx)
        htab = nc.dram_tensor("htab", [ROWS, ROW], F32).ap()
        x1 = nc.dram_tensor("x_after_ffn", [ROWS, D], F32).ap()
        x2 = nc.dram_tensor("x_after_attention", [TOK, D], F32).ap()
        slot_dram = nc.dram_tensor("slot_table", [E * CAP], F32).ap()
        setup(nc, a, k, htab, (x1, out))

        def ffn(n, src, acc):
            with nc.sbuf_tensor(f"slots{n}", [HALF, 2 * E], U32) as slots:
                with nc.sbuf_tensor(f"logits{n}", [P, NT, 2 * E], F32) as logits:
                    dense_ffn(nc, k, n, src, acc, htab, logits)
                    route(nc, a, k, n, htab, logits, slot_dram, slots)
                routed_experts(nc, a, k, n, htab, acc, slots)

        ffn(0, a["x"], x1)
        attention(nc, a, k, x1, x2)
        ffn(1, x2, out)


def constants():
    tok = np.arange(TOK).reshape(NT, P)
    part, col = np.arange(P)[:, None], np.arange(P)[None, :]
    seg = np.ones((P, NT, E), np.float32)
    seg[:, :, 0] = 0.0
    diag = np.zeros((EG * SA, EG, SB_), np.float32)
    for g in range(EG):
        diag[g * SA:(g + 1) * SA, g, :] = 1.0
    dims = np.arange(DH // 2)
    ang = np.power(np.float32(2500.0), (-dims / (DH // 2)).astype(np.float32)).astype(np.float32)
    rad = np.arange(SEQ).astype(np.float32)[:, None] * ang[None, :]
    turn = lambda t: np.ascontiguousarray(t.astype(np.float32).reshape(NQ, P, DH // 2).transpose(1, 0, 2))
    return {
        "ident": np.eye(P, dtype=np.float32),
        "causal": np.where(col > part, np.float32(-1e30), np.float32(0)).astype(np.float32),
        "upto": (part <= col).astype(np.float32),
        "seg": seg,
        "iota_a": np.broadcast_to(np.arange(SA, dtype=np.float32), (P, SA)).copy(),
        "iota_b": np.broadcast_to(np.arange(SB_, dtype=np.float32), (P, SB_)).copy(),
        "tok_id": (tok.T - DUMP).astype(np.float32),
        "diag": diag,
        "dump": np.arange(HALF, dtype=np.float32)[:, None].copy(),
        "cos": turn(np.cos(rad)),
        "sin": np.concatenate([turn(-np.sin(rad)), turn(np.sin(rad))], 2),
    }


def laid_out(x, wq, wk, wv, wo, gq, gk, gate_w, bias, w_gate, w_up, w_down, sg, su, sd):
    rows = lambda w, blocks: w.reshape(blocks, P, -1).transpose(1, 0, 2)
    whole = lambda g, u, d: np.concatenate(
        [rows(np.concatenate([g.T, u.T], 1), KB).reshape(P, WGU), rows(d.T, FB).reshape(P, WDN)], 1)
    out = {
        "x": x.reshape(TOK, D),
        "router_w": rows(gate_w.T, KB),
        "bias": np.broadcast_to(bias, (P, E)),
        "w_shared": whole(sg, su, sd),
        "w_experts": np.stack([whole(w_gate[e], w_up[e], w_down[e]) for e in range(E)]),
        "w_qkv": rows(np.concatenate([wq, wk, wv], 1), KB),
        "w_out": rows(wo, H),
        "gains": np.broadcast_to(np.concatenate([gq.reshape(H, DH), gk.reshape(1, DH)], 0), (P, H + 1, DH)),
    }
    return {name: np.ascontiguousarray(t) for name, t in out.items()}


def kernel(**inputs):
    import concourse.bacc as bacc
    from concourse.bass_utils import run_bass_kernel_spmd

    arrays = laid_out(*(np.asarray(inputs[name]) for name in (
        "L0_attn_x", "L0_attn_wq", "L0_attn_wk", "L0_attn_wv", "L0_attn_wo", "L0_attn_gq", "L0_attn_gk",
        "L0_ffn_gate_w", "L0_ffn_bias", "L0_ffn_w_gate", "L0_ffn_w_up", "L0_ffn_w_down",
        "L0_ffn_sg", "L0_ffn_su", "L0_ffn_sd")))
    arrays.update(constants())
    arrays = {f"in_{name}": t for name, t in arrays.items()}
    nc = bacc.Bacc("TRN2", target_bir_lowering=False, num_devices=1)
    a = {name[3:]: nc.dram_tensor(name, t.shape, mybir.dt.from_np(t.dtype), kind="ExternalInput").ap()
         for name, t in arrays.items()}
    out = nc.dram_tensor("out", [ROWS, D], F32, kind="ExternalOutput").ap()
    build_program(nc, a, out)
    got = run_bass_kernel_spmd(nc, [arrays], core_ids=[0])
    return got.results[0]["out"][0:TOK].reshape(B, SEQ, D)
```

```python
from contextlib import ExitStack

import numpy as np

import concourse.bass as bass
from concourse import mybir

F32 = mybir.dt.float32
F32R = mybir.dt.float32r
BF16 = mybir.dt.bfloat16
I32 = mybir.dt.int32
U32 = mybir.dt.uint32
ALU = mybir.AluOpType
ACT = mybir.ActivationFunctionType
AX = mybir.AxisListType

P = 128
B, SEQ, D = 4, 1024, 512
TOK = B * SEQ
NT = TOK // P
KB = D // P
E, TOPK, FF = 32, 6, 256
FB = FF // P
CAP = 192
HALF = CAP // 2
ROUTE_SCALE = 1.5
H, DH = 4, 128
GT = 4
G = NT // GT
GTOK = GT * P
GA = 5
HT_OF = {5: 1, 6: 0, 7: 2}
SA, SB_ = 12, 16
ROW = D + E
DUMP = TOK
ROWS = TOK + HALF
EG = 8
GE = E // EG
HOTS = 4
NQ = SEQ // P
HEADS = NQ * H
EXP_AHEAD, SCORES_AHEAD = 5, 6
BEHIND = range(NQ // 2)
RING = 9
WGU, WDN = KB * 2 * FF, FB * D
WALL = WGU + WDN
NO_SLOT = 4000.0
SWIGLU_LIMIT = 10.0
LN_EPS, RMS_EPS = 1e-5, 1e-6


def split_products(pe, out, hi_lo_weights, hi_lo_moving, first, last):
    wh, wl = hi_lo_weights
    mh, ml = hi_lo_moving
    pe.matmul(out, wh, mh, start=first, stop=False)
    pe.matmul(out, wh, ml, start=False, stop=False)
    return pe.matmul(out, wl, mh, start=False, stop=last)


class Kept:
    pass


def own_semaphore(nc, k, name):
    k.ffn_semaphores.append(nc.alloc_semaphore(name=name))
    return k.ffn_semaphores[-1]


def allocate_kept(nc, ctx):
    k = Kept()
    k.ffn_semaphores = []

    def sb(name, shape, dt):
        return ctx.enter_context(nc.sbuf_tensor(name, shape, dt))

    k.ident = sb("ident", [P, P], F32)
    k.causal_bf = sb("causal_bf", [P, P], BF16)
    k.ident_bf = sb("ident_bf", [P, P], BF16)
    k.upto_bf = sb("upto_bf", [P, P], BF16)
    k.ones_bf = sb("ones_bf", [P, P], BF16)
    k.ln_eps = sb("ln_eps", [P, 1], F32)
    k.rms_eps = sb("rms_eps", [P, 1], F32)
    k.shared_hi = sb("shared_hi", [P, WALL], F32R)
    k.shared_lo = sb("shared_lo", [P, WALL], F32R)
    k.router = sb("router", [P, KB, 3, E], F32R)
    k.wqkv_hi = sb("wqkv_hi", [P, KB, 6 * DH], F32R)
    k.wqkv_lo = sb("wqkv_lo", [P, KB, 6 * DH], F32R)
    k.wo_hi = sb("wo_hi", [P, H, D], F32R)
    k.wo_lo = sb("wo_lo", [P, H, D], F32R)
    return k


def setup(nc, a, k, htab, accs):
    with ExitStack() as ctx:
        sb = lambda name, shape, dt: ctx.enter_context(nc.sbuf_tensor(name, shape, dt))
        sem = lambda name: ctx.enter_context(nc.semaphore(name))
        raw_shared = sb("raw_shared", [P, WALL], F32)
        raw_router = sb("raw_router", [P, KB, E], F32)
        raw_causal = sb("raw_causal", [P, P], F32)
        raw_upto = sb("raw_upto", [P, P], F32)
        zeros = sb("zeros", [HALF, ROW], F32)
        no_weights = sb("no_weights", [P, KB, E], F32)
        zeroed, dumps, hi_ready = sem("setup_zeroed"), sem("setup_dumps"), sem("setup_hi")
        loaded = {name: sem(f"setup_loaded_{name}") for name in ("small", "shared", "shared_down")}
        with nc.Block() as block:

            @block.sync
            def _(sp):
                for name, dst, src in (("small", raw_router[:, :, :], a["router_w"]), ("small", k.ident[:, :], a["ident"]),
                                       ("small", raw_causal[:, :], a["causal"]), ("small", raw_upto[:, :], a["upto"]),
                                       ("shared", raw_shared[:, 0:WGU], a["w_shared"][:, 0:WGU]),
                                       ("shared_down", raw_shared[:, WGU:], a["w_shared"][:, WGU:])):
                    sp.dma_start(dst, src).then_inc(loaded[name], 16)
                sp.wait_ge(zeroed, 1)
                sp.dma_start(htab[DUMP:ROWS, :], zeros[:, :]).then_inc(dumps, 16)
                for acc in accs:
                    sp.dma_start(acc[DUMP:ROWS, :], zeros[:, 0:D]).then_inc(dumps, 16)
                sp.wait_ge(dumps, 16 * (1 + len(accs)))

            @block.gpsimd
            def _(pool):
                pool.memset(k.ones_bf[:, :], 1.0)
                pool.memset(no_weights[:, :, :], 0.0)
                pool.memset(k.ln_eps[:, :], LN_EPS)
                pool.memset(k.rms_eps[:, :], RMS_EPS)
                pool.memset(zeros[:, :], 0.0).then_inc(zeroed, 1)

            @block.scalar
            def _(act):
                act.wait_ge(zeroed, 1)
                act.activation(k.router[:, :, 2, :], no_weights[:, :, :], ACT.Copy)
                act.wait_ge(loaded["small"], 16 * 4)
                act.activation(k.router[:, :, 0, :], raw_router[:, :, :], ACT.Copy).then_inc(hi_ready, 1)
                act.activation(k.ident_bf[:, :], k.ident[:, :], ACT.Copy)
                act.activation(k.causal_bf[:, :], raw_causal[:, :], ACT.Copy)
                act.activation(k.upto_bf[:, :], raw_upto[:, :], ACT.Copy)
                act.wait_ge(loaded["shared"], 16)
                act.activation(k.shared_hi[:, 0:WGU], raw_shared[:, 0:WGU], ACT.Copy).then_inc(hi_ready, 1)
                act.wait_ge(loaded["shared_down"], 16)
                act.activation(k.shared_hi[:, WGU:], raw_shared[:, WGU:], ACT.Copy).then_inc(hi_ready, 1)

            @block.vector
            def _(dve):
                for n, (lo, raw, hi) in enumerate(((k.router[:, :, 1, :], raw_router[:, :, :], k.router[:, :, 0, :]),
                                                   (k.shared_lo[:, 0:WGU], raw_shared[:, 0:WGU], k.shared_hi[:, 0:WGU]),
                                                   (k.shared_lo[:, WGU:], raw_shared[:, WGU:], k.shared_hi[:, WGU:]))):
                    dve.wait_ge(hi_ready, n + 1)
                    dve.tensor_tensor(lo, raw, hi.bitcast(F32), ALU.subtract)


def dense_ffn(nc, a, k, n, src, acc, htab, logits, ht_hi, ht_lo):
    with ExitStack() as ctx:
        sb = lambda name, shape, dt: ctx.enter_context(nc.sbuf_tensor(f"{name}{n}", shape, dt))
        pb = lambda name: ctx.enter_context(nc.psum_tensor(f"{name}{n}", [P, 512], F32))
        sem = lambda name: own_semaphore(nc, k, f"{name}{n}")
        x = [sb(f"d_x{u}_", [P, GT, D], F32) for u in range(3)]
        h = [sb(f"d_h{u}_", [P, GT, D], F32) for u in range(2)]
        y = [sb(f"d_y{u}_", [P, GT, D], F32) for u in range(2)]
        stats = sb("d_stats", [P, GT, 6], F32)
        mv = [sb(f"d_mv{u}_", [P, GT, 2], F32) for u in range(2)]
        std = [sb(f"d_std{u}_", [P, GT], F32) for u in range(2)]
        rstd = [sb(f"d_rstd{u}_", [P, GT], F32) for u in range(2)]
        silu = [sb(f"d_silu{b}_", [P, GTOK], F32) for b in range(FB)]
        inter = [sb(f"d_inter{b}_", [P, GTOK], F32) for b in range(FB)]
        in_hi = [sb(f"d_in_hi{u}_", [P, FB, GTOK], F32R) for u in range(2)]
        in_lo = [sb(f"d_in_lo{u}_", [P, FB, GTOK], F32R) for u in range(2)]
        ps_t = [pb(f"d_ps_t{i}_") for i in range(2)]
        ps_gate = [pb(f"d_ps_gate{b}_") for b in range(FB)]
        ps_up = [pb(f"d_ps_up{b}_") for b in range(FB)]
        ps_down = [pb(f"d_ps_down{i}_") for i in range(2)]
        lg_t = sb("d_lg_t", [3 * E, GTOK], F32)
        d_bank = (ps_down[0], ps_down[1], ps_gate[0], ps_up[0])
        t_bank = lambda c, late: ps_gate[c - 2] if late and c >= 2 else ps_t[c % 2]
        lg_banks = lambda late: ps_up if late else ps_t
        x_loaded = [[sem(f"d_x_loaded{u}{m}_") for m in range(2)] for u in range(3)]
        h_stored = [sem(f"d_h_stored{u}_") for u in range(2)]
        y_stored = [sem(f"d_y_stored{u}_") for u in range(2)]
        stats_ready, std_ready, h_ready = sem("d_stats_ready"), sem("d_std_ready"), sem("d_h_ready")
        t_ready, t_hi, t_lo = sem("d_t_ready"), sem("d_t_hi"), sem("d_t_lo")
        lg_ready, lg_out, lg_turned, lg_taken = sem("d_lg_ready"), sem("d_lg_out"), sem("d_lg_turned"), sem("d_lg_taken")
        gu_ready, silu_ready, mul_ready = sem("d_gu_ready"), sem("d_silu_ready"), sem("d_mul_ready")
        ihi_ready, ilo_ready = sem("d_ihi_ready"), sem("d_ilo_ready")
        d_ready, y_done = sem("d_d_ready"), sem("d_y_done")
        gu_hi = k.shared_hi[:, 0:WGU].rearrange("p (k c) -> p k c", k=KB)
        gu_lo = k.shared_lo[:, 0:WGU].rearrange("p (k c) -> p k c", k=KB)
        dn_hi = k.shared_hi[:, WGU:].rearrange("p (k c) -> p k c", k=FB)
        dn_lo = k.shared_lo[:, WGU:].rearrange("p (k c) -> p k c", k=FB)
        group = lambda ap, g: ap[bass.ds(g * GTOK, GTOK), :].rearrange("(j p) d -> p j d", p=P)
        whole = GA // 2
        half = lambda ap, g, m: ap[bass.ds(g * GTOK + m * (GTOK // 2), GTOK // 2), :].rearrange("(j p) d -> p j d", p=P)

        att_loaded = [sem(f"d_att_loaded{i}_") for i in range(3)]
        att_split = sem("d_att_split")
        raw_qkv = [y[i][:, :, :].rearrange("p j d -> p (j d)")[:, 0:2 * 6 * DH].rearrange("p (k c) -> p k c", k=2)
                   for i in range(2)]

        with nc.Block() as block:

            @block.sync
            def _(sp):
                def load(g, u, m):
                    sp.dma_start(x[u][:, 2 * m:2 * m + 2, :], half(src, g, m)).then_inc(x_loaded[u][m], 16)

                for u in range(2):
                    sp.sem_inc(h_stored[u], 16)
                    sp.sem_inc(y_stored[u], 16)
                    for m in range(2):
                        load(u, u, m)
                if n == 0:
                    sp.dma_start(x[2][:, :, :], a["w_out"]).then_inc(att_loaded[0], 16)
                    for i in range(2):
                        sp.dma_start(raw_qkv[i], a["w_qkv"][:, 2 * i:2 * i + 2, :]).then_inc(att_loaded[1 + i], 16)
                sp.wait_ge(h_ready, 1)
                sp.dma_start(group(htab, 0)[:, :, 0:D], h[0][:, :, :]).then_inc(h_stored[0], 16)
                if n == 0:
                    sp.wait_ge(att_split, 1)
                for m in range(2):
                    load(GA + 1, 2, m)

                def body(i, u, load_last=False):
                    g = 2 * i + u
                    sp.wait_ge(h_ready, g + 2)
                    sp.dma_start(group(htab, g + 1)[:, :, 0:D], h[1 - u][:, :, :]).then_inc(h_stored[1 - u], 16)
                    if load_last:
                        load(g + 3, 1 - u, 0)
                        load(g + 3, 1 - u, 1)
                    for m in range(2):
                        sp.wait_ge(y_done, 4 * g + 2 * m + 2 + 2)
                        if not load_last:
                            load(g + 2, u, m)
                    sp.dma_start(group(acc, g), y[u][:, :, :]).then_inc(y_stored[u], 16)

                with sp.Fori(0, whole) as i:
                    body(i, 0)
                    body(i, 1)
                body(whole, 0, load_last=True)
                for g in range(GA + 1, G):
                    sp.wait_ge(h_ready, g + 1)
                    sp.dma_start(group(htab, g)[:, :, 0:D], h[g % 2][:, :, :]).then_inc(h_stored[g % 2], 16)
                for u in range(2):
                    sp.wait_ge(h_stored[u], 16 * (G // 2 + 1))
                    sp.wait_ge(y_stored[u], 16 * ((GA + 1 - u) // 2 + 1))

            @block.gpsimd
            def _(pool):
                if n == 0:
                    for i, (hi, lo, raw) in enumerate(((k.wo_hi[:, :, :], k.wo_lo[:, :, :], x[2][:, :, :]),
                                                       (k.wqkv_hi[:, 0:2, :], k.wqkv_lo[:, 0:2, :], raw_qkv[0]),
                                                       (k.wqkv_hi[:, 2:4, :], k.wqkv_lo[:, 2:4, :], raw_qkv[1]))):
                        pool.wait_ge(att_loaded[i], 16)
                        pool.tensor_copy(hi, raw)
                        pool.drain()
                        pool.tensor_tensor(lo, raw, hi.bitcast(F32), ALU.subtract).then_inc(att_split, 1)

            @block.scalar
            def _(act):
                def root(g, u):
                    act.wait_ge(stats_ready, g + 1)
                    act.activation(std[u][:, :], mv[u][:, :, 1], ACT.Sqrt, bias=k.ln_eps[:, :]).then_inc(std_ready, 1)

                def turn(g, u, late=False):
                    for c in range(KB):
                        act.wait_ge(t_ready, 4 * g + c + 1)
                        act.activation(ht_hi[u][:, c, :], t_bank(c, late)[:, :], ACT.Copy).then_inc(t_hi, 1)
                    act.wait_ge(lg_ready, g + 1)
                    act.activation(lg_t[:, :], lg_banks(late)[0][0:3 * E, :], ACT.Copy).then_inc(lg_out, 1)

                def inner(g, u, b):
                    act.wait_ge(gu_ready, 2 * g + b + 1)
                    act.activation(silu[b][:, :], ps_gate[b][:, :], ACT.Silu).then_inc(silu_ready, 1)
                    act.wait_ge(mul_ready, 2 * g + b + 1 + 2)
                    act.activation(in_hi[u][:, b, :], inter[b][:, :], ACT.Copy).then_inc(ihi_ready, 1)

                def body(i, u):
                    g = 2 * i + u
                    root(g + 1, 1 - u)
                    inner(g, u, 0)
                    inner(g, u, 1)
                    turn(g + 1, 1 - u)

                root(0, 0)
                turn(0, 0)
                with act.Fori(0, whole) as i:
                    body(i, 0)
                    body(i, 1)
                body(whole, 0)
                for g in range(GA + 1, G):
                    root(g, g % 2)
                for g in range(GA + 1, G):
                    turn(g, HT_OF[g], late=True)

            @block.vector
            def _(dve):
                dve.sem_inc(t_lo, 2)
                dve.sem_inc(mul_ready, 2)
                dve.sem_inc(y_done, 2)

                def take_stats(i, u, third=False):
                    v = 2 if third else u
                    for m in range(2):
                        dve.wait_ge(x_loaded[v][m], 16 if third else 16 * i + 16)
                        for j in (2 * m, 2 * m + 1):
                            dve.bn_stats(stats[:, j, :], x[v][:, j, :])
                    dve.drain()
                    for j in range(GT):
                        got = dve.bn_aggr(mv[u][:, j, :], stats[:, j, :])
                    got.then_inc(stats_ready, 1)

                def normalise(i, u, third=False):
                    v = 2 if third else u
                    dve.wait_ge(std_ready, 2 * i + u + 1)
                    dve.reciprocal(rstd[u][:, :], std[u][:, :])
                    dve.drain()
                    dve.wait_ge(h_stored[u], 16 * i + 16)
                    for j in range(GT):
                        got = dve.tensor_scalar(h[u][:, j, :], x[v][:, j, :], mv[u][:, j, 0:1],
                                                rstd[u][:, j:j + 1], ALU.subtract, ALU.mult)
                    got.then_inc(h_ready, 1)

                def turn(g, u, late=False):
                    for c in range(KB):
                        dve.wait_ge(t_hi, 4 * g + c + 1)
                        dve.tensor_tensor(ht_lo[u][:, c, :], t_bank(c, late)[:, :], ht_hi[u][:, c, :].bitcast(F32),
                                          ALU.subtract).then_inc(t_lo, 1)

                def take_logits(g, late=False):
                    dve.wait_ge(lg_turned, g + 1)
                    dve.tensor_scalar(logits[:, bass.ds(g * GT, GT), :],
                                      lg_banks(late)[1][:, 0:GT * 3 * E].rearrange("p (j c) -> p j c", j=GT)[:, :, 0:2 * E],
                                      1.0, None, ALU.mult).then_inc(lg_taken, 1)

                def inner(g, u, b):
                    dve.wait_ge(silu_ready, 2 * g + b + 1)
                    dve.tensor_tensor(inter[b][:, :], silu[b][:, :], ps_up[b][:, :], ALU.mult)
                    dve.drain()
                    dve.tensor_scalar(inter[b][:, :], inter[b][:, :], SWIGLU_LIMIT, -SWIGLU_LIMIT,
                                      ALU.min, ALU.max).then_inc(mul_ready, 1)
                    dve.wait_ge(ihi_ready, 2 * g + b + 1)
                    dve.tensor_tensor(in_lo[u][:, b, :], inter[b][:, :], in_hi[u][:, b, :].bitcast(F32),
                                      ALU.subtract).then_inc(ilo_ready, 1)

                def body(i, u):
                    g = 2 * i + u
                    take_stats(i + u, 1 - u)
                    normalise(i + u, 1 - u)
                    inner(g, u, 0)
                    take_logits(g)
                    inner(g, u, 1)
                    dve.wait_ge(y_stored[u], 16 * i + 16)
                    if n == 0:
                        dve.wait_ge(att_split, 2 + u)

                    def add_residual(j):
                        dve.wait_ge(d_ready, 4 * g + j + 1)
                        dve.scalar_tensor_tensor(y[u][:, j, :], d_bank[j][:, :], 0.5, x[u][:, j, :],
                                                 ALU.mult, ALU.add).then_inc(y_done, 1)

                    for j in range(GT):
                        dve.wait_ge(t_hi, 4 * g + 4 + j + 1)
                        dve.tensor_tensor(ht_lo[1 - u][:, j, :], ps_t[j % 2][:, :],
                                          ht_hi[1 - u][:, j, :].bitcast(F32), ALU.subtract).then_inc(t_lo, 1)
                        if j:
                            add_residual(j - 1)
                    add_residual(GT - 1)

                take_stats(0, 0)
                normalise(0, 0)
                turn(0, 0)
                with dve.Fori(0, whole) as i:
                    body(i, 0)
                    body(i, 1)
                body(whole, 0)
                take_stats(GA // 2, 0, third=True)
                normalise((GA + 1) // 2, 0, third=True)
                take_logits(GA)
                take_stats((GA + 2) // 2, 1)
                turn(GA + 1, HT_OF[GA + 1], late=True)
                normalise((GA + 2) // 2, 1)
                take_logits(GA + 1, late=True)
                turn(GA + 2, HT_OF[GA + 2], late=True)
                take_logits(GA + 2, late=True)

            @block.tensor
            def _(pe):
                def turn(g, u, c, late=False):
                    if not late:
                        pe.wait_ge(t_lo, 4 * g + c + 1)
                    for j in range(GT):
                        got = pe.transpose(t_bank(c, late)[:, j * P:(j + 1) * P], h[u][:, j, c * P:(c + 1) * P],
                                           k.ident[:, :])
                    got.then_inc(t_ready, 1)

                def router(g, u, late=False):
                    pe.wait_ge(t_lo, 4 * g + 4 + 2)
                    for c in range(KB):
                        for part, ht in enumerate((ht_hi, ht_lo)):
                            got = pe.matmul(lg_banks(late)[0][0:3 * E, :], k.router[:, c, :, :].rearrange("p s e -> p (s e)"),
                                            ht[u][:, c, :], start=(c == 0 and part == 0),
                                            stop=(c == KB - 1 and part == 1))
                    got.then_inc(lg_ready, 1)

                def turn_logits(g, late=False):
                    pe.wait_ge(lg_out, g + 1)
                    for j in range(GT):
                        got = pe.transpose(lg_banks(late)[1][:, j * 3 * E:(j + 1) * 3 * E], lg_t[:, j * P:(j + 1) * P],
                                           k.ident[0:3 * E, 0:3 * E])
                    got.then_inc(lg_turned, 1)

                def gate_up(g, u, b):
                    pe.wait_ge(mul_ready, 2 * g + b + 1)
                    for n_, (bank, at) in enumerate(((ps_gate[b], b * P), (ps_up[b], FF + b * P))):
                        if b == 0:
                            pe.wait_ge(y_done, 4 * g + n_ + 1)
                        for c in range(KB):
                            got = split_products(pe, bank[:, :], (gu_hi[:, c, at:at + P], gu_lo[:, c, at:at + P]),
                                                 (ht_hi[u][:, c, :], ht_lo[u][:, c, :]), c == 0, c == KB - 1)
                    got.then_inc(gu_ready, 1)

                def down(g, u, j, b):
                    pe.wait_ge(ilo_ready, 2 * g + b + 1)
                    tok = slice(j * P, (j + 1) * P)
                    got = split_products(pe, d_bank[j][:, :], (in_hi[u][:, b, tok], in_lo[u][:, b, tok]),
                                         (dn_hi[:, b, :], dn_lo[:, b, :]), b == 0, b == FB - 1)
                    if b == FB - 1:
                        got.then_inc(d_ready, 1)

                def body(i, u):
                    g = 2 * i + u
                    gate_up(g, u, 0)
                    turn_logits(g)
                    gate_up(g, u, 1)
                    pe.wait_ge(h_ready, g + 2)
                    pe.wait_ge(lg_taken, g + 1)
                    turn(g + 1, 1 - u, 0)
                    turn(g + 1, 1 - u, 1)
                    for j in range(GT):
                        down(g, u, j, 0)
                    for j in range(GT):
                        down(g, u, j, 1)
                        if j < 2:
                            turn(g + 1, 1 - u, j + 2)
                    router(g + 1, 1 - u)

                pe.wait_ge(h_ready, 1)
                for c in range(KB):
                    turn(0, 0, c)
                router(0, 0)
                with pe.Fori(0, whole) as i:
                    body(i, 0)
                    body(i, 1)
                body(whole, 0)
                turn_logits(GA)
                pe.wait_ge(mul_ready, FB * GA + 2)
                pe.wait_ge(y_done, 4 * GA + 2)
                pe.wait_ge(lg_taken, GA + 1)
                for g in range(GA + 1, G):
                    pe.wait_ge(h_ready, g + 1)
                    for c in range(KB):
                        turn(g, g % 2, c, late=True)
                    if g == G - 1:
                        turn_logits(g - 1, late=True)
                    router(g, HT_OF[g], late=True)
                pe.wait_ge(lg_taken, G - 1)
                turn_logits(G - 1, late=True)


def route(nc, a, k, n, src, acc, htab, logits, ht_hi, ht_lo, slots, raw, w_loaded, y_stored):
    with ExitStack() as ctx:
        sb = lambda name, shape, dt: ctx.enter_context(nc.sbuf_tensor(f"{name}{n}", shape, dt))
        pb = lambda name: ctx.enter_context(nc.psum_tensor(f"{name}{n}", [P, 512], F32))
        sem = lambda name: own_semaphore(nc, k, f"{name}{n}")
        wide = [P, NT, E]
        t1, t2, t3, t4, t5 = (sb(f"r_t{i}_", wide, F32) for i in range(1, 6))
        score = sb("r_score", wide, F32)
        seg = sb("r_seg", wide, F32)
        mask = sb("r_mask", wide, BF16)
        bias = sb("r_bias", [P, E], F32)
        top8 = sb("r_top8", [P, NT, 8], F32)
        per_tok = sb("r_per_tok", [P, NT], F32)
        slot_a = sb("r_slot_a", wide, BF16)
        slot_b = sb("r_slot_b", wide, BF16)
        iota_a = sb("r_iota_a", [P, SA, E], BF16)
        iota_b = sb("r_iota_b", [P, SB_, E], BF16)
        part_id = sb("r_part_id", [P, 1], F32)
        tile_id = sb("r_tile_id", [P, NT], F32)
        diag = sb("r_diag", [SA * EG, SB_, EG], F32)
        dump = sb("r_dump", [HALF, 1], F32)
        hot_a = [sb(f"r_hot_a{u}_", [P, GE, SA, EG], BF16) for u in range(HOTS)]
        part_a = [sb(f"r_part_a{u}_", [P, GE, SA, EG], BF16) for u in range(HOTS)]
        tile_a = [sb(f"r_tile_a{u}_", [P, GE, SA, EG], BF16) for u in range(HOTS)]
        hot_b = [sb(f"r_hot_b{u}_", [P, SB_, E], BF16) for u in range(HOTS)]
        picked = sb("r_picked", [SA * EG, GE, SB_, EG], F32)
        table = sb("r_table", [SA * EG, GE, SB_], F32)
        table2 = sb("r_table2", [SA * EG, GE, SB_], F32)
        to_slot = sb("r_to_slot", [GE * SB_, SA // 2, HALF], F32)
        own_group = sb("r_own_group", [GE * SB_, GE], F32)
        by_group = (picked[0:GE * SB_, :, :, :].rearrange("p g b e -> p (g b e)")[:, 0:GE * SA * EG]
                    .rearrange("p (g a e) -> p g a e", g=GE, a=SA))
        idx = sb("r_idx", [HALF, 2 * E], F32)
        off = sb("r_off", [HALF, 2 * E], F32)
        ps_cum = [pb(f"r_ps_cum{i}_") for i in range(2)]
        ps_tot = [pb(f"r_ps_tot{i}_") for i in range(2)]
        ps_tab = pb("r_ps_tab")
        xs = [sb(f"r_xs{u}_", [P, GT, D], F32) for u in range(2)]
        silu, inter = sb("r_silu", [P, GTOK], F32), sb("r_inter", [P, GTOK], F32)
        raw_a = silu[:, 0:SA * E].rearrange("p (s e) -> p s e", e=E)
        raw_b = inter[:, :].rearrange("p (s e) -> p s e", e=E)
        in_hi, in_lo = sb("r_in_hi", [P, FB, GTOK], F32R), sb("r_in_lo", [P, FB, GTOK], F32R)
        ps_gate, ps_up = pb("r_ps_gate"), pb("r_ps_up")
        gu_banks = lambda g, b: {(GA, 1): ps_cum, (GA + 2, 1): ps_tot}.get((g, b), (ps_gate, ps_up))
        d_bank = lambda g, j: (ps_gate, ps_up, ps_tot[0], ps_tot[1])[j] if g == GA + 2 else ps_down[j % 2]
        ps_down = [pb("r_ps_down"), ps_tab]
        gu_hi = k.shared_hi[:, 0:WGU].rearrange("p (k c) -> p k c", k=KB)
        gu_lo = k.shared_lo[:, 0:WGU].rearrange("p (k c) -> p k c", k=KB)
        dn_hi = k.shared_hi[:, WGU:].rearrange("p (k c) -> p k c", k=FB)
        dn_lo = k.shared_lo[:, WGU:].rearrange("p (k c) -> p k c", k=FB)
        group = lambda ap, g: ap[g * GTOK:(g + 1) * GTOK, :].rearrange("(j p) d -> p j d", p=P)
        x_loaded = [sem(f"r_x_loaded{u}_") for u in range(2)]
        gu_ready, silu_ready, mul_ready = sem("r_gu_ready"), sem("r_silu_ready"), sem("r_mul_ready")
        ihi_ready, ilo_ready = sem("r_ihi_ready"), sem("r_ilo_ready")
        d_ready, y_done = sem("r_d_ready"), sem("r_y_done")
        iotas, seen, idt = sem("r_iotas"), sem("r_seen_by_gpsimd"), sem("r_idt")
        hotb, zeroed, tot_read = sem("r_hotb"), sem("r_zeroed"), sem("r_tot_read")
        no_slots = sb("r_no_slots", [P, SA * EG], BF16)
        loaded, w_stored, weighed, inverted = sem("r_loaded"), sem("r_w_stored"), sem("r_weighed"), sem("r_inverted")
        grouped = sem("r_grouped")
        lg_sum, exp_done, poly, ln_done = sem("r_lg_sum"), sem("r_exp"), sem("r_poly"), sem("r_ln")
        sp_done, score_done, mask_done, w_done = sem("r_sp"), sem("r_score_d"), sem("r_mask_d"), sem("r_w")
        counted, code_done = sem("r_counted"), sem("r_code_d")
        hots, ida, tabbed, tab_done = sem("r_hots"), sem("r_ida"), sem("r_tabbed"), sem("r_tab")
        turned = sem("r_turned")
        flat = lambda t: t[:, :, :].rearrange("p t e -> p (t e)")
        per_token = lambda ap: ap.rearrange("p (t o) -> p t o", o=1).to_broadcast(wide)

        with nc.Block() as block:

            @block.sync
            def _(sp):
                for dst, from_ in ((bias[:, :], a["bias"]), (seg[:, :, :], a["seg"]), (raw_a, a["iota_a"]),
                                 (raw_b, a["iota_b"]), (tile_id[:, :], a["tile_id"]), (part_id[:, :], a["part_id"]),
                                 (diag[:, :, :], a["diag"]), (dump[:, :], a["dump"]),
                                 (to_slot[:, :, :], a["to_slot"]), (own_group[:, :], a["own_group"])):
                    sp.dma_start(dst, from_).then_inc(loaded, 16)
                for g in range(GA, GA + 2):
                    sp.dma_start(xs[(g - GA) % 2][:, :, :], group(src, g)).then_inc(x_loaded[(g - GA) % 2], 16)

                def store(g):
                    sp.wait_ge(y_done, 4 * (g - GA) + 4)
                    sp.dma_start(group(acc, g), xs[(g - GA) % 2][:, :, :]).then_inc(y_stored[(g - GA) % 2], 16)

                for u, g in ((HT_OF[GA], GA), (HT_OF[GA + 1], GA + 1)):
                    sp.wait_ge(gu_ready, FB * (g - GA) + FB)
                    sp.dma_start(raw[u][:, :], a["w_experts"][u, :, :]).then_inc(w_loaded[u], 16)
                    if g == GA:
                        store(GA)
                        sp.wait_ge(y_stored[0], 16)
                        sp.dma_start(xs[0][:, :, :], group(src, GA + 2)).then_inc(x_loaded[0], 16)
                store(GA + 1)
                sp.wait_ge(w_done, 1)
                with nc.allow_non_contiguous_dma(reason="32 weights behind each row of tokens"):
                    sp.dma_start(htab[0:TOK, D:ROW].rearrange("(t p) e -> p t e", p=P), t1[:, :, :]).then_inc(w_stored, 16)
                store(GA + 2)
                sp.wait_ge(w_stored, 16)

            @block.scalar
            def _(act):
                act.wait_ge(lg_sum, 1)
                act.activation(t2[:, :, :], t1[:, :, :], ACT.Abs)
                act.drain()
                act.activation(t3[:, :, :], t2[:, :, :], ACT.Exp, scale=-1.0).then_inc(exp_done, 1)
                act.drain()
                act.activation(t4[:, :, :], t3[:, :, :], ACT.Ln, bias=1.0).then_inc(ln_done, 1)

                def inner(g, b):
                    at = FB * (g - GA) + b
                    act.wait_ge(gu_ready, at + 1)
                    act.activation(silu[:, :], gu_banks(g, b)[0][:, :], ACT.Silu).then_inc(silu_ready, 1)
                    act.wait_ge(mul_ready, at + 1)
                    act.activation(in_hi[:, b, :], inter[:, :], ACT.Copy).then_inc(ihi_ready, 1)

                act.wait_ge(loaded, 16 * 10)
                act.activation(iota_a[:, :, :], raw_a, ACT.Copy)
                act.activation(iota_b[:, :, :], raw_b, ACT.Copy).then_inc(iotas, 1)
                act.drain()
                inner(GA, 0)
                act.wait_ge(sp_done, 1)
                act.activation(score[:, :, :], t5[:, :, :], ACT.Sqrt).then_inc(score_done, 1)
                inner(GA, 1)
                inner(GA + 1, 0)
                inner(GA + 1, 1)
                inner(GA + 2, 0)
                inner(GA + 2, 1)
                with act.Fori(0, NT // HOTS) as i:
                    for u in range(HOTS):
                        act.wait_ge(hots, HOTS * i + u + 1)
                        act.wait_ge(tabbed, HOTS * i + u + 1)
                        act.activation(tile_a[u][:, :, :, :], hot_a[u][:, :, :, :], ACT.Copy,
                                       scale=tile_id[:, bass.ds(HOTS * i + u, 1)]).then_inc(ida, 1)

            @block.gpsimd
            def _(pool):
                pool.memset(no_slots[:, :], 0.0).then_inc(zeroed, 1)

                def split_inner(g, b):
                    pool.wait_ge(ihi_ready, FB * (g - GA) + b + 1)
                    pool.tensor_tensor(in_lo[:, b, :], inter[:, :], in_hi[:, b, :].bitcast(F32),
                                       ALU.subtract).then_inc(ilo_ready, 1)

                split_inner(GA, 0)
                split_inner(GA, 1)
                pool.wait_ge(mask_done, 1)
                pool.tensor_tensor(t1[:, :, :], score[:, :, :], mask[:, :, :], ALU.mult).then_inc(weighed, 1)
                split_inner(GA + 1, 0)
                split_inner(GA + 1, 1)
                pool.wait_ge(inverted, 1)
                pool.tensor_tensor(t1[:, :, :], t1[:, :, :], per_token(per_tok[:, :]), ALU.mult).then_inc(w_done, 1)
                split_inner(GA + 2, 0)
                split_inner(GA + 2, 1)
                pool.wait_ge(loaded, 16 * 10)
                with pool.Fori(0, NT // HOTS) as i:
                    for u in range(HOTS):
                        pool.wait_ge(hots, HOTS * i + u + 1)
                        pool.wait_ge(tabbed, HOTS * i + u + 1)
                        pool.sem_inc(seen, 1)
                        pool.tensor_scalar(part_a[u][:, :, :, :], hot_a[u][:, :, :, :], part_id[:, :], 1.0,
                                           ALU.mult, ALU.mult).then_inc(idt, 1)

            @block.vector
            def _(dve):
                def inner(g, b):
                    at = FB * (g - GA) + b
                    dve.wait_ge(silu_ready, at + 1)
                    if at:
                        dve.wait_ge(ilo_ready, at)
                    dve.tensor_tensor(inter[:, :], silu[:, :], gu_banks(g, b)[1][:, :], ALU.mult)
                    dve.drain()
                    dve.tensor_scalar(inter[:, :], inter[:, :], SWIGLU_LIMIT, -SWIGLU_LIMIT,
                                      ALU.min, ALU.max).then_inc(mul_ready, 1)

                def add_residual(g, j):
                    u = (g - GA) % 2
                    dve.wait_ge(x_loaded[u], 16 * ((g - GA) // 2) + 16)
                    dve.wait_ge(d_ready, 4 * (g - GA) + j + 1)
                    dve.scalar_tensor_tensor(xs[u][:, j, :], d_bank(g, j)[:, :], 0.5, xs[u][:, j, :],
                                             ALU.mult, ALU.add).then_inc(y_done, 1)

                dve.tensor_tensor(t1[:, :, :], logits[:, :, 0:E], logits[:, :, E:2 * E], ALU.add).then_inc(lg_sum, 1)
                dve.wait_ge(exp_done, 1)
                dve.tensor_scalar(t5[:, :, :], t3[:, :, :], 1.0 / 3.0, -0.5, ALU.mult, ALU.add)
                small = flat(score).bitcast(U32)
                dve.tensor_scalar(small, flat(t3), 0.01, None, ALU.is_lt)
                dve.drain()
                dve.tensor_tensor(t2[:, :, :], t5[:, :, :], t3[:, :, :], ALU.mult)
                dve.drain()
                dve.scalar_tensor_tensor(t5[:, :, :], t2[:, :, :], 1.0, t3[:, :, :], ALU.add, ALU.mult)
                dve.wait_ge(ln_done, 1)
                dve.drain()
                dve.copy_predicated(flat(t4), small, flat(t5))
                dve.drain()
                dve.scalar_tensor_tensor(t5[:, :, :], t1[:, :, :], 0.0, t4[:, :, :], ALU.max, ALU.add).then_inc(sp_done, 1)
                inner(GA, 0)
                dve.wait_ge(score_done, 1)
                dve.wait_ge(loaded, 16 * 10)
                dve.tensor_tensor(t1[:, :, :], score[:, :, :],
                                  bias[:, :].rearrange("p (o e) -> p o e", o=1).to_broadcast(wide), ALU.add)
                dve.drain()
                for t in range(NT):
                    dve.max(top8[:, t, :], t1[:, t, :])
                    if t == 3:
                        inner(GA, 1)
                dve.drain()
                sixth = top8[:, :, TOPK - 1:TOPK].to_broadcast(wide)
                dve.tensor_tensor(t2[:, :, :], t1[:, :, :], sixth, ALU.is_gt)
                dve.tensor_tensor(t3[:, :, :], t1[:, :, :], sixth, ALU.is_equal)
                dve.drain()
                dve.tensor_reduce(per_tok[:, :], t2[:, :, :], AX.X, ALU.add)
                dve.tensor_tensor_scan(flat(t4), flat(seg), flat(t3), 0.0, ALU.mult, ALU.add)
                add_residual(GA, 0)
                add_residual(GA, 1)
                dve.drain()
                dve.tensor_tensor(t5[:, :, :], t4[:, :, :], per_token(per_tok[:, :]), ALU.add)
                add_residual(GA, 2)
                dve.drain()
                dve.scalar_tensor_tensor(t4[:, :, :], t5[:, :, :], float(TOPK), t3[:, :, :], ALU.is_le, ALU.mult)
                add_residual(GA, 3)
                dve.drain()
                dve.tensor_tensor(mask[:, :, :], t4[:, :, :], t2[:, :, :], ALU.add).then_inc(mask_done, 1)
                inner(GA + 1, 0)
                dve.drain()
                inner(GA + 1, 1)
                dve.wait_ge(counted, 1)
                by_expert = lambda t: flat(t).rearrange("p (e t) -> p e t", t=NT)
                for i in range(2):
                    got = dve.tensor_copy(by_expert(t2)[:, :, i * NT // 2:(i + 1) * NT // 2],
                                          ps_tot[i][:, :].rearrange("p (t e) -> p e t", e=E))
                got.then_inc(tot_read, 1)
                dve.drain()
                dve.tensor_tensor_scan(flat(t3), flat(seg), flat(t2), 0.0, ALU.mult, ALU.add)
                add_residual(GA + 1, 0)
                add_residual(GA + 1, 1)
                dve.drain()
                dve.tensor_tensor(t4[:, :, :], t3[:, :, :], t2[:, :, :], ALU.subtract)
                dve.drain()
                for i in range(2):
                    dve.tensor_tensor(t5[:, i * NT // 2:(i + 1) * NT // 2, :],
                                      ps_cum[i][:, :].rearrange("p (t e) -> p t e", e=E),
                                      by_expert(t4)[:, :, i * NT // 2:(i + 1) * NT // 2].rearrange("p e t -> p t e"),
                                      ALU.add)
                dve.drain()
                dve.scalar_tensor_tensor(t2[:, :, :], t5[:, :, :], float(CAP), mask[:, :, :], ALU.is_le, ALU.mult)
                dve.wait_ge(weighed, 1)
                dve.tensor_reduce(per_tok[:, :], t1[:, :, :], AX.X, ALU.add)
                dve.drain()
                dve.reciprocal(top8[:, :, 0:1].rearrange("p t o -> p (t o)"), per_tok[:, :])
                dve.scalar_tensor_tensor(t3[:, :, :], t5[:, :, :], -1.0 - NO_SLOT, t2[:, :, :], ALU.add, ALU.mult)
                dve.drain()
                dve.tensor_scalar(per_tok[:, :], top8[:, :, 0:1].rearrange("p t o -> p (t o)"), ROUTE_SCALE * 0.5, None,
                                  ALU.mult).then_inc(inverted, 1)
                add_residual(GA + 1, 2)
                add_residual(GA + 1, 3)
                dve.drain()
                code, code_a, code_b = (flat(t).bitcast(I32) for t in (t2, t4, t5))
                dve.tensor_scalar(code, flat(t3), NO_SLOT, None, ALU.add)
                dve.drain()
                dve.tensor_scalar(code_a, code, 4, None, ALU.arith_shift_right)
                dve.tensor_scalar(code_b, code, SB_ - 1, None, ALU.bitwise_and)
                dve.drain()
                dve.tensor_copy(flat(slot_a), code_a)
                dve.tensor_copy(flat(slot_b), code_b)
                inner(GA + 2, 0)
                dve.wait_ge(iotas, 1)
                inner(GA + 2, 1)
                dve.drain()
                with dve.Fori(0, NT // HOTS) as i:
                    for u in range(HOTS):
                        t = HOTS * i + u
                        dve.wait_ge(tabbed, HOTS * i + u + 1)
                        dve.tensor_tensor(hot_a[u][:, :, :, :],
                                          slot_a[:, bass.ds(t, 1), :].rearrange("p o (g e) -> p g o e", g=GE)
                                          .to_broadcast([P, GE, SA, EG]),
                                          iota_a[:, :, :].rearrange("p s (g e) -> p g s e", g=GE),
                                          ALU.is_equal).then_inc(hots, 1)
                        dve.tensor_tensor(hot_b[u][:, :, :], slot_b[:, bass.ds(t, 1), :].to_broadcast([P, SB_, E]),
                                          iota_b[:, :, :], ALU.is_equal).then_inc(hotb, 1)
                dve.wait_ge(tabbed, NT + HOTS)
                for g in range(E // EG):
                    dve.tensor_tensor(picked[:, g, :, :],
                                      ps_tab[0:SA * EG, g * EG * SB_:(g + 1) * EG * SB_].rearrange("p (s e) -> p s e", e=EG),
                                      diag[:, :, :], ALU.mult)
                dve.drain()
                for g in range(E // EG):
                    dve.tensor_reduce(table[:, g, :], picked[:, g, :, :], AX.X, ALU.add)
                dve.drain()
                dve.tensor_scalar(table2[:, :, :], table[:, :, :], float(DUMP), None, ALU.add).then_inc(tab_done, 1)
                add_residual(GA + 2, 0)
                add_residual(GA + 2, 1)
                dve.wait_ge(turned, 1)
                dve.tensor_tensor(by_group[:, :, :, :].rearrange("p g a e -> p g (a e)"),
                                  ps_tab[0:GE * SB_, 0:SA * EG].rearrange("p (o r) -> p o r", o=1)
                                  .to_broadcast([GE * SB_, GE, SA * EG]),
                                  own_group[:, :].rearrange("p (g o) -> p g o", o=1).to_broadcast([GE * SB_, GE, SA * EG]),
                                  ALU.mult).then_inc(grouped, 1)
                add_residual(GA + 2, 2)
                add_residual(GA + 2, 3)
                dve.wait_ge(turned, 2)
                dve.tensor_copy(idx[:, :], ps_cum[0][0:HALF, 0:2 * E])
                dve.drain()
                dve.tensor_scalar(off[:, :], idx[:, :], float(DUMP), dump[:, :], ALU.is_ge, ALU.mult)
                dve.drain()
                in_halves = lambda t: t[:, :].rearrange("s (h e) -> s h e", h=2)
                dve.memset(slots[:, 2 * E:], 0)
                dve.tensor_tensor(slots[:, 0:2 * E].rearrange("s (e h) -> s h e", h=2), in_halves(idx), in_halves(off), ALU.add)

            @block.tensor
            def _(pe):
                pe.wait_ge(zeroed, 1)

                def gate_up(g, b):
                    at = FB * (g - GA) + b
                    if (g, b) == (GA + 2, 1):
                        pe.wait_ge(tot_read, 1)
                    elif at > 1:
                        pe.wait_ge(mul_ready, 1 if at == 2 else at)
                    for bank, col in zip(gu_banks(g, b), (b * P, FF + b * P)):
                        for c in range(KB):
                            got = split_products(pe, bank[:, :], (gu_hi[:, c, col:col + P], gu_lo[:, c, col:col + P]),
                                                 (ht_hi[HT_OF[g]][:, c, :], ht_lo[HT_OF[g]][:, c, :]), c == 0, c == KB - 1)
                    got.then_inc(gu_ready, 1)

                def down(g, j):
                    at = 4 * (g - GA) + j
                    if at > 1 and g < GA + 2:
                        pe.wait_ge(y_done, at - 1)
                    pe.wait_ge(ilo_ready, FB * (g - GA) + FB)
                    tok = slice(j * P, (j + 1) * P)
                    for b in range(FB):
                        got = split_products(pe, d_bank(g, j)[:, :], (in_hi[:, b, tok], in_lo[:, b, tok]),
                                             (dn_hi[:, b, :], dn_lo[:, b, :]), b == 0, b == FB - 1)
                    got.then_inc(d_ready, 1)

                gate_up(GA, 0)
                gate_up(GA, 1)
                for j in range(GT):
                    down(GA, j)
                gate_up(GA + 1, 0)
                gate_up(GA + 1, 1)
                pe.wait_ge(mul_ready, 2)
                pe.wait_ge(mask_done, 1)
                for i in range(2):
                    cols = flat(mask)[:, i * 512:(i + 1) * 512]
                    pe.matmul(ps_cum[i][:, :], k.upto_bf[:, :], cols, start=True, stop=True)
                    got = pe.matmul(ps_tot[i][:, :], k.ones_bf[:, :], cols, start=True, stop=True)
                got.then_inc(counted, 1)
                pe.sem_inc(tabbed, HOTS)
                for j in range(GT):
                    down(GA + 1, j)
                gate_up(GA + 2, 0)
                gate_up(GA + 2, 1)
                for j in range(GT):
                    down(GA + 2, j)
                pe.wait_ge(y_done, 4 * 2)

                def body(i, u, first=False, last=False):
                    pe.wait_ge(ida, HOTS * i + u + 1)
                    pe.wait_ge(idt, HOTS * i + u + 1)
                    pe.wait_ge(hotb, HOTS * i + u + 1)
                    if first:
                        pe.matmul(ps_tab[0:SA * EG, :], no_slots[:, :], hot_b[0][:, :, :].rearrange("p s e -> p (s e)"),
                                  start=True, stop=False)
                    for g in range(GE):
                        of_group = lambda t: t[:, g, :, :].rearrange("p s e -> p (s e)")
                        b_of_group = hot_b[u][:, :, g * EG:(g + 1) * EG]
                        out = ps_tab[0:SA * EG, g * EG * SB_:(g + 1) * EG * SB_]
                        pe.matmul(out, of_group(tile_a[u]), b_of_group, start=False, stop=False)
                        got = pe.matmul(out, of_group(part_a[u]), b_of_group, start=False, stop=last and g == GE - 1)
                    got.then_inc(tabbed, 1)

                for u in range(HOTS):
                    body(0, u, first=u == 0)
                with pe.Fori(1, NT // HOTS - 1) as i:
                    for u in range(HOTS):
                        body(i, u)
                for u in range(HOTS):
                    body(NT // HOTS - 1, u, last=u == HOTS - 1)
                pe.wait_ge(tab_done, 1)
                pe.transpose(ps_tab[0:GE * SB_, 0:SA * EG], table2[:, :, :].rearrange("r g b -> r (g b)"),
                             k.ident[0:SA * EG, 0:SA * EG]).then_inc(turned, 1)
                pe.wait_ge(grouped, 1)
                for at in range(SA // 2):
                    got = pe.matmul(ps_cum[0][0:HALF, 0:2 * E], to_slot[:, at, :],
                                    by_group[:, :, :, :].rearrange("p g (h a) e -> p h g a e", h=2)[:, :, :, at, :],
                                    start=at == 0, stop=at == SA // 2 - 1)
                got.then_inc(turned, 1)


def routed_experts(nc, a, k, n, htab, acc, slots, raw, w_loaded, y_stored):
    with ExitStack() as ctx:
        sb = lambda name, shape, dt: ctx.enter_context(nc.sbuf_tensor(f"{name}{n}", shape, dt))
        pb = lambda name: ctx.enter_context(nc.psum_tensor(f"{name}{n}", [P, 512], F32))
        sem = lambda name: own_semaphore(nc, k, f"{name}{n}")
        w_hi = [sb(f"e_w_hi{u}_", [P, WALL], F32R) for u in range(2)]
        w_lo = [sb(f"e_w_lo{u}_", [P, WALL], F32R) for u in range(2)]
        gather_idx = [sb(f"e_gather_idx{u}_", [HALF, 2], U32) for u in range(2)]
        add_idx = [sb(f"e_add_idx{u}_", [HALF, 2], U32) for u in range(2)]
        xg = [[sb(f"e_xg{u}{q}_", [HALF, ROW], F32) for q in range(2)] for u in range(2)]
        xt_hi = [sb(f"e_xt_hi{u}_", [P, KB, CAP], F32R) for u in range(2)]
        xt_lo = [sb(f"e_xt_lo{u}_", [P, KB, CAP], F32R) for u in range(2)]
        wcol = sb("e_wcol", [HALF, 2 * E], F32)
        silu = sb("e_silu", [HALF, 2, FF], F32)
        inter = sb("e_inter", [HALF, 2, FF], F32)
        in_hi = sb("e_in_hi", [P, FB * CAP], F32R)
        in_lo = sb("e_in_lo", [P, FB * CAP], F32R)
        y = [[sb(f"e_y{u}{q}_", [HALF, D], F32) for q in range(2)] for u in range(2)]
        ps_t = [pb(f"e_ps_t{i}_") for i in range(2)]
        ps_gu = [pb(f"e_ps_gu{q}_") for q in range(2)]
        ps_in = pb("e_ps_in")
        ps_down = [pb(f"e_ps_down{q}_") for q in range(2)]
        gathered = [sem(f"e_gathered{u}_") for u in range(2)]
        added, y_free, seen = sem("e_added"), sem("e_y_free"), sem("e_seen_by_gpsimd")
        hi_ready, lo_ready = sem("e_hi_ready"), sem("e_lo_ready")
        t_ready, t_hi, t_lo, col_done = sem("e_t_ready"), sem("e_t_hi"), sem("e_t_lo"), sem("e_col_done")
        gu_ready, silu_ready, mul_ready = sem("e_gu_ready"), sem("e_silu_ready"), sem("e_mul_ready")
        in_turned, ihi_ready, ilo_ready = sem("e_in_turned"), sem("e_ihi_ready"), sem("e_ilo_ready")
        d_ready, y_ready = sem("e_d_ready"), sem("e_y_ready")
        TC = 2 * CAP
        THIRD = WALL // 3

        with nc.Block() as block:

            @block.sync
            def _(sp):
                with sp.Fori(0, E // 2 - 1) as i:
                    for u in range(2):
                        e = 2 * i + u
                        sp.wait_ge(lo_ready, 3 * e + 3)
                        sp.dma_start(raw[u][:, :], a["w_experts"][bass.ds(e + 2, 1), :, :].rearrange("o p c -> p (o c)")).then_inc(w_loaded[u], 16)

            @block.gpsimd
            def _(pool):
                pool.sem_inc(y_free, 2)

                def gather(u):
                    for q in range(2):
                        pool.indirect_dma_start(xg[u][q][:, :], None, htab,
                                                bass.IndirectOffsetOnAxis(ap=gather_idx[u][:, q:q + 1], axis=0)).then_inc(gathered[u], 16)

                def scatter(i, u):
                    e = 2 * i + u
                    pool.wait_ge(y_ready, 2 * e + 2 + 2)
                    pool.sem_inc(seen, 1)
                    for q in range(2):
                        pool.indirect_dma_start(acc, bass.IndirectOffsetOnAxis(ap=add_idx[u][:, q:q + 1], axis=0),
                                                y[u][q][:, :], None, compute_op=ALU.add).then_inc(added, 16)
                    pool.wait_ge(added, 32 * e + 32)
                    pool.sem_inc(y_free, 1)

                def gather_next(i, u):
                    pool.wait_ge(col_done, 2 * i + u + 1)
                    pool.sem_inc(seen, 1)
                    gather(u)

                for u in range(2):
                    pool.tensor_copy(gather_idx[u][:, :], slots[:, 2 * u:2 * u + 2])
                pool.drain()
                gather(0)
                gather(1)
                gather_next(0, 0)
                gather_next(0, 1)
                pool.wait_ge(y_stored[0], 16 * 2)
                pool.wait_ge(y_stored[1], 16)
                with pool.Fori(1, E // 2 - 1) as i:
                    for u in range(2):
                        gather_next(i, u)
                        scatter(i - 1, u)
                for i in (E // 2 - 2, E // 2 - 1):
                    for u in range(2):
                        scatter(i, u)

            @block.scalar
            def _(act):
                act.sem_inc(y_ready, 2)

                def split(i, u, thirds):
                    act.wait_ge(w_loaded[u], 16 * i + 16)
                    for c in thirds:
                        cols = slice(c * THIRD, (c + 1) * THIRD)
                        act.activation(w_hi[u][:, cols], raw[u][:, cols], ACT.Copy).then_inc(hi_ready, 1)

                def turn(i, u):
                    e = 2 * i + u
                    for c in range(2):
                        act.wait_ge(t_ready, 2 * e + c + 1)
                        act.activation(xt_hi[u][:, 2 * c:2 * c + 2, :].rearrange("p k s -> p (k s)"),
                                       ps_t[c][:, 0:TC], ACT.Copy).then_inc(t_hi, 1)

                def gate(i, u):
                    e = 2 * i + u
                    for q in range(2):
                        act.wait_ge(gu_ready, 2 * e + q + 1)
                        act.activation(silu[:, q, :], ps_gu[q][0:HALF, 0:FF], ACT.Silu).then_inc(silu_ready, 1)

                def turn_inner(i, u):
                    act.wait_ge(in_turned, 2 * i + u + 1)
                    act.activation(in_hi[:, :], ps_in[:, 0:FB * CAP], ACT.Copy).then_inc(ihi_ready, 1)

                def weigh(i, u):
                    e = 2 * i + u
                    act.wait_ge(y_free, e + 1)
                    act.wait_ge(col_done, e + 1)
                    act.activation(add_idx[u][:, :], slots[:, bass.ds(2 * e, 2)], ACT.Copy)
                    for q in range(2):
                        act.wait_ge(d_ready, 2 * e + q + 1)
                        act.activation(y[u][q][:, :], ps_down[q][0:HALF, :], ACT.Copy,
                                       scale=wcol[:, bass.ds(2 * e + q, 1)]).then_inc(y_ready, 1)

                def step(i, u, ahead=True, behind=True):
                    ni, nu = (i, 1) if u == 0 else (i + 1, 0)
                    pi = i if u == 1 else i - 1
                    if behind:
                        turn_inner(pi, nu)
                    if ahead:
                        turn(ni, nu)
                        split(ni, nu, (0, 1))
                    gate(i, u)
                    if behind:
                        weigh(pi, nu)
                    if ahead:
                        split(ni, nu, (2,))

                split(0, 0, (0, 1))
                turn(0, 0)
                split(0, 0, (2,))
                step(0, 0, behind=False)
                with act.Fori(0, E // 2 - 1) as i:
                    step(i, 1)
                    step(i + 1, 0)
                step(E // 2 - 1, 1, ahead=False)
                turn_inner(E // 2 - 1, 1)
                weigh(E // 2 - 1, 1)

            @block.vector
            def _(dve):
                dve.sem_inc(t_lo, 2)
                dve.sem_inc(mul_ready, 2)
                dve.sem_inc(ilo_ready, 1)

                def split(i, u, thirds):
                    e = 2 * i + u
                    for c in thirds:
                        cols = slice(c * THIRD, (c + 1) * THIRD)
                        dve.wait_ge(hi_ready, 3 * e + c + 1)
                        dve.tensor_tensor(w_lo[u][:, cols], raw[u][:, cols], w_hi[u][:, cols].bitcast(F32),
                                          ALU.subtract).then_inc(lo_ready, 1)

                def turn(i, u):
                    e = 2 * i + u
                    for c in range(2):
                        dve.wait_ge(t_hi, 2 * e + c + 1)
                        dve.tensor_tensor(xt_lo[u][:, 2 * c:2 * c + 2, :].rearrange("p k s -> p (k s)"), ps_t[c][:, 0:TC],
                                          xt_hi[u][:, 2 * c:2 * c + 2, :].rearrange("p k s -> p (k s)").bitcast(F32),
                                          ALU.subtract).then_inc(t_lo, 1)
                    for q in range(2):
                        dve.tensor_scalar(wcol[:, bass.ds(2 * e + q, 1)], xg[u][q][:, bass.ds(D + e, 1)],
                                                1.0, None, ALU.mult)
                    dve.tensor_copy(gather_idx[u][:, :], slots[:, bass.ds(2 * e + 4, 2)]).then_inc(col_done, 1)

                def gate(i, u):
                    e = 2 * i + u
                    for q in range(2):
                        dve.wait_ge(silu_ready, 2 * e + q + 1)
                        dve.tensor_tensor(inter[:, q, :], silu[:, q, :], ps_gu[q][0:HALF, FF:2 * FF],
                                          ALU.mult).then_inc(mul_ready, 1)

                def turn_inner(i, u):
                    dve.wait_ge(ihi_ready, 2 * i + u + 1)
                    dve.tensor_tensor(in_lo[:, :], ps_in[:, 0:FB * CAP], in_hi[:, :].bitcast(F32),
                                      ALU.subtract).then_inc(ilo_ready, 1)

                def step(i, u, ahead=True, behind=True):
                    ni, nu = (i, 1) if u == 0 else (i + 1, 0)
                    if behind:
                        turn_inner(i if u == 1 else i - 1, nu)
                    if ahead:
                        turn(ni, nu)
                        split(ni, nu, (0, 1))
                    gate(i, u)
                    if ahead:
                        split(ni, nu, (2,))

                split(0, 0, (0, 1))
                turn(0, 0)
                split(0, 0, (2,))
                step(0, 0, behind=False)
                with dve.Fori(0, E // 2 - 1) as i:
                    step(i, 1)
                    step(i + 1, 0)
                step(E // 2 - 1, 1, ahead=False)
                turn_inner(E // 2 - 1, 1)

            @block.tensor
            def _(pe):
                def turn(i, u):
                    e = 2 * i + u
                    pe.wait_ge(gathered[u], 32 * i + 32)
                    for c in range(2):
                        pe.wait_ge(t_lo, 2 * e + c + 1)
                        for b in range(2):
                            for q in range(2):
                                at = b * CAP + q * HALF
                                got = pe.transpose(ps_t[c][:, at:at + HALF],
                                                   xg[u][q][:, (2 * c + b) * P:(2 * c + b + 1) * P],
                                                   k.ident[0:HALF, 0:HALF])
                        got.then_inc(t_ready, 1)

                def gate_up(i, u):
                    e = 2 * i + u
                    w = [t[u][:, 0:WGU].rearrange("p (k c) -> p k c", k=KB) for t in (w_hi, w_lo)]
                    pe.wait_ge(t_lo, 2 * e + 2 + 2)
                    pe.wait_ge(lo_ready, 3 * e + 2)
                    for q in range(2):
                        pe.wait_ge(mul_ready, 2 * e + q + 1)
                        s = slice(q * HALF, (q + 1) * HALF)
                        for c in range(KB):
                            got = split_products(pe, ps_gu[q][0:HALF, :], (xt_hi[u][:, c, s], xt_lo[u][:, c, s]),
                                                 (w[0][:, c, :], w[1][:, c, :]), c == 0, c == KB - 1)
                        got.then_inc(gu_ready, 1)

                def turn_inner(i, u):
                    e = 2 * i + u
                    pe.wait_ge(mul_ready, 2 * e + 2 + 2)
                    pe.wait_ge(ilo_ready, e + 1)
                    for b in range(FB):
                        for q in range(2):
                            at = b * CAP + q * HALF
                            got = pe.transpose(ps_in[:, at:at + HALF], inter[:, q, b * P:(b + 1) * P],
                                               k.ident[0:HALF, 0:HALF])
                    got.then_inc(in_turned, 1)

                def down(i, u):
                    e = 2 * i + u
                    w = [t[u][:, WGU:].rearrange("p (k c) -> p k c", k=FB) for t in (w_hi, w_lo)]
                    pe.wait_ge(lo_ready, 3 * e + 3)
                    pe.wait_ge(ilo_ready, e + 1 + 1)
                    for q in range(2):
                        pe.wait_ge(y_ready, 2 * e + q + 1)
                        for b in range(FB):
                            s = slice(b * CAP + q * HALF, b * CAP + (q + 1) * HALF)
                            got = split_products(pe, ps_down[q][0:HALF, :], (in_hi[:, s], in_lo[:, s]),
                                                 (w[0][:, b, :], w[1][:, b, :]), b == 0, b == FB - 1)
                        got.then_inc(d_ready, 1)

                turn(0, 0)
                turn(0, 1)
                gate_up(0, 0)
                with pe.Fori(0, E // 2 - 1) as i:
                    for u in range(2):
                        turn_inner(i, u)
                        turn(i + 1, u)
                        gate_up(i if u == 0 else i + 1, 1 - u)
                        down(i, u)
                turn_inner(E // 2 - 1, 0)
                gate_up(E // 2 - 1, 1)
                down(E // 2 - 1, 0)
                turn_inner(E // 2 - 1, 1)
                down(E // 2 - 1, 1)


def attention(nc, a, k, src, dst):
    softmax_scale = DH ** -0.5
    HK = H + 1
    half = DH // 2
    with ExitStack() as ctx:
        sb = lambda name, shape, dt: ctx.enter_context(nc.sbuf_tensor(name, shape, dt))
        sem = lambda name: ctx.enter_context(nc.semaphore(name))
        cos = sb("a_cos", [P, NQ, half], F32)
        sin = sb("a_sin", [P, NQ, DH], F32)
        gains = sb("a_gains", [P, HK, DH], F32)
        qt = [sb(f"a_qt_{part}", [P, H, SEQ], F32R) for part in ("hi", "lo")]
        kt_ = [sb(f"a_kt_{part}", [P, SEQ], F32R) for part in ("hi", "lo")]
        v = [sb(f"a_v_{part}", [P, NQ, DH], F32R) for part in ("hi", "lo")]
        q_scale = sb("a_q_scale", [P, NQ, H], F32)
        x = [sb(f"q_x{u}", [P, D], F32) for u in range(2)]
        h = [sb(f"q_h{u}", [P, D], F32) for u in range(2)]
        stats = [sb(f"q_stats{u}", [P, 6], F32) for u in range(2)]
        mv = [sb(f"q_mv{u}", [P, 2], F32) for u in range(2)]
        std = [sb(f"q_std{u}", [P, 1], F32) for u in range(2)]
        rstd = [sb(f"q_rstd{u}", [P, 1], F32) for u in range(2)]
        ht = [[sb(f"q_ht{part}{u}", [P, KB, P], F32R) for u in range(2)] for part in range(2)]
        raw = sb("q_raw", [P, HK, DH], F32)
        sum_sq = sb("q_sum_sq", [P, HK], F32)
        rms = [sb(f"q_rms{u}", [P, HK], F32) for u in range(2)]
        inv_rms = sb("q_inv_rms", [P, HK], F32)
        gained = sb("q_gained", [P, HK, DH], F32)
        by_cos = sb("q_by_cos", [P, HK, DH], F32)
        by_sin = sb("q_by_sin", [P, HK, DH], F32)
        rot = [sb(f"q_rot{u}", [P, HK, DH], F32) for u in range(2)]
        res = [sb(f"t_res{u}", [P, D], F32) for u in range(2)]
        top, neg_max, total, inv = (sb(f"t_{name}", [P, 2 * H], F32) for name in ("top", "neg_max", "total", "inv"))
        prob = sb("t_prob", [P, RING, SEQ], F32)
        pt = [[sb(f"t_pt{part}{r}", [P, H * P], F32R) for r in range(2)] for part in range(2)]
        ot = [sb(f"t_ot{part}", [P, H * P], F32R) for part in range(2)]
        wide = [ctx.enter_context(nc.psum_tensor(f"a_wide{i}", [P, SEQ], F32)) for i in range(2)]
        bank = [ctx.enter_context(nc.psum_tensor(f"a_bank{i}", [P, 512], F32)) for i in range(4)]
        ps_t = [wide[0][:, 0:512], wide[0][:, 512:1024]]
        ps_q = [wide[1][:, 0:512], bank[0][:, :]]
        ps_kv = [wide[1][:, 512:1024], bank[1][:, :]]
        ps_qt, ps_kt = bank[2][:, :], bank[3][:, :]
        ps_s, ps_p, ps_o, ps_y = wide, [bank[0][:, :], bank[1][:, :]], bank[2][:, :], bank[3][:, :]

        loaded, seen = sem("a_loaded"), sem("a_seen_by_gpsimd")
        x_loaded = [sem(f"a_x_loaded{u}") for u in range(2)]
        stats_ready, std_ready, h_ready = sem("a_stats"), sem("a_std_ready"), sem("a_h_ready")
        t_ready, t_hi, t_lo = sem("a_t_ready"), sem("a_t_hi"), sem("a_t_lo")
        proj_ready, raw_ready, rms_ready = sem("a_proj_ready"), sem("a_raw_ready"), sem("a_rms_ready")
        gained_ready, sin_ready = sem("a_gained_ready"), sem("a_sin_ready")
        rot_ready, qk_turned, qk_hi, qk_lo = sem("a_rot_ready"), sem("a_qk_turned"), sem("a_qk_hi"), sem("a_qk_lo")
        s_ready, m_ready, exp_ready = sem("a_s_ready"), sem("a_m_ready"), sem("a_exp_ready")
        inv_ready, p_ready = sem("a_inv_ready"), sem("a_p_ready")
        p_turned, p_hi, p_lo = sem("a_p_turned"), sem("a_p_hi"), sem("a_p_lo")
        o_ready, o_hi, o_lo = sem("a_o_ready"), sem("a_o_hi"), sem("a_o_lo")
        out_ready, y_done = sem("a_out_ready"), sem("a_y_done")
        r_loaded = [sem(f"a_r_loaded{u}") for u in range(2)]
        y_stored = [sem(f"a_y_stored{u}") for u in range(2)]
        nc.clear_and_free_semaphores(k.ffn_semaphores)
        k.ffn_semaphores = []

        keys = lambda s: s + 1
        base = [s * (s + 1) // 2 for s in range(NQ)]
        width = lambda i: keys(i // H) * P
        quarter = lambda s, m: range(keys(s) * m // H, keys(s) * (m + 1) // H)
        tiles0, heads0, blocks0 = (lambda b: b * NQ), (lambda b: b * HEADS), (lambda b: b * (NQ * (NQ + 1) // 2))

        def over_batches(engine, prepare, body):
            prepare(0)
            with engine.Fori(0, B - 2) as b:
                body(b, True)
            body(B - 2, True)
            body(B - 1, False)

        with nc.Block() as block:

            @block.sync
            def _(sp):
                for t, name in ((cos, "cos"), (sin, "sin"), (gains, "gains")):
                    sp.dma_start(t[:, :, :], a[name]).then_inc(loaded, 16)
                for u in range(2):
                    sp.sem_inc(y_stored[u], 16)

                def load_x(b, j, wait=True):
                    row = sp.snap(b * SEQ + j * P)
                    if wait:
                        sp.wait_ge(h_ready, tiles0(b) + j - 1)
                    sp.dma_start(x[j % 2][:, :], src[bass.ds(row, P), :]).then_inc(x_loaded[j % 2], 16)

                def load_res(b, s):
                    row = sp.snap(b * SEQ + s * P)
                    sp.wait_ge(y_stored[s % 2], b * 16 * (NQ // 2) + 16 * (s // 2) + 16)
                    sp.dma_start(res[s % 2][:, :], src[bass.ds(row, P), :]).then_inc(r_loaded[s % 2], 16)

                def store(b, s):
                    row = sp.snap(b * SEQ + s * P)
                    sp.wait_ge(y_done, tiles0(b) + s + 1 + 1)
                    sp.dma_start(dst[bass.ds(row, P), :], res[s % 2][:, :]).then_inc(y_stored[s % 2], 16)

                def prepare(b):
                    load_x(b, 0, wait=False)
                    load_x(b, 1, wait=False)
                    load_x(b, 2)
                    load_x(b, 3)

                def body(b, ahead):
                    for j in range(4, NQ):
                        load_x(b, j)
                    load_res(b, 0)
                    load_res(b, 1)
                    for s in range(NQ):
                        store(b, s)
                        if s + 2 < NQ:
                            load_res(b, s + 2)
                        if ahead and s == 4:
                            load_x(b + 1, 0)
                            load_x(b + 1, 1)
                        if ahead and s == NQ - 2:
                            load_x(b + 1, 2)
                            load_x(b + 1, 3)

                over_batches(sp, prepare, body)
                for u in range(2):
                    sp.wait_ge(y_stored[u], 16 * (B * NQ // 2 + 1))

            @block.scalar
            def _(act):
                act.sem_inc(exp_ready, 2)

                def root(b, j):
                    act.wait_ge(stats_ready, tiles0(b) + j + 1)
                    act.activation(std[j % 2][:, :], mv[j % 2][:, 1:2], ACT.Sqrt, bias=k.ln_eps[:, :]).then_inc(std_ready, 1)

                def turn(b, j):
                    act.wait_ge(t_ready, tiles0(b) + j + 1)
                    act.activation(ht[0][j % 2][:, :, :].rearrange("p k t -> p (k t)"), ps_t[j % 2],
                                   ACT.Copy).then_inc(t_hi, 1)

                def unload(b, j):
                    act.wait_ge(proj_ready, tiles0(b) + j + 1)
                    act.activation(v[0][:, j, :], ps_kv[j % 2][:, DH:2 * DH], ACT.Copy)
                    act.wait_ge(gained_ready, tiles0(b) + j + 1)
                    act.activation(raw[:, 0:H, :].rearrange("p m d -> p (m d)"), ps_q[j % 2], ACT.Copy)
                    act.activation(raw[:, H, :], ps_kv[j % 2][:, 0:DH], ACT.Copy).then_inc(raw_ready, 1)

                def mean_square(j):
                    act.drain()
                    for m in range(HK):
                        act.activation(rot[j % 2][:, m, :], raw[:, m, :], ACT.Square, accum_out=sum_sq[:, m:m + 1])
                    act.drain()
                    act.activation(rms[j % 2][:, :], sum_sq[:, :], ACT.Sqrt, scale=1.0 / DH,
                                   bias=k.rms_eps[:, :]).then_inc(rms_ready, 1)

                def turn_qk(b, j):
                    act.wait_ge(qk_turned, tiles0(b) + j + 1)
                    tok = slice(j * P, (j + 1) * P)
                    act.activation(qt[0][:, :, tok], ps_qt.rearrange("p (m t) -> p m t", m=H), ACT.Copy)
                    act.activation(kt_[0][:, tok], ps_kt[:, 0:P], ACT.Copy).then_inc(qk_hi, 1)

                def soften(b, i):
                    u = i % (2 * H)
                    act.wait_ge(m_ready, heads0(b) + i + 1)
                    act.activation(prob[:, i % RING, 0:width(i)], ps_s[i % 2][:, 0:width(i)], ACT.Exp,
                                   scale=q_scale[:, i // H, i % H:i % H + 1], bias=neg_max[:, u:u + 1],
                                   accum_out=total[:, u:u + 1]).then_inc(exp_ready, 1)

                def turn_prob(b, s, c):
                    at = base[s] + c
                    act.wait_ge(p_turned, blocks0(b) + at + 1)
                    act.activation(pt[0][at % 2][:, :], ps_p[at % 2], ACT.Copy).then_inc(p_hi, 1)

                def collect(b, s):
                    act.wait_ge(o_ready, tiles0(b) + s + 1)
                    act.activation(ot[0][:, :], ps_o, ACT.Copy).then_inc(o_hi, 1)

                def prepare(b):
                    root(b, 0)
                    root(b, 1)
                    turn(b, 0)
                    turn(b, 1)
                    root(b, 2)

                def body(b, ahead):
                    for j in range(1, NQ + 1):
                        unload(b, j - 1)
                        if j + 1 < NQ:
                            turn(b, j + 1)
                        if j >= 3:
                            turn_qk(b, j - 3)
                        if j + 2 < NQ:
                            root(b, j + 2)
                        mean_square(j - 1)
                    soften(b, 0)
                    soften(b, 1)
                    turn_qk(b, NQ - 2)
                    soften(b, 2)
                    soften(b, 3)
                    turn_qk(b, NQ - 1)
                    soften(b, 4)
                    for s in range(NQ):
                        if s:
                            collect(b, s - 1)
                        for m in range(H):
                            for c in quarter(s, m):
                                turn_prob(b, s, c)
                            if s * H + m + EXP_AHEAD < HEADS:
                                soften(b, s * H + m + EXP_AHEAD)
                            if ahead and s == NQ - 1 and m in (0, 1):
                                root(b + 1, m)
                    if ahead:
                        turn(b + 1, 0)
                        turn(b + 1, 1)
                    collect(b, NQ - 1)
                    if ahead:
                        root(b + 1, 2)

                over_batches(act, prepare, body)

            @block.vector
            def _(dve):
                dve.sem_inc(t_lo, 2)
                dve.sem_inc(rot_ready, 2)
                dve.sem_inc(qk_lo, 1)
                dve.sem_inc(p_lo, 2)
                dve.sem_inc(o_lo, 1)
                dve.sem_inc(y_done, 1)

                def take_stats(b, j):
                    dve.wait_ge(x_loaded[j % 2], b * 16 * (NQ // 2) + 16 * (j // 2) + 16)
                    dve.bn_stats(stats[j % 2][:, :], x[j % 2][:, :])

                def add_stats(j):
                    dve.bn_aggr(mv[j % 2][:, :], stats[j % 2][:, :]).then_inc(stats_ready, 1)

                def invert_std(b, j):
                    dve.wait_ge(std_ready, tiles0(b) + j + 1)
                    dve.reciprocal(rstd[j % 2][:, :], std[j % 2][:, :])

                def normalise(j):
                    dve.tensor_scalar(h[j % 2][:, :], x[j % 2][:, :], mv[j % 2][:, 0:1], rstd[j % 2][:, :],
                                      ALU.subtract, ALU.mult).then_inc(h_ready, 1)

                def turn(b, j):
                    dve.wait_ge(t_hi, tiles0(b) + j + 1)
                    dve.tensor_tensor(ht[1][j % 2][:, :, :].rearrange("p k t -> p (k t)"), ps_t[j % 2],
                                      ht[0][j % 2][:, :, :].rearrange("p k t -> p (k t)").bitcast(F32),
                                      ALU.subtract).then_inc(t_lo, 1)

                def turn_qk(b, j):
                    dve.wait_ge(qk_hi, tiles0(b) + j + 1)
                    tok = slice(j * P, (j + 1) * P)
                    dve.tensor_tensor(qt[1][:, :, tok], ps_qt.rearrange("p (m t) -> p m t", m=H),
                                      qt[0][:, :, tok].bitcast(F32), ALU.subtract)
                    dve.tensor_tensor(kt_[1][:, tok], ps_kt[:, 0:P], kt_[0][:, tok].bitcast(F32),
                                      ALU.subtract).then_inc(qk_lo, 1)

                def window(b, w):
                    j = w - 1
                    if w + 2 < NQ:
                        take_stats(b, w + 2)
                    dve.wait_ge(raw_ready, tiles0(b) + j + 1)
                    dve.tensor_tensor(v[1][:, j, :], ps_kv[j % 2][:, DH:2 * DH], v[0][:, j, :].bitcast(F32), ALU.subtract)
                    if w + 1 < NQ:
                        turn(b, w + 1)
                    if w + 2 < NQ:
                        dve.drain()
                        add_stats(w + 2)
                    if w >= 3:
                        turn_qk(b, w - 3)
                    dve.wait_ge(gained_ready, tiles0(b) + j + 1 + 1)
                    by_half = lambda t, m: t[:, :, :].rearrange("p m (s d) -> p m s d", s=2)[:, :, m, :]
                    for m in range(2):
                        dve.tensor_tensor(by_half(by_cos, m), by_half(gained, m),
                                          cos[:, j:j + 1, :].to_broadcast([P, HK, half]), ALU.mult)
                    if w + 2 < NQ:
                        invert_std(b, w + 2)
                        dve.drain()
                        normalise(w + 2)
                    dve.wait_ge(rms_ready, tiles0(b) + j + 1)
                    dve.reciprocal(inv_rms[:, :], rms[j % 2][:, :])
                    dve.drain()
                    dve.tensor_scalar(q_scale[:, j, :], inv_rms[:, 0:H], softmax_scale, None, ALU.mult)
                    if w == NQ:
                        maximum(b, 0)
                        maximum(b, 1)
                    dve.wait_ge(sin_ready, tiles0(b) + j + 1)
                    dve.tensor_tensor(by_cos[:, H, :], by_cos[:, H, :], by_sin[:, H, :], ALU.add)
                    dve.tensor_tensor(rot[j % 2][:, 0:H, :], by_cos[:, 0:H, :], by_sin[:, 0:H, :], ALU.add)
                    dve.drain()
                    dve.tensor_scalar(rot[j % 2][:, H, :], by_cos[:, H, :], inv_rms[:, H:HK], None,
                                      ALU.mult).then_inc(rot_ready, 1)

                def maximum(b, i):
                    u = i % (2 * H)
                    dve.wait_ge(s_ready, heads0(b) + i + 1)
                    dve.reduce_max(top[:, u:u + 1], ps_s[i % 2][:, 0:width(i)], AX.X)
                    dve.drain()
                    dve.tensor_scalar(neg_max[:, u:u + 1], top[:, u:u + 1], q_scale[:, i // H, i % H:i % H + 1],
                                      -1.0, ALU.mult, ALU.mult).then_inc(m_ready, 1)

                def invert(b, i):
                    u = i % (2 * H)
                    dve.wait_ge(exp_ready, heads0(b) + i + 1 + 2)
                    dve.reciprocal(inv[:, u:u + 1], total[:, u:u + 1]).then_inc(inv_ready, 1)

                def turn_prob(b, s, c):
                    at = base[s] + c
                    dve.wait_ge(p_hi, blocks0(b) + at + 1)
                    dve.tensor_tensor(pt[1][at % 2][:, :], ps_p[at % 2], pt[0][at % 2][:, :].bitcast(F32),
                                      ALU.subtract).then_inc(p_lo, 1)

                def collect(b, s):
                    dve.wait_ge(o_hi, tiles0(b) + s + 1)
                    dve.tensor_tensor(ot[1][:, :], ps_o, ot[0][:, :].bitcast(F32), ALU.subtract).then_inc(o_lo, 1)

                def add_residual(b, s):
                    u = s % 2
                    dve.wait_ge(r_loaded[u], b * 16 * (NQ // 2) + 16 * (s // 2) + 16)
                    dve.wait_ge(out_ready, tiles0(b) + s + 1)
                    dve.tensor_tensor(res[u][:, :], ps_y, res[u][:, :], ALU.add).then_inc(y_done, 1)

                def first_stats(b):
                    take_stats(b, 0)
                    take_stats(b, 1)
                    dve.drain()
                    add_stats(0)
                    add_stats(1)

                def first_roots(b):
                    invert_std(b, 0)
                    invert_std(b, 1)
                    dve.drain()
                    normalise(0)
                    normalise(1)

                def first_turns(b):
                    turn(b, 0)
                    turn(b, 1)
                    take_stats(b, 2)
                    dve.drain()
                    add_stats(2)

                def third_tile(b):
                    invert_std(b, 2)
                    dve.drain()
                    normalise(2)

                def prepare(b):
                    first_stats(b)
                    first_roots(b)
                    first_turns(b)
                    third_tile(b)
                    dve.wait_ge(loaded, 16 * 3)

                def body(b, ahead):
                    for w in range(1, NQ + 1):
                        window(b, w)
                    invert(b, 0)
                    turn_qk(b, NQ - 2)
                    maximum(b, 2)
                    invert(b, 1)
                    maximum(b, 3)
                    invert(b, 2)
                    turn_qk(b, NQ - 1)
                    maximum(b, 4)
                    invert(b, 3)
                    for s in range(NQ):
                        if s:
                            collect(b, s - 1)
                        for m in range(H):
                            i = s * H + m + EXP_AHEAD
                            if i < HEADS:
                                maximum(b, i)
                            for c in quarter(s, m):
                                turn_prob(b, s, c)
                            if i - 1 < HEADS:
                                invert(b, i - 1)
                            if s and m == 1:
                                add_residual(b, s - 1)
                            if ahead and s == NQ - 1 and m in (0, 1):
                                (first_stats, first_roots)[m](b + 1)
                    if ahead:
                        first_turns(b + 1)
                    collect(b, NQ - 1)
                    if ahead:
                        third_tile(b + 1)
                    add_residual(b, NQ - 1)

                over_batches(dve, prepare, body)

            @block.gpsimd
            def _(pool):
                pool.sem_inc(gained_ready, 1)

                def rotate(b, j):
                    pool.wait_ge(rot_ready, tiles0(b) + j + 2)
                    pool.wait_ge(raw_ready, tiles0(b) + j + 1)
                    pool.sem_inc(seen, 1)
                    pool.tensor_tensor(gained[:, :, :], raw[:, :, :], gains[:, :, :], ALU.mult).then_inc(gained_ready, 1)
                    pool.drain()
                    for m in range(2):
                        one, other = slice(m * half, (m + 1) * half), slice((1 - m) * half, (2 - m) * half)
                        got = pool.tensor_tensor(by_sin[:, :, one], gained[:, :, other],
                                                 sin[:, j:j + 1, one].to_broadcast([P, HK, half]), ALU.mult)
                    got.then_inc(sin_ready, 1)

                def prepare(b):
                    pool.wait_ge(loaded, 16 * 3)

                def body(b, ahead):
                    for w in range(1, NQ + 1):
                        rotate(b, w - 1)
                    for i in range(HEADS):
                        u = i % (2 * H)
                        pool.wait_ge(inv_ready, heads0(b) + i + 1)
                        pool.sem_inc(seen, 1)
                        pool.tensor_scalar(prob[:, i % RING, 0:width(i)], prob[:, i % RING, 0:width(i)], inv[:, u:u + 1],
                                           1.0, ALU.mult, ALU.mult).then_inc(p_ready, 1)
                over_batches(pool, prepare, body)

            @block.tensor
            def _(pe):
                def turn(b, j):
                    pe.wait_ge(h_ready, tiles0(b) + j + 1)
                    for c in range(KB):
                        got = pe.transpose(ps_t[j % 2][:, c * P:(c + 1) * P], h[j % 2][:, c * P:(c + 1) * P], k.ident[:, :])
                    got.then_inc(t_ready, 1)

                def project(b, j):
                    u = j % 2
                    pe.wait_ge(t_lo, tiles0(b) + j + 1 + 2)
                    pe.wait_ge(rot_ready, tiles0(b) + j + 1)
                    for bank_, at, n in ((ps_kv[u], H * DH, 2 * DH), (ps_q[u], 0, H * DH)):
                        for c in range(KB):
                            got = split_products(pe, bank_[:, 0:n], (ht[0][u][:, c, :], ht[1][u][:, c, :]),
                                                 (k.wqkv_hi[:, c, at:at + n], k.wqkv_lo[:, c, at:at + n]),
                                                 c == 0, c == KB - 1)
                    got.then_inc(proj_ready, 1)

                def turn_qk(b, j):
                    u = j % 2
                    pe.wait_ge(rot_ready, tiles0(b) + j + 1 + 2)
                    pe.wait_ge(qk_lo, tiles0(b) + j + 1)
                    if j == 0:
                        pe.wait_ge(y_done, tiles0(b) + 1)
                    for m in range(H):
                        pe.transpose(ps_qt[:, m * P:(m + 1) * P], rot[u][:, m, :], k.ident[:, :])
                    pe.transpose(ps_kt[:, 0:P], rot[u][:, H, :], k.ident[:, :]).then_inc(qk_turned, 1)

                def scores(b, i):
                    m, s = i % H, i // H
                    if m == 0:
                        pe.wait_ge(qk_lo, tiles0(b) + s + 1 + 1)
                    pe.wait_ge(exp_ready, heads0(b) + i + 1)
                    tok = slice(s * P, (s + 1) * P)
                    qh, ql = (t[:, m, tok] for t in qt)
                    for at in range(0, width(i), 512):
                        cols = slice(at, min(at + 512, width(i)))
                        out = ps_s[i % 2][:, cols]
                        pe.matmul(out, qh, kt_[0][:, cols], start=True, stop=False)
                        if cols.stop == width(i):
                            pe.matmul(ps_s[i % 2][:, tok], k.ident_bf[:, :], k.causal_bf[:, :], start=False, stop=False)
                        pe.matmul(out, qh, kt_[1][:, cols], start=False, stop=False)
                        got = pe.matmul(out, ql, kt_[0][:, cols], start=False, stop=True)
                    got.then_inc(s_ready, 1)

                def turn_prob(b, s, c):
                    at = base[s] + c
                    if c == 0:
                        pe.wait_ge(p_ready, heads0(b) + H * (s + 1))
                    pe.wait_ge(p_lo, blocks0(b) + at + 1)
                    for m in range(H):
                        got = pe.transpose(ps_p[at % 2][:, m * P:(m + 1) * P],
                                           prob[:, (H * s + m) % RING, c * P:(c + 1) * P], k.ident[:, :])
                    got.then_inc(p_turned, 1)

                def values(b, s, c):
                    at = base[s] + c
                    if c == 0:
                        pe.wait_ge(o_lo, tiles0(b) + s + 1)
                    pe.wait_ge(p_lo, blocks0(b) + at + 1 + 2)
                    got = split_products(pe, ps_o, (v[0][:, c, :], v[1][:, c, :]),
                                         (pt[0][at % 2][:, :], pt[1][at % 2][:, :]), c == 0, c == keys(s) - 1)
                    if c == keys(s) - 1:
                        got.then_inc(o_ready, 1)

                def output(b, s):
                    pe.wait_ge(o_lo, tiles0(b) + s + 1 + 1)
                    pe.wait_ge(y_done, tiles0(b) + s + 1)
                    for m in range(H):
                        tok = slice(m * P, (m + 1) * P)
                        got = split_products(pe, ps_y, (ot[0][:, tok], ot[1][:, tok]),
                                             (k.wo_hi[:, m, :], k.wo_lo[:, m, :]), m == 0, m == H - 1)
                    got.then_inc(out_ready, 1)

                def prepare(b):
                    turn(b, 0)
                    turn(b, 1)
                    project(b, 0)

                def body(b, ahead):
                    turn(b, 2)
                    for j in range(1, NQ):
                        project(b, j)
                        if j >= 2:
                            turn_qk(b, j - 2)
                        if j + 2 < NQ:
                            turn(b, j + 2)
                    scores(b, 0)
                    scores(b, 1)
                    turn_qk(b, NQ - 2)
                    scores(b, 2)
                    scores(b, 3)
                    turn_qk(b, NQ - 1)
                    scores(b, 4)
                    pe.wait_ge(qk_lo, tiles0(b) + NQ + 1)
                    scores(b, 5)
                    for s in range(NQ):
                        for m in range(H):
                            blocks, behind = quarter(s, m), s in BEHIND
                            for c in blocks[0:1] if behind else blocks:
                                turn_prob(b, s, c)
                            if s * H + m + SCORES_AHEAD < HEADS:
                                scores(b, s * H + m + SCORES_AHEAD)
                            if s and m == 0:
                                output(b, s - 1)
                            if ahead and s == NQ - 1 and m == H - 1:
                                pe.wait_ge(exp_ready, heads0(b) + HEADS + 2)
                                turn(b + 1, 0)
                                turn(b + 1, 1)
                            for c in blocks:
                                if not behind:
                                    values(b, s, c)
                                    continue
                                if c > blocks[0]:
                                    turn_prob(b, s, c)
                                if c:
                                    values(b, s, c - 1)
                        if s in BEHIND:
                            values(b, s, keys(s) - 1)
                    if ahead:
                        project(b + 1, 0)
                    output(b, NQ - 1)

                over_batches(pe, prepare, body)


def staged_buffers(nc, places, n):
    part = KB * GTOK * 4
    ht_hi, ht_lo, raw = [], [], []
    for u in range(2):
        at = (nc.sbuf_base + 31) // 32 * 32
        places.enter_context(nc.sbuf_tensor(f"place{u}_{n}", [P, 2 * KB * GTOK], F32))
        ht_hi.append(nc.alloc_sbuf_tensor_at(f"ht_hi{u}_{n}", [P, KB, GTOK], F32R, offset=at))
        ht_lo.append(nc.alloc_sbuf_tensor_at(f"ht_lo{u}_{n}", [P, KB, GTOK], F32R, offset=at + part))
        raw.append(nc.alloc_sbuf_tensor_at(f"e_raw{u}_{n}", [P, WALL], F32, offset=at))
    return ht_hi, ht_lo, raw


def build_program(nc, a, out):
    with ExitStack() as ctx:
        k = allocate_kept(nc, ctx)
        htab = nc.dram_tensor("htab", [ROWS, ROW], F32).ap()
        x1 = nc.dram_tensor("x_after_ffn", [ROWS, D], F32).ap()
        x2 = nc.dram_tensor("x_after_attention", [TOK, D], F32).ap()
        setup(nc, a, k, htab, (x1, out))

        def ffn(n, src, acc):
            with nc.sbuf_tensor(f"slots{n}", [HALF, 2 * E + 4], U32) as slots, ExitStack() as places:
                ht_hi, ht_lo, raw = staged_buffers(nc, places, n)
                w_loaded = [own_semaphore(nc, k, f"e_w_loaded{u}_{n}") for u in range(2)]
                y_stored = [own_semaphore(nc, k, f"r_y_stored{u}_{n}") for u in range(2)]
                with ExitStack() as shared:
                    sb = lambda name, shape, dt: shared.enter_context(nc.sbuf_tensor(f"{name}{n}", shape, dt))
                    logits = sb("logits", [P, NT, 2 * E], F32)
                    ht_hi.append(sb("ht_hi2_", [P, KB, GTOK], F32R))
                    ht_lo.append(sb("ht_lo2_", [P, KB, GTOK], F32R))
                    dense_ffn(nc, a, k, n, src, acc, htab, logits, ht_hi, ht_lo)
                    route(nc, a, k, n, src, acc, htab, logits, ht_hi, ht_lo, slots, raw, w_loaded, y_stored)
                routed_experts(nc, a, k, n, htab, acc, slots, raw, w_loaded, y_stored)

        ffn(0, a["x"], x1)
        attention(nc, a, k, x1, x2)
        ffn(1, x2, out)


def constants():
    tok = np.arange(TOK).reshape(NT, P)
    part, col = np.arange(P)[:, None], np.arange(P)[None, :]
    seg = np.ones((P, NT, E), np.float32)
    seg[:, :, 0] = 0.0
    diag = np.zeros((SA, EG, SB_, EG), np.float32)
    for e in range(EG):
        diag[:, e, :, e] = 1.0
    to_slot = np.zeros((GE * SB_, SA // 2, HALF), np.float32)
    for a in range(SA // 2):
        to_slot[:, a, a * SB_:(a + 1) * SB_] = np.tile(np.eye(SB_), (GE, 1))
    dims = np.arange(DH // 2)
    ang = np.power(np.float32(2500.0), (-dims / (DH // 2)).astype(np.float32)).astype(np.float32)
    rad = np.arange(SEQ).astype(np.float32)[:, None] * ang[None, :]
    turn = lambda t: np.ascontiguousarray(t.astype(np.float32).reshape(NQ, P, DH // 2).transpose(1, 0, 2))
    return {
        "ident": np.eye(P, dtype=np.float32),
        "causal": np.where(col > part, np.float32(-1e30), np.float32(0)).astype(np.float32),
        "upto": (part <= col).astype(np.float32),
        "seg": seg,
        "iota_a": np.broadcast_to(np.arange(SA, dtype=np.float32)[:, None], (P, SA, E)).copy(),
        "iota_b": np.broadcast_to(np.arange(SB_, dtype=np.float32)[:, None], (P, SB_, E)).copy(),
        "part_id": np.arange(P, dtype=np.float32)[:, None].copy(),
        "tile_id": np.broadcast_to((tok[:, 0] - DUMP).astype(np.float32), (P, NT)).copy(),
        "diag": diag.reshape(SA * EG, SB_, EG),
        "to_slot": to_slot,
        "own_group": np.repeat(np.eye(GE, dtype=np.float32), SB_, axis=0),
        "dump": np.arange(HALF, dtype=np.float32)[:, None].copy(),
        "cos": turn(np.cos(rad)),
        "sin": np.concatenate([turn(-np.sin(rad)), turn(np.sin(rad))], 2),
    }


def laid_out(x, wq, wk, wv, wo, gq, gk, gate_w, bias, w_gate, w_up, w_down, sg, su, sd):
    rows = lambda w, blocks: w.reshape(blocks, P, -1).transpose(1, 0, 2)
    whole = lambda g, u, d: np.concatenate(
        [rows(np.concatenate([g.T, u.T], 1), KB).reshape(P, WGU), rows(d.T, FB).reshape(P, WDN)], 1)
    out = {
        "x": x.reshape(TOK, D),
        "router_w": rows(gate_w.T, KB),
        "bias": np.broadcast_to(bias, (P, E)),
        "w_shared": whole(sg, su, sd),
        "w_experts": np.stack([whole(w_gate[e], w_up[e], w_down[e]) for e in range(E)]),
        "w_qkv": rows(np.concatenate([wq, wk, wv], 1), KB),
        "w_out": rows(wo, H),
        "gains": np.broadcast_to(np.concatenate([gq.reshape(H, DH), gk.reshape(1, DH)], 0), (P, H + 1, DH)),
    }
    return {name: np.ascontiguousarray(t) for name, t in out.items()}


def kernel(**inputs):
    import concourse.bacc as bacc
    from concourse.bass_utils import run_bass_kernel_spmd

    arrays = laid_out(*(np.asarray(inputs[name]) for name in (
        "L0_attn_x", "L0_attn_wq", "L0_attn_wk", "L0_attn_wv", "L0_attn_wo", "L0_attn_gq", "L0_attn_gk",
        "L0_ffn_gate_w", "L0_ffn_bias", "L0_ffn_w_gate", "L0_ffn_w_up", "L0_ffn_w_down",
        "L0_ffn_sg", "L0_ffn_su", "L0_ffn_sd")))
    arrays.update(constants())
    arrays = {f"in_{name}": t for name, t in arrays.items()}
    nc = bacc.Bacc("TRN2", target_bir_lowering=False, num_devices=1)
    a = {name[3:]: nc.dram_tensor(name, t.shape, mybir.dt.from_np(t.dtype), kind="ExternalInput").ap()
         for name, t in arrays.items()}
    out = nc.dram_tensor("out", [ROWS, D], F32, kind="ExternalOutput").ap()
    build_program(nc, a, out)
    got = run_bass_kernel_spmd(nc, [arrays], core_ids=[0])
    return got.results[0]["out"][0:TOK].reshape(B, SEQ, D)
```
